# Optimizing a Trainium2 kernel written in Bass

```python
import numpy as np
import jax
import jax.numpy as jnp

def _softmax(x, axis=-1):
    return jax.nn.softmax(x, axis=axis)

def _gelu(x):
    return jax.nn.gelu(x, approximate=True)

def _silu(x):
    return jax.nn.silu(x)

def _sigmoid(x):
    return jax.nn.sigmoid(x)

def _layernorm(x, axis=-1, eps=1e-05):
    m = jnp.mean(x, axis=axis, keepdims=True)
    v = jnp.var(x, axis=axis, keepdims=True)
    return (x - m) / jnp.sqrt(v + eps)

def _scatter_add(tgt, idx, src, axis=0):
    return tgt.at[idx].add(src)

def _segment_sum(src, seg, n):
    return jax.ops.segment_sum(src, seg, n)
kernel_name = 'mk_seq_preln_d4_jaxref_r8_8b3cd0'

def setup_inputs(seed: int=0):
    np.random.seed(seed)
    _w = jnp.asarray

    def _L0_attn_setup():
        import jax, jax.numpy as jnp
        import numpy as np
        DECAY = 0.95

        def smear(x, decay):
            a = jnp.full_like(x, decay)

            def combine(c1, c2):
                a1, b1 = c1
                a2, b2 = c2
                return (a1 * a2, a2 * b1 + b2)
            _, y = jax.lax.associative_scan(combine, (a, x), axis=1)
            return y
        key = jax.random.key(seed)
        ks = jax.random.split(key, 5)
        B, S, E, M = (4, 512, 256, 256)
        x = jax.random.normal(ks[0], (B, S, E), dtype=jnp.float32)
        s = 0.02
        Wv = jax.random.normal(ks[1], (E, M), dtype=jnp.float32) * s
        Wg = jax.random.normal(ks[2], (E, M), dtype=jnp.float32) * s
        bg = jnp.zeros((M,), dtype=jnp.float32)
        Wq = jax.random.normal(ks[3], (E, M), dtype=jnp.float32) * s
        bq = jnp.zeros((M,), dtype=jnp.float32)
        Wo = jax.random.normal(ks[4], (M, E), dtype=jnp.float32) * s
        return {'x': x, 'Wv': Wv, 'Wg': Wg, 'bg': bg, 'Wq': Wq, 'bq': bq, 'Wo': Wo}
    _L0_attn_in = _L0_attn_setup()

    def _L0_ffn_setup():
        import jax, jax.numpy as jnp
        import numpy as np
        from jax import lax
        TOP_K = 4
        ROUTED_SCALING = 1.0
        RENORMALIZE = True

        def _swiglu_ffn(x, wg, wu, wd):
            return jax.nn.silu(x @ wg.T) * (x @ wu.T) @ wd.T
        key = jax.random.key(seed)
        ks = jax.random.split(key, 9)
        H, I, E = (256, 128, 16)
        s = 0.02
        return {'hidden_states': jax.random.normal(ks[0], (2, 128, H), jnp.float32), 'gate_w': jax.random.normal(ks[1], (E, H), jnp.float32) * s, 'expert_bias': jax.random.normal(ks[2], (E,), jnp.float32) * s, 'w_gate': jax.random.normal(ks[3], (E, I, H), jnp.float32) * s, 'w_up': jax.random.normal(ks[4], (E, I, H), jnp.float32) * s, 'w_down': jax.random.normal(ks[5], (E, H, I), jnp.float32) * s, 'sw_gate': jax.random.normal(ks[6], (I, H), jnp.float32) * s, 'sw_up': jax.random.normal(ks[7], (I, H), jnp.float32) * s, 'sw_down': jax.random.normal(ks[8], (H, I), jnp.float32) * s}
    _L0_ffn_in = _L0_ffn_setup()

    def _L1_attn_setup():
        import jax, jax.numpy as jnp
        import numpy as np
        D_ATTN = 256
        D_STATE = 64
        SHIFT_FRAC = 0.5
        LN_EPS = 1e-05

        def _reference_tuple_inner(x, W_key, W_value, W_output, W_shift, gate, time_decay, time_first, ln_gamma, ln_beta):
            B, T, D = x.shape
            shift_len = max(1, int(T * SHIFT_FRAC))
            x_cat = jnp.roll(x, -shift_len, axis=1)
            g = jax.nn.sigmoid(gate)
            x_shift = jnp.einsum('btd,ed->bte', x_cat, W_shift) * g + x * (1.0 - g)
            mu = jnp.mean(x_shift, axis=-1, keepdims=True)
            var = jnp.var(x_shift, axis=-1, keepdims=True)
            x_norm = (x_shift - mu) * jax.lax.rsqrt(var + LN_EPS) * ln_gamma + ln_beta
            k = jnp.einsum('btd,sd->bts', x_norm, W_key)
            v = jnp.einsum('btd,sd->bts', x_norm, W_value)
            w = jnp.exp(time_decay)
            u = jnp.exp(time_first)
            wkv = jnp.exp(-u * jax.nn.sigmoid(k)) * v

            def step(state, wkv_t):
                state = state * w + wkv_t
                return (state, state)
            init = jnp.zeros((B, k.shape[-1]), x.dtype)
            last_state, states = jax.lax.scan(step, init, jnp.swapaxes(wkv, 0, 1))
            states = jnp.swapaxes(states, 0, 1)
            output = jnp.einsum('bts,ds->btd', states, W_output)
            return (output, jax.lax.stop_gradient(last_state))
        key = jax.random.key(seed)
        ks = jax.random.split(key, 8)
        B, T = (8, 256)
        s_attn = 1.0 / np.sqrt(D_ATTN)
        s_state = 1.0 / np.sqrt(D_STATE)
        x = jax.random.normal(ks[0], (B, T, D_ATTN), jnp.float32)
        W_key = jax.random.normal(ks[1], (D_STATE, D_ATTN), jnp.float32) * s_attn
        W_value = jax.random.normal(ks[2], (D_STATE, D_ATTN), jnp.float32) * s_attn
        W_output = jax.random.normal(ks[3], (D_ATTN, D_STATE), jnp.float32) * s_state
        W_shift = jax.random.normal(ks[4], (D_ATTN, D_ATTN), jnp.float32) * s_attn
        gate = jnp.ones((D_ATTN,), jnp.float32)
        time_decay = -jax.random.uniform(ks[5], (D_STATE,), jnp.float32, 0.05, 1.0)
        time_first = jax.random.normal(ks[6], (D_STATE,), jnp.float32) * 0.1
        ln_gamma = jnp.ones((D_ATTN,), jnp.float32)
        ln_beta = jnp.zeros((D_ATTN,), jnp.float32)
        return dict(x=x, W_key=W_key, W_value=W_value, W_output=W_output, W_shift=W_shift, gate=gate, time_decay=time_decay, time_first=time_first, ln_gamma=ln_gamma, ln_beta=ln_beta)
    _L1_attn_in = _L1_attn_setup()

    def _L1_ffn_setup():
        import jax, jax.numpy as jnp
        import numpy as np
        B, S, D = (2, 256, 256)
        I = 128
        E = 32
        K = 4
        NS = 1
        ALPHA = 7.0

        def _clamped_swiglu(x, wg, wu, wd):
            g = jnp.clip(x @ wg.T, -ALPHA, ALPHA)
            u = jnp.clip(x @ wu.T, -ALPHA, ALPHA)
            return jax.nn.silu(g) * u @ wd.T
        key = jax.random.key(seed)
        ks = jax.random.split(key, 9)
        s = 0.02
        return {'hidden': jax.random.normal(ks[0], (B, S, D), jnp.float32), 'router_w': jax.random.normal(ks[1], (E, D), jnp.float32) * s, 'expert_bias': jax.random.normal(ks[2], (E,), jnp.float32) * s, 'gate_w': jax.random.normal(ks[3], (E, I, D), jnp.float32) * s, 'up_w': jax.random.normal(ks[4], (E, I, D), jnp.float32) * s, 'down_w': jax.random.normal(ks[5], (E, D, I), jnp.float32) * s, 'shared_gate_w': jax.random.normal(ks[6], (NS * I, D), jnp.float32) * s, 'shared_up_w': jax.random.normal(ks[7], (NS * I, D), jnp.float32) * s, 'shared_down_w': jax.random.normal(ks[8], (D, NS * I), jnp.float32) * s}
    _L1_ffn_in = _L1_ffn_setup()

    def _L2_attn_setup():
        import jax, jax.numpy as jnp
        import numpy as np
        HIDDEN = 256
        HEADS = 16
        HEAD_DIM = HIDDEN // HEADS
        NEG = -10000000000.0
        key = jax.random.key(seed)
        k1, k2, k3 = jax.random.split(key, 3)
        x = jax.random.normal(k1, (2, 256, HIDDEN), dtype=jnp.float32)
        w_qkv = jax.random.normal(k2, (HIDDEN, 3 * HIDDEN), dtype=jnp.float32) / np.sqrt(HIDDEN)
        w_out = jax.random.normal(k3, (HIDDEN, HIDDEN), dtype=jnp.float32) / np.sqrt(HIDDEN)
        return {'x': x, 'w_qkv': w_qkv, 'w_out': w_out}
    _L2_attn_in = _L2_attn_setup()

    def _L2_ffn_setup():
        import jax, jax.numpy as jnp
        import numpy as np
        H = 256
        I = 128
        E = 32
        K = 4
        N_SHARED = 1
        EPS = 1e-06

        def _rmsnorm(x, w, eps=EPS):
            var = jnp.mean(jnp.square(x), axis=-1, keepdims=True)
            return x * jax.lax.rsqrt(var + eps) * w

        def _moe_core(x, gate_w, w13, w2):
            T = x.shape[0]
            N = T * K
            C = 2 * N // E
            logits = jnp.einsum('th,eh->te', x.astype(jnp.float32), gate_w.astype(jnp.float32))
            scores = jax.nn.softmax(logits, axis=-1)
            topk_w, topk_ids = jax.lax.top_k(scores, K)
            topk_w = topk_w / jnp.sum(topk_w, axis=-1, keepdims=True)
            flat_ids = topk_ids.reshape(-1)
            flat_w = topk_w.reshape(-1)
            order = jnp.argsort(flat_ids)
            sorted_eid = flat_ids[order]
            tok = order // K
            counts = jnp.zeros((E,), jnp.int32).at[flat_ids].add(1)
            starts = jnp.cumsum(counts) - counts
            pos = jnp.arange(N) - starts[sorted_eid]
            buf = jnp.zeros((E, C, x.shape[1]), x.dtype).at[sorted_eid, pos].set(x[tok], mode='drop')
            gu = jnp.einsum('ech,ehf->ecf', buf, w13)
            g, u = jnp.split(gu, 2, axis=-1)
            act = jax.nn.silu(g) * u
            eo = jnp.einsum('eci,eih->ech', act, w2)
            out_slots = eo[sorted_eid, pos]
            routed = jnp.zeros_like(x).at[tok].add(out_slots * flat_w[order][:, None])
            return routed
        key = jax.random.key(seed)
        ks = jax.random.split(key, 8)
        s = 1.0 / np.sqrt(H)
        si = 1.0 / np.sqrt(I)
        return {'hidden_states': jax.random.normal(ks[0], (1, 512, H), jnp.float32), 'norm_w': jnp.ones((H,), jnp.float32), 'gate_w': jax.random.normal(ks[1], (E, H), jnp.float32) * s, 'w13': jax.random.normal(ks[2], (E, H, 2 * I), jnp.float32) * s, 'w2': jax.random.normal(ks[3], (E, I, H), jnp.float32) * si, 'shared_gate_w': jax.random.normal(ks[4], (H, I * N_SHARED), jnp.float32) * s, 'shared_up_w': jax.random.normal(ks[5], (H, I * N_SHARED), jnp.float32) * s, 'shared_down_w': jax.random.normal(ks[6], (I * N_SHARED, H), jnp.float32) * si}
    _L2_ffn_in = _L2_ffn_setup()

    def _L3_attn_setup():
        import jax, jax.numpy as jnp
        import numpy as np
        B, S, E, H = (2, 256, 256, 16)
        D = E // H
        ROPE_BASE = 10000.0

        def rotate_half(x):
            x1 = x[..., ::2]
            x2 = x[..., 1::2]
            return jnp.stack((-x2, x1), axis=-1).reshape(x.shape[:-1] + (x.shape[-1],))

        def rope_cos_sin(seq_len, head_dim, start_pos=0):
            inv_freq = 1.0 / ROPE_BASE ** (jnp.arange(0, head_dim, 2, dtype=jnp.float32) / head_dim)
            positions = jnp.arange(start_pos, start_pos + seq_len, dtype=jnp.float32)
            freqs = jnp.outer(positions, inv_freq)
            emb = jnp.concatenate([freqs, freqs], axis=-1)
            return (emb[None, None].astype(jnp.float32), emb)
        key = jax.random.key(seed)
        k1, k2, k3 = jax.random.split(key, 3)
        x = jax.random.normal(k1, (B, S, E), dtype=jnp.float32)
        Wqkv = jax.random.normal(k2, (3 * E, E), dtype=jnp.float32) * E ** (-0.5)
        Wout = jax.random.normal(k3, (E, E), dtype=jnp.float32) * E ** (-0.5)
        return {'x': x, 'Wqkv': Wqkv, 'Wout': Wout}
    _L3_attn_in = _L3_attn_setup()

    def _L3_ffn_setup():
        import jax, jax.numpy as jnp
        import numpy as np
        HIDDEN = 256
        INTER = 704
        B, S = (2, 256)

        def _ternary(key, shape):
            return jax.random.randint(key, shape, -1, 2).astype(jnp.float32)
        key = jax.random.key(seed)
        ks = jax.random.split(key, 7)
        x = jax.random.normal(ks[0], (B, S, HIDDEN), dtype=jnp.float32)
        gate_w = _ternary(ks[1], (INTER, HIDDEN))
        up_w = _ternary(ks[2], (INTER, HIDDEN))
        down_w = _ternary(ks[3], (HIDDEN, INTER))
        gate_s = jax.random.uniform(ks[4], (INTER,), minval=0.01, maxval=0.1, dtype=jnp.float32)
        up_s = jax.random.uniform(ks[5], (INTER,), minval=0.01, maxval=0.1, dtype=jnp.float32)
        down_s = jax.random.uniform(ks[6], (HIDDEN,), minval=0.01, maxval=0.1, dtype=jnp.float32)
        return {'x': x, 'gate_w': gate_w, 'up_w': up_w, 'down_w': down_w, 'gate_s': gate_s, 'up_s': up_s, 'down_s': down_s}
    _L3_ffn_in = _L3_ffn_setup()
    _d = {'L0_attn_x': _L0_attn_in['x'], 'L0_attn_Wv': _L0_attn_in['Wv'], 'L0_attn_Wg': _L0_attn_in['Wg'], 'L0_attn_bg': _L0_attn_in['bg'], 'L0_attn_Wq': _L0_attn_in['Wq'], 'L0_attn_bq': _L0_attn_in['bq'], 'L0_attn_Wo': _L0_attn_in['Wo'], 'L0_ffn_gate_w': _L0_ffn_in['gate_w'], 'L0_ffn_expert_bias': _L0_ffn_in['expert_bias'], 'L0_ffn_w_gate': _L0_ffn_in['w_gate'], 'L0_ffn_w_up': _L0_ffn_in['w_up'], 'L0_ffn_w_down': _L0_ffn_in['w_down'], 'L0_ffn_sw_gate': _L0_ffn_in['sw_gate'], 'L0_ffn_sw_up': _L0_ffn_in['sw_up'], 'L0_ffn_sw_down': _L0_ffn_in['sw_down'], 'L1_attn_W_key': _L1_attn_in['W_key'], 'L1_attn_W_value': _L1_attn_in['W_value'], 'L1_attn_W_output': _L1_attn_in['W_output'], 'L1_attn_W_shift': _L1_attn_in['W_shift'], 'L1_attn_gate': _L1_attn_in['gate'], 'L1_attn_time_decay': _L1_attn_in['time_decay'], 'L1_attn_time_first': _L1_attn_in['time_first'], 'L1_attn_ln_gamma': _L1_attn_in['ln_gamma'], 'L1_attn_ln_beta': _L1_attn_in['ln_beta'], 'L1_ffn_router_w': _L1_ffn_in['router_w'], 'L1_ffn_expert_bias': _L1_ffn_in['expert_bias'], 'L1_ffn_gate_w': _L1_ffn_in['gate_w'], 'L1_ffn_up_w': _L1_ffn_in['up_w'], 'L1_ffn_down_w': _L1_ffn_in['down_w'], 'L1_ffn_shared_gate_w': _L1_ffn_in['shared_gate_w'], 'L1_ffn_shared_up_w': _L1_ffn_in['shared_up_w'], 'L1_ffn_shared_down_w': _L1_ffn_in['shared_down_w'], 'L2_attn_w_qkv': _L2_attn_in['w_qkv'], 'L2_attn_w_out': _L2_attn_in['w_out'], 'L2_ffn_norm_w': _L2_ffn_in['norm_w'], 'L2_ffn_gate_w': _L2_ffn_in['gate_w'], 'L2_ffn_w13': _L2_ffn_in['w13'], 'L2_ffn_w2': _L2_ffn_in['w2'], 'L2_ffn_shared_gate_w': _L2_ffn_in['shared_gate_w'], 'L2_ffn_shared_up_w': _L2_ffn_in['shared_up_w'], 'L2_ffn_shared_down_w': _L2_ffn_in['shared_down_w'], 'L3_attn_Wqkv': _L3_attn_in['Wqkv'], 'L3_attn_Wout': _L3_attn_in['Wout'], 'L3_ffn_gate_w': _L3_ffn_in['gate_w'], 'L3_ffn_up_w': _L3_ffn_in['up_w'], 'L3_ffn_down_w': _L3_ffn_in['down_w'], 'L3_ffn_gate_s': _L3_ffn_in['gate_s'], 'L3_ffn_up_s': _L3_ffn_in['up_s'], 'L3_ffn_down_s': _L3_ffn_in['down_s']}
    _x0 = _d['L0_attn_x']
    _d['L0_attn_x'] = jax.random.normal(jax.random.fold_in(jax.random.key(seed), 1), (2, 1024, 256), dtype=_x0.dtype)
    del _x0
    return _d

def reference(L0_attn_x, L0_attn_Wv, L0_attn_Wg, L0_attn_bg, L0_attn_Wq, L0_attn_bq, L0_attn_Wo, L0_ffn_gate_w, L0_ffn_expert_bias, L0_ffn_w_gate, L0_ffn_w_up, L0_ffn_w_down, L0_ffn_sw_gate, L0_ffn_sw_up, L0_ffn_sw_down, L1_attn_W_key, L1_attn_W_value, L1_attn_W_output, L1_attn_W_shift, L1_attn_gate, L1_attn_time_decay, L1_attn_time_first, L1_attn_ln_gamma, L1_attn_ln_beta, L1_ffn_router_w, L1_ffn_expert_bias, L1_ffn_gate_w, L1_ffn_up_w, L1_ffn_down_w, L1_ffn_shared_gate_w, L1_ffn_shared_up_w, L1_ffn_shared_down_w, L2_attn_w_qkv, L2_attn_w_out, L2_ffn_norm_w, L2_ffn_gate_w, L2_ffn_w13, L2_ffn_w2, L2_ffn_shared_gate_w, L2_ffn_shared_up_w, L2_ffn_shared_down_w, L3_attn_Wqkv, L3_attn_Wout, L3_ffn_gate_w, L3_ffn_up_w, L3_ffn_down_w, L3_ffn_gate_s, L3_ffn_up_s, L3_ffn_down_s):

    def _L0_attn_ref(x, Wv, Wg, bg, Wq, bq, Wo):
        import jax, jax.numpy as jnp
        import numpy as np
        DECAY = 0.95

        def smear(x, decay):
            a = jnp.full_like(x, decay)

            def combine(c1, c2):
                a1, b1 = c1
                a2, b2 = c2
                return (a1 * a2, a2 * b1 + b2)
            _, y = jax.lax.associative_scan(combine, (a, x), axis=1)
            return y
        scale = jnp.float32(np.sqrt(1.0 - DECAY))
        gate = jax.nn.sigmoid(jnp.einsum('bse,em->bsm', x, Wg) + bg)
        store = jnp.einsum('bse,em->bsm', x, Wv) * gate * scale
        mem = smear(store, DECAY)
        que = jax.nn.sigmoid(jnp.einsum('bse,em->bsm', x, Wq) + bq)
        load = mem * que * scale
        return jnp.einsum('bsm,me->bse', load, Wo)

    def _L0_ffn_ref(hidden_states, gate_w, expert_bias, w_gate, w_up, w_down, sw_gate, sw_up, sw_down):
        import jax, jax.numpy as jnp
        import numpy as np
        from jax import lax
        TOP_K = 4
        ROUTED_SCALING = 1.0
        RENORMALIZE = True

        def _swiglu_ffn(x, wg, wu, wd):
            return jax.nn.silu(x @ wg.T) * (x @ wu.T) @ wd.T
        orig_shape = hidden_states.shape
        H = orig_shape[-1]
        x = hidden_states.reshape(-1, H)
        T = x.shape[0]
        logits = x.astype(jnp.float32) @ gate_w.T
        scores = jax.nn.sigmoid(logits)
        _, topk_idx = lax.top_k(scores + expert_bias[None, :], TOP_K)
        topk_w = jnp.take_along_axis(scores, topk_idx, axis=-1)
        if RENORMALIZE:
            topk_w = topk_w / jnp.sum(topk_w, axis=-1, keepdims=True)
        topk_w = topk_w * ROUTED_SCALING
        E = gate_w.shape[0]
        combine = jnp.zeros((T, E), dtype=x.dtype).at[jnp.arange(T)[:, None], topk_idx].set(topk_w.astype(x.dtype))

        def step(acc, ws):
            wg, wu, wd, cw = ws
            return (acc + cw[:, None] * _swiglu_ffn(x, wg, wu, wd), None)
        routed, _ = lax.scan(step, jnp.zeros_like(x), (w_gate, w_up, w_down, combine.T))
        shared = _swiglu_ffn(x, sw_gate, sw_up, sw_down)
        return (routed + shared).reshape(orig_shape)

    def _L1_attn_ref(x, W_key, W_value, W_output, W_shift, gate, time_decay, time_first, ln_gamma, ln_beta):
        import jax, jax.numpy as jnp
        import numpy as np
        D_ATTN = 256
        D_STATE = 64
        SHIFT_FRAC = 0.5
        LN_EPS = 1e-05

        def _reference_tuple_inner(x, W_key, W_value, W_output, W_shift, gate, time_decay, time_first, ln_gamma, ln_beta):
            B, T, D = x.shape
            shift_len = max(1, int(T * SHIFT_FRAC))
            x_cat = jnp.roll(x, -shift_len, axis=1)
            g = jax.nn.sigmoid(gate)
            x_shift = jnp.einsum('btd,ed->bte', x_cat, W_shift) * g + x * (1.0 - g)
            mu = jnp.mean(x_shift, axis=-1, keepdims=True)
            var = jnp.var(x_shift, axis=-1, keepdims=True)
            x_norm = (x_shift - mu) * jax.lax.rsqrt(var + LN_EPS) * ln_gamma + ln_beta
            k = jnp.einsum('btd,sd->bts', x_norm, W_key)
            v = jnp.einsum('btd,sd->bts', x_norm, W_value)
            w = jnp.exp(time_decay)
            u = jnp.exp(time_first)
            wkv = jnp.exp(-u * jax.nn.sigmoid(k)) * v

            def step(state, wkv_t):
                state = state * w + wkv_t
                return (state, state)
            init = jnp.zeros((B, k.shape[-1]), x.dtype)
            last_state, states = jax.lax.scan(step, init, jnp.swapaxes(wkv, 0, 1))
            states = jnp.swapaxes(states, 0, 1)
            output = jnp.einsum('bts,ds->btd', states, W_output)
            return (output, jax.lax.stop_gradient(last_state))
        return _reference_tuple_inner(x, W_key, W_value, W_output, W_shift, gate, time_decay, time_first, ln_gamma, ln_beta)[0]

    def _L1_ffn_ref(hidden, router_w, expert_bias, gate_w, up_w, down_w, shared_gate_w, shared_up_w, shared_down_w):
        import jax, jax.numpy as jnp
        import numpy as np
        B, S, D = (2, 256, 256)
        I = 128
        E = 32
        K = 4
        NS = 1
        ALPHA = 7.0

        def _clamped_swiglu(x, wg, wu, wd):
            g = jnp.clip(x @ wg.T, -ALPHA, ALPHA)
            u = jnp.clip(x @ wu.T, -ALPHA, ALPHA)
            return jax.nn.silu(g) * u @ wd.T
        Bb, Ss, Dd = hidden.shape
        flat = hidden.reshape(-1, Dd)
        T = flat.shape[0]
        logits = flat @ router_w.T
        scores = jnp.sqrt(jax.nn.softplus(logits))
        _, idx = jax.lax.top_k(scores + expert_bias, K)
        topv = jnp.take_along_axis(scores, idx, axis=1)
        topv = topv / (topv.sum(axis=-1, keepdims=True) + 1e-20)
        probs = jnp.zeros((T, E), flat.dtype).at[jnp.arange(T)[:, None], idx].set(topv)

        def body(acc, xs):
            wg, wu, wd, p = xs
            return (acc + p[:, None] * _clamped_swiglu(flat, wg, wu, wd), None)
        out, _ = jax.lax.scan(body, jnp.zeros_like(flat), (gate_w, up_w, down_w, probs.T))
        out = out + _clamped_swiglu(flat, shared_gate_w, shared_up_w, shared_down_w)
        return out.reshape(Bb, Ss, Dd)

    def _L2_attn_ref(x, w_qkv, w_out):
        import jax, jax.numpy as jnp
        import numpy as np
        HIDDEN = 256
        HEADS = 16
        HEAD_DIM = HIDDEN // HEADS
        NEG = -10000000000.0
        b, s, _ = x.shape
        qkv = x @ w_qkv
        qkv = qkv.reshape(b, s, 3, HEADS, HEAD_DIM)
        q, k, v = (qkv[:, :, 0], qkv[:, :, 1], qkv[:, :, 2])
        scale = jnp.sqrt(jnp.float32(HEAD_DIM)).astype(x.dtype)
        q = q / scale
        scores = jnp.einsum('bqhd,bkhd->bhqk', q, k)
        causal_mask = jnp.arange(s)[:, None] >= jnp.arange(s)[None, :]
        scores = jnp.where(causal_mask[None, None], scores, NEG)
        attn = jax.nn.softmax(scores, axis=-1)
        out = jnp.einsum('bhqk,bkhd->bqhd', attn, v).reshape(b, s, HIDDEN)
        return out @ w_out

    def _L2_ffn_ref(hidden_states, norm_w, gate_w, w13, w2, shared_gate_w, shared_up_w, shared_down_w):
        import jax, jax.numpy as jnp
        import numpy as np
        H = 256
        I = 128
        E = 32
        K = 4
        N_SHARED = 1
        EPS = 1e-06

        def _rmsnorm(x, w, eps=EPS):
            var = jnp.mean(jnp.square(x), axis=-1, keepdims=True)
            return x * jax.lax.rsqrt(var + eps) * w

        def _moe_core(x, gate_w, w13, w2):
            T = x.shape[0]
            N = T * K
            C = 2 * N // E
            logits = jnp.einsum('th,eh->te', x.astype(jnp.float32), gate_w.astype(jnp.float32))
            scores = jax.nn.softmax(logits, axis=-1)
            topk_w, topk_ids = jax.lax.top_k(scores, K)
            topk_w = topk_w / jnp.sum(topk_w, axis=-1, keepdims=True)
            flat_ids = topk_ids.reshape(-1)
            flat_w = topk_w.reshape(-1)
            order = jnp.argsort(flat_ids)
            sorted_eid = flat_ids[order]
            tok = order // K
            counts = jnp.zeros((E,), jnp.int32).at[flat_ids].add(1)
            starts = jnp.cumsum(counts) - counts
            pos = jnp.arange(N) - starts[sorted_eid]
            buf = jnp.zeros((E, C, x.shape[1]), x.dtype).at[sorted_eid, pos].set(x[tok], mode='drop')
            gu = jnp.einsum('ech,ehf->ecf', buf, w13)
            g, u = jnp.split(gu, 2, axis=-1)
            act = jax.nn.silu(g) * u
            eo = jnp.einsum('eci,eih->ech', act, w2)
            out_slots = eo[sorted_eid, pos]
            routed = jnp.zeros_like(x).at[tok].add(out_slots * flat_w[order][:, None])
            return routed
        B, S, Hd = hidden_states.shape
        residual = hidden_states
        h = _rmsnorm(hidden_states, norm_w)
        x = h.reshape(-1, Hd)
        routed = _moe_core(x, gate_w, w13, w2)
        shared = jax.nn.silu(x @ shared_gate_w) * (x @ shared_up_w) @ shared_down_w
        out = residual + (routed + shared).reshape(B, S, Hd)
        return out

    def _L3_attn_ref(x, Wqkv, Wout):
        import jax, jax.numpy as jnp
        import numpy as np
        B, S, E, H = (2, 256, 256, 16)
        D = E // H
        ROPE_BASE = 10000.0

        def rotate_half(x):
            x1 = x[..., ::2]
            x2 = x[..., 1::2]
            return jnp.stack((-x2, x1), axis=-1).reshape(x.shape[:-1] + (x.shape[-1],))

        def rope_cos_sin(seq_len, head_dim, start_pos=0):
            inv_freq = 1.0 / ROPE_BASE ** (jnp.arange(0, head_dim, 2, dtype=jnp.float32) / head_dim)
            positions = jnp.arange(start_pos, start_pos + seq_len, dtype=jnp.float32)
            freqs = jnp.outer(positions, inv_freq)
            emb = jnp.concatenate([freqs, freqs], axis=-1)
            return (emb[None, None].astype(jnp.float32), emb)
        batch, seq_len, emb = x.shape
        scale = D ** (-0.5)
        qkv = x @ Wqkv.T
        qkv = qkv.reshape(batch, seq_len, 3, H, D)
        qkv = jnp.transpose(qkv, (2, 0, 3, 1, 4))
        q, k, v = (qkv[0], qkv[1], qkv[2])
        inv_freq = 1.0 / ROPE_BASE ** (jnp.arange(0, D, 2, dtype=jnp.float32) / D)
        positions = jnp.arange(seq_len, dtype=jnp.float32)
        freqs = jnp.outer(positions, inv_freq)
        emb_ang = jnp.concatenate([freqs, freqs], axis=-1)
        cos = jnp.cos(emb_ang)[None, None]
        sin = jnp.sin(emb_ang)[None, None]
        q = q * cos + rotate_half(q) * sin
        k = k * cos + rotate_half(k) * sin
        scores = jnp.einsum('bhqd,bhkd->bhqk', q, k) * scale
        causal = jnp.arange(seq_len)[None, :] > jnp.arange(seq_len)[:, None]
        scores = jnp.where(causal[None, None], -jnp.inf, scores)
        attn = jax.nn.softmax(scores, axis=-1)
        out = jnp.einsum('bhqk,bhkd->bhqd', attn, v)
        out = jnp.transpose(out, (0, 2, 1, 3)).reshape(batch, seq_len, emb)
        return out @ Wout.T

    def _L3_ffn_ref(x, gate_w, up_w, down_w, gate_s, up_s, down_s):
        import jax, jax.numpy as jnp
        import numpy as np
        HIDDEN = 256
        INTER = 704
        B, S = (2, 256)

        def _ternary(key, shape):
            return jax.random.randint(key, shape, -1, 2).astype(jnp.float32)
        b, s, h = x.shape
        xf = x.reshape(b * s, h)
        g = jnp.einsum('th,ih->ti', xf, gate_w) * gate_s
        u = jnp.einsum('th,ih->ti', xf, up_w) * up_s
        hdn = jax.nn.silu(g) * u
        out = jnp.einsum('ti,hi->th', hdn, down_w) * down_s
        return out.reshape(b, s, -1)
    x = L0_attn_x
    x = x + _L0_attn_ref(_layernorm(x, axis=-1), L0_attn_Wv, L0_attn_Wg, L0_attn_bg, L0_attn_Wq, L0_attn_bq, L0_attn_Wo)
    x = x + _L0_ffn_ref(_layernorm(x, axis=-1), L0_ffn_gate_w, L0_ffn_expert_bias, L0_ffn_w_gate, L0_ffn_w_up, L0_ffn_w_down, L0_ffn_sw_gate, L0_ffn_sw_up, L0_ffn_sw_down)
    x = x + _L1_attn_ref(_layernorm(x, axis=-1), L1_attn_W_key, L1_attn_W_value, L1_attn_W_output, L1_attn_W_shift, L1_attn_gate, L1_attn_time_decay, L1_attn_time_first, L1_attn_ln_gamma, L1_attn_ln_beta)
    x = x + _L1_ffn_ref(_layernorm(x, axis=-1), L1_ffn_router_w, L1_ffn_expert_bias, L1_ffn_gate_w, L1_ffn_up_w, L1_ffn_down_w, L1_ffn_shared_gate_w, L1_ffn_shared_up_w, L1_ffn_shared_down_w)
    x = x + _L2_attn_ref(_layernorm(x, axis=-1), L2_attn_w_qkv, L2_attn_w_out)
    x = x + _L2_ffn_ref(_layernorm(x, axis=-1), L2_ffn_norm_w, L2_ffn_gate_w, L2_ffn_w13, L2_ffn_w2, L2_ffn_shared_gate_w, L2_ffn_shared_up_w, L2_ffn_shared_down_w)
    x = x + _L3_attn_ref(_layernorm(x, axis=-1), L3_attn_Wqkv, L3_attn_Wout)
    x = x + _L3_ffn_ref(_layernorm(x, axis=-1), L3_ffn_gate_w, L3_ffn_up_w, L3_ffn_down_w, L3_ffn_gate_s, L3_ffn_up_s, L3_ffn_down_s)
    return x

_drawn_inputs = setup_inputs


def setup_inputs(seed=0):
    import zlib

    import numpy as np

    out = dict(_drawn_inputs(seed))
    spreads = {'L0_attn_bg': (0.0, 0.8),
     'L0_attn_bq': (0.0, 1.535),
     'L1_attn_gate': (1.0, 0.2),
     'L1_attn_ln_gamma': (1.0, 0.2),
     'L1_attn_ln_beta': (0.0, 0.1),
     'L2_ffn_norm_w': (1.0, 0.2)}
    factors = {'L0_attn_Wv': 2.79,
     'L0_ffn_w_down': 2.857,
     'L1_ffn_expert_bias': 31.68,
     'L1_ffn_shared_gate_w': 3.164,
     'L1_ffn_shared_up_w': 3.228,
     'L0_attn_Wq': 4.398,
     'L0_ffn_expert_bias': 2.724,
     'L0_ffn_sw_gate': 2.685,
     'L1_ffn_router_w': 2.993,
     'L1_ffn_gate_w': 3.101,
     'L1_ffn_up_w': 2.672,
     'L1_ffn_down_w': 3.971}
    for name, (base, spread) in spreads.items():
        noise = np.random.default_rng([zlib.crc32(name.encode()), seed]).standard_normal(out[name].shape)
        drawn = base * np.exp(spread * noise) if base else spread * noise
        out[name] = jnp.asarray(drawn.astype(out[name].dtype))
    for name, factor in factors.items():
        out[name] = (out[name] * factor).astype(out[name].dtype)
    return out
```

```python
from contextlib import ExitStack, contextmanager

import numpy as np

import concourse.bass as bass
from concourse import mybir

F32 = mybir.dt.float32
BF16 = mybir.dt.bfloat16
I32 = mybir.dt.int32
U32 = mybir.dt.uint32
ALU = mybir.AluOpType
ACT = mybir.ActivationFunctionType
AX = mybir.AxisListType

P = 128
B, S, H = 2, 1024, 256
T = B * S
NT = T // P
KH = H // P
CH = 512
NC = T // CH
SUB = CH // P
TOPK = 4
I = 128
WE = 2 * KH * I + H
HEADS, D = 16, 16
BH = B * HEADS
KT = S // P
SEGS = 6
ROWS = SEGS * D
VD = D + 1
NS = 64
FI = 704
DECAY = 0.95
LN_EPS = 1e-5
RMS_EPS = 1e-6
CLIP = 7.0
NEG = -1e30

BASE = 8


def ready(t):
    return t + BASE + 1


def free(t, ring):
    return t + BASE + 1 - ring


def at(tensor, i):
    if isinstance(i, int):
        return tensor[:, i, :]
    return tensor[:, bass.ds(i, 1), :].rearrange("p a h -> p (a h)")


def col(tensor, i):
    if isinstance(i, int):
        return tensor[:, i:i + 1]
    return tensor[:, bass.ds(i, 1)]


def flat(ap):
    return ap.rearrange("p a b -> p (a b)")


class Step:

    def __init__(self, m, r, n):
        self.m, self.r, self.n = m, r, n

    def on(self, lag):
        return not isinstance(self.m, int) or 0 <= 4 * self.m + self.r - lag < self.n

    def tile(self, lag):
        q = self.r - lag
        return 4 * self.m + q, q % 4, self.m + q // 4


def pipeline(eng, n, step, lags, peel=2):
    for m in range(n // 4):
        for r in range(4):
            step(Step(m, r, n))
    for r in range(lags):
        step(Step(n // 4, r, n))


def settle(eng):
    eng.nop(nofuse=True)


class Chain:

    def __init__(self, eng, sem):
        self.eng, self.sem, self.n = eng, sem, 0

    def __call__(self, ins):
        self.n += 1
        ins.then_inc(self.sem, 1)
        self.eng.wait_ge(self.sem, self.n)


class Core:

    def __init__(self, nc):
        self.nc, self.open = nc, []

    def sem(self, name):
        self.open.append(self.nc.alloc_semaphore(name=name))
        return self.open[-1]

    @contextmanager
    def layer(self):
        outer, self.open = self.open, []
        yield
        self.nc.clear_and_free_semaphores(self.open)
        self.nc.all_engine_barrier()
        self.open = outer

    def sems(self, stage, names):
        return {n: self.sem(f"{stage}_{n}") for n in names.split()}


def scratch(nc, ctx):
    def sb(name, shape, dt=F32):
        return ctx.enter_context(nc.sbuf_tensor(name, shape, dt))

    def ps(name, shape, dt=F32):
        return ctx.enter_context(nc.psum_tensor(name, shape, dt))
    return sb, ps


def open_sems(eng, *sems):
    for s in sems:
        eng.sem_inc(s, BASE)



def norm_stats(core, stage, src, rms=False):
    nc = core.nc
    with ExitStack() as ctx:
        sb, _ = scratch(nc, ctx)
        st = sb(f"{stage}_st", [P, NT, 6])
        work = sb(f"{stage}_work", [P, 6, NT])
        mean, dev, var, root, ysq, tmp = (work[:, i, :] for i in range(6))
        s = core.sems(stage, "stats chain var root")
        rstd, nmr = core.rstd, core.nmr

        with nc.Block() as block:
            @block.vector
            def _(dve):
                with dve.Fori(0, NT) as t:
                    nc.vector.bn_stats(at(st, t), at(src, t)).then_inc(s["stats"], 1)
                dve.wait_ge(s["stats"], NT)
                do = Chain(dve, s["chain"])

                def inverse_root(out, value):
                    nc.vector.tensor_copy(tmp, value).then_inc(s["var"], 1)
                    inverse_root.n += 1
                    dve.wait_ge(s["root"], inverse_root.n)
                    do(nc.vector.reciprocal(out, root))
                    do(nc.vector.tensor_tensor(ysq, out, out, ALU.mult))
                    do(nc.vector.tensor_tensor(ysq, ysq, tmp, ALU.mult))
                    do(nc.vector.tensor_scalar(ysq, ysq, -0.5, 1.5, ALU.mult, ALU.add))
                    do(nc.vector.tensor_tensor(out, out, ysq, ALU.mult))
                inverse_root.n = 0

                do(nc.vector.tensor_tensor(mean, st[:, :, 1], st[:, :, 4], ALU.add))
                do(nc.vector.tensor_tensor(dev, st[:, :, 1], st[:, :, 4], ALU.subtract))
                do(nc.vector.tensor_scalar(mean, mean, 0.5, None, ALU.mult))
                do(nc.vector.tensor_scalar(dev, dev, 0.5, None, ALU.mult))
                do(nc.vector.tensor_tensor(dev, dev, dev, ALU.mult))
                do(nc.vector.tensor_tensor(var, st[:, :, 2], st[:, :, 5], ALU.add))
                do(nc.vector.scalar_tensor_tensor(var, var, 1.0 / H, dev, ALU.mult, ALU.add))
                do(nc.vector.tensor_scalar(dev, var, LN_EPS, None, ALU.add))
                inverse_root(rstd[:, :], dev)
                do(nc.vector.scalar_tensor_tensor(nmr[:, :], mean, -1.0, rstd[:, :], ALU.mult, ALU.mult))
                if rms:
                    do(nc.vector.tensor_tensor(var, var, rstd[:, :], ALU.mult))
                    do(nc.vector.tensor_tensor(var, var, rstd[:, :], ALU.mult))
                    do(nc.vector.tensor_scalar(var, var, RMS_EPS, None, ALU.add))
                    inverse_root(core.rstd2[:, :], var)
                    do(nc.vector.tensor_tensor(core.rstd2[:, :], core.rstd2[:, :], rstd[:, :], ALU.mult))
                    do(nc.vector.scalar_tensor_tensor(core.nmr2[:, :], mean, -1.0, core.rstd2[:, :],
                                                      ALU.mult, ALU.mult))
                    do(nc.vector.tensor_scalar(core.rstd1[:, :], rstd[:, :], 1.0, None, ALU.add))

            @block.scalar
            def _(act):
                for n in range(2 if rms else 1):
                    act.wait_ge(s["var"], n + 1)
                    nc.scalar.activation(root, tmp, ACT.Sqrt).then_inc(s["root"], 1)



class Front:

    def __init__(self, core, stage, sb, psT, src, wait_used):
        self.core, self.nc, self.src = core, core.nc, src
        self.xn = [sb(f"{stage}_xn{i}", [P, H]) for i in range(4)]
        self.xt = [sb(f"{stage}_xt{i}", [P, KH, CH]) for i in range(2)]
        self.psT = psT
        self.s = core.sems(stage, "xn turned xt")
        self.wait_used = wait_used

    def open(self, eng, name):
        open_sems(eng, self.s[name])

    def vector(self, dve, c, group=None, done=None):
        for sub in range(SUB):
            t = SUB * c + sub
            g = SUB * (c if group is None else group) + sub
            dve.wait_ge(self.s["turned"], free(t, 4))
            ins = self.nc.vector.tensor_scalar(self.xn[sub][:, :], at(self.src, g), col(self.core.rstd, g),
                                               col(self.core.nmr, g), ALU.mult, ALU.add)
            ins.then_inc(done or self.s["xn"], 1)

    def tensor(self, pe, c):
        for sub in range(SUB):
            t = SUB * c + sub
            pe.wait_ge(self.s["xn"], ready(t))
            pe.wait_ge(self.s["xt"], free(t, 2))
            for k in range(KH):
                ins = self.nc.tensor.transpose(self.psT[sub % 2][:, k * P:(k + 1) * P],
                                               self.xn[sub][:, k * P:(k + 1) * P], self.core.ident[:, :])
            ins.then_inc(self.s["turned"], 1)

    def scalar(self, act, c, slot):
        self.wait_used(act, c)
        for sub in range(SUB):
            t = SUB * c + sub
            act.wait_ge(self.s["turned"], ready(t))
            self.nc.scalar.activation(self.xt[slot][:, :, sub * P:(sub + 1) * P],
                                      self.psT[sub % 2][:, 0:H].rearrange("p (k c) -> p k c", k=KH),
                                      ACT.Copy).then_inc(self.s["xt"], 1)



def layer0_attention(core, wv, wg, bg, wq, bq, wo):
    nc, x = core.nc, core.x
    norm_stats(core, "n0", x)
    with ExitStack() as ctx:
        sb, ps = scratch(nc, ctx)
        w = {n: sb(f"a0_w{n}", [P, KH, H]) for n in "vgqo"}
        bias = {n: sb(f"a0_b{n}", [P, KH]) for n in "gq"}
        decay = sb("a0_decay", [P, CH])
        sig_g = [sb(f"a0_sg{m}", [P, CH]) for m in range(KH)]
        sig_q = [sb(f"a0_sq{m}", [P, CH]) for m in range(KH)]
        store = [sb(f"a0_st{m}", [P, CH]) for m in range(KH)]
        mem = [[sb(f"a0_m{c}{m}", [P, CH]) for m in range(KH)] for c in range(2)]
        load = [[sb(f"a0_l{c}{m}", [P, CH]) for m in range(KH)] for c in range(2)]
        psT = [ps(f"a0_pT{i}", [P, CH]) for i in range(2)]
        psO = [ps(f"a0_pO{i}", [P, CH]) for i in range(2)]
        psG, psQ = ps("a0_pG", [P, CH]), ps("a0_pQ", [P, CH])
        psV = [ps(f"a0_pV{i}", [P, CH]) for i in range(2)]
        s = core.sems("a0", "weights decay pg pv pq sg sq store mem load po added")
        front = Front(core, "a0", sb, psT, x, lambda act, c: act.wait_ge(s["pq"], ready(KH * (c - 2) + KH - 1)))
        scale2 = float(np.float32(np.sqrt(1.0 - DECAY))) ** 2

        with nc.Block() as block:
            @block.sync
            def _(sp):
                for n, src in (("v", wv), ("g", wg), ("q", wq), ("o", wo)):
                    sp.dma_start(w[n][:, :, :], src).then_inc(s["weights"], 16)
                for n, src in (("g", bg), ("q", bq)):
                    sp.dma_start(bias[n][:, :], src).then_inc(s["weights"], 16)

            @block.tensor
            def _(pe):
                front.open(pe, "turned")
                open_sems(pe, s["pg"], s["pv"], s["pq"], s["po"])
                pe.wait_ge(s["weights"], 96)
                with pe.Fori(0, NC // 2) as b:
                    for cc in range(2):
                        c = 2 * b + cc
                        front.tensor(pe, c)
                        pe.wait_ge(front.s["xt"], ready(SUB * c + SUB - 1))
                        for m in range(KH):
                            e = 2 * c + m
                            for name, dst, ring, freed, done in (("g", psG, 1, "sg", "pg"), ("v", psV[m], 2, "store", "pv"),
                                                                 ("q", psQ, 1, "sq", "pq")):
                                pe.wait_ge(s[freed], free(e, ring))
                                for k in range(KH):
                                    ins = nc.tensor.matmul(dst[:, :], w[name][:, k, m * P:(m + 1) * P],
                                                           front.xt[cc][:, k, :], start=k == 0, stop=k == KH - 1)
                                ins.then_inc(s[done], 1)
                        pe.wait_ge(s["load"], ready(2 * c + 1))
                        for sub in range(SUB):
                            pe.wait_ge(s["added"], free(SUB * c + sub, 2))
                            for m in range(KH):
                                ins = nc.tensor.matmul(psO[sub % 2][:, 0:H], load[cc][m][:, sub * P:(sub + 1) * P],
                                                       w["o"][:, m, :], start=m == 0, stop=m == KH - 1)
                            ins.then_inc(s["po"], 1)

            @block.scalar
            def _(act):
                front.open(act, "xt")
                open_sems(act, s["sg"], s["sq"])
                nc.scalar.preload_act_table(ACT.Sigmoid)
                act.wait_ge(s["weights"], 96)
                with act.Fori(0, NC // 2) as b:
                    for cc in range(2):
                        c = 2 * b + cc
                        front.scalar(act, c, cc)
                        for m in range(KH):
                            e = 2 * c + m
                            act.wait_ge(s["pg"], ready(e))
                            act.wait_ge(s["store"], free(e, 2))
                            nc.scalar.activation(sig_g[m][:, :], psG[:, :], ACT.Sigmoid,
                                                 bias=bias["g"][:, m:m + 1]).then_inc(s["sg"], 1)
                            act.wait_ge(s["pq"], ready(e))
                            act.wait_ge(s["load"], free(e, 2))
                            nc.scalar.activation(sig_q[m][:, :], psQ[:, :], ACT.Sigmoid,
                                                 bias=bias["q"][:, m:m + 1]).then_inc(s["sq"], 1)

            @block.vector
            def _(dve):
                front.open(dve, "xn")
                open_sems(dve, s["store"], s["mem"], s["load"], s["added"])
                nc.vector.memset(decay[:, :], DECAY).then_inc(s["decay"], 1)
                dve.wait_ge(s["decay"], 1)
                with dve.Fori(0, NC // 2) as b:
                    for cc in range(2):
                        c = 2 * b + cc
                        front.vector(dve, c)
                        for m in range(KH):
                            e = 2 * c + m
                            dve.wait_ge(s["sg"], ready(e))
                            dve.wait_ge(s["pv"], ready(e))
                            dve.wait_ge(s["mem"], free(e, 2))
                            nc.vector.tensor_tensor(store[m][:, :], psV[m][:, :], sig_g[m][:, :],
                                                    ALU.mult).then_inc(s["store"], 1)
                            dve.wait_ge(s["store"], ready(e))
                            nc.vector.tensor_tensor_scan(mem[cc][m][:, :], decay[:, :], store[m][:, :],
                                                         mem[0][m][:, CH - 1:CH] if cc else 0.0,
                                                         ALU.mult, ALU.add).then_inc(s["mem"], 1)
                            dve.wait_ge(s["mem"], ready(e))
                            dve.wait_ge(s["sq"], ready(e))
                            dve.wait_ge(s["po"], free(SUB * c, SUB + 1))
                            nc.vector.scalar_tensor_tensor(load[cc][m][:, :], mem[cc][m][:, :], scale2, sig_q[m][:, :],
                                                           ALU.mult, ALU.mult).then_inc(s["load"], 1)
                        for sub in range(SUB):
                            t = SUB * c + sub
                            dve.wait_ge(s["po"], ready(t))
                            nc.vector.tensor_tensor(at(x, t), at(x, t), psO[sub % 2][:, 0:H],
                                                    ALU.add).then_inc(s["added"], 1)



class Moe:

    def __init__(self, core, name, experts, kind, weights):
        self.core, self.name, self.E, self.kind, self.w = core, name, experts, kind, weights
        most = (T * TOPK - experts) // P + experts
        self.tiles = -(-most // 4) * 4


class FfnPipe:

    def __init__(self, core, stage, sb, ps, clip):
        self.core, self.nc, self.clip = core, core.nc, clip
        self.src = [sb(f"{stage}_src{i}", [P, H]) for i in range(4)]
        self.xt = [sb(f"{stage}_xt{i}", [P, KH, P]) for i in range(2)]
        self.gu = [sb(f"{stage}_gu{i}", [P, 2 * I]) for i in range(2)]
        self.act = [sb(f"{stage}_act{i}", [P, I]) for i in range(2)]
        self.h = [sb(f"{stage}_h{i}", [P, I]) for i in range(2)]
        self.ht = [sb(f"{stage}_ht{i}", [P, I]) for i in range(2)]
        self.psT = [ps(f"{stage}_pT{i}", [P, CH]) for i in range(2)]
        self.psG = [ps(f"{stage}_pG{i}", [P, CH]) for i in range(2)]
        self.psH = [ps(f"{stage}_pH{i}", [P, CH]) for i in range(2)]
        self.psO = [ps(f"{stage}_pO{i}", [P, CH]) for i in range(2)]
        self.s = core.sems(stage, "turned xt pg clip act h ph ht po out")

    def open_tensor(self, pe):
        open_sems(pe, *(self.s[n] for n in ("turned", "pg", "ph", "po")))

    def open_scalar(self, act):
        open_sems(act, *(self.s[n] for n in ("xt", "act")))

    def open_vector(self, dve):
        open_sems(dve, *(self.s[n] for n in ("clip", "ht", "out")))
        if not self.clip:
            open_sems(dve, self.s["h"])

    def open_pool(self, pool):
        if self.clip:
            open_sems(pool, self.s["h"])

    def tensor(self, pe, st, wait_source, weights, after_gate=None):
        nc, s = self.nc, self.s
        if st.on(0):
            t, r, m = st.tile(0)
            wait_source(pe, t, r, m)
            pe.wait_ge(s["xt"], free(t, 2))
            for k in range(KH):
                ins = nc.tensor.transpose(self.psT[r % 2][:, k * P:(k + 1) * P],
                                          self.src[r][:, k * P:(k + 1) * P], self.core.ident[:, :])
            ins.then_inc(s["turned"], 1)
        if st.on(1):
            t, r, _ = st.tile(1)
            w = weights(pe, t, 0)
            pe.wait_ge(s["xt"], ready(t))
            pe.wait_ge(s["clip" if self.clip else "h"], free(t, 2))
            for k in range(KH):
                ins = nc.tensor.matmul(self.psG[r % 2][:, 0:2 * I], self.xt[r % 2][:, k, :], w(k * 2 * I, 2 * I),
                                       start=k == 0, stop=k == KH - 1)
            if after_gate:
                after_gate(pe, t, r)
            else:
                ins.then_inc(s["pg"], 1)
        if st.on(2):
            t, r, _ = st.tile(2)
            pe.wait_ge(s["h"], ready(t))
            pe.wait_ge(s["ht"], free(t, 2))
            nc.tensor.transpose(self.psH[r % 2][:, 0:I], self.h[r % 2][:, :],
                                self.core.ident[:, :]).then_inc(s["ph"], 1)
        if st.on(3):
            t, r, _ = st.tile(3)
            w = weights(pe, t, 1)
            pe.wait_ge(s["ht"], ready(t))
            pe.wait_ge(s["out"], free(t, 2))
            nc.tensor.matmul(self.psO[r % 2][:, 0:H], self.ht[r % 2][:, :], w(2 * KH * I, H),
                             start=True, stop=True).then_inc(s["po"], 1)

    def scalar(self, act, st):
        nc, s = self.nc, self.s
        if st.on(0):
            t, r, _ = st.tile(0)
            act.wait_ge(s["turned"], ready(t))
            act.wait_ge(s["pg"], free(t, 2))
            nc.scalar.activation(flat(self.xt[r % 2][:, :, :]), self.psT[r % 2][:, 0:H],
                                 ACT.Copy).then_inc(s["xt"], 1)
        if st.on(1):
            t, r, _ = st.tile(1)
            act.wait_ge(s["clip" if self.clip else "pg"], ready(t))
            act.wait_ge(s["h"], free(t, 2))
            gate = self.gu[r % 2][:, 0:I] if self.clip else self.psG[r % 2][:, 0:I]
            nc.scalar.activation(self.act[r % 2][:, :], gate, ACT.Silu).then_inc(s["act"], 1)

    def vector(self, dve, st, take):
        nc, s = self.nc, self.s
        if st.on(1):
            t, r, _ = st.tile(1)
            if self.clip:
                dve.wait_ge(s["pg"], ready(t))
                dve.wait_ge(s["h"], free(t, 2))
                nc.vector.tensor_scalar(self.gu[r % 2][:, :], self.psG[r % 2][:, 0:2 * I], -CLIP, CLIP,
                                        ALU.max, ALU.min).then_inc(s["clip"], 1)
            else:
                dve.wait_ge(s["act"], ready(t))
                dve.wait_ge(s["ph"], free(t, 2))
                nc.vector.tensor_tensor(self.h[r % 2][:, :], self.psG[r % 2][:, I:2 * I], self.act[r % 2][:, :],
                                        ALU.mult).then_inc(s["h"], 1)
        if st.on(2):
            t, r, _ = st.tile(2)
            dve.wait_ge(s["ph"], ready(t))
            dve.wait_ge(s["po"], free(t, 2))
            nc.vector.tensor_copy(self.ht[r % 2][:, :], self.psH[r % 2][:, 0:I]).then_inc(s["ht"], 1)
        if st.on(3):
            t, r, m = st.tile(3)
            dve.wait_ge(s["po"], ready(t))
            take(t, r, m).then_inc(s["out"], 1)

    def pool(self, pool, st):
        if self.clip and st.on(1):
            t, r, _ = st.tile(1)
            pool.wait_ge(self.s["act"], ready(t))
            pool.wait_ge(self.s["ph"], free(t, 2))
            self.nc.gpsimd.tensor_tensor(self.h[r % 2][:, :], self.gu[r % 2][:, I:2 * I], self.act[r % 2][:, :],
                                         ALU.mult).then_inc(self.s["h"], 1)


def moe_dense(moe, shared, router, norm_w, logits):
    core, nc, E = moe.core, moe.core.nc, moe.E
    x = core.x
    stage = moe.name + "d"
    rms = norm_w is not None
    norm_stats(core, moe.name + "n", x, rms)
    with ExitStack() as ctx:
        sb, ps = scratch(nc, ctx)
        pipe = FfnPipe(core, stage, sb, ps, moe.kind == "softplus")
        ws = sb(f"{stage}_ws", [P, WE])
        wr = sb(f"{stage}_wr", [P, KH, E])
        nw = sb(f"{stage}_nw", [P, H]) if rms else None
        s = core.sems(stage, "weights norm xn logits")
        kept = [core.sem(f"{stage}_kept{i}") for i in range(4)]

        with nc.Block() as block:
            @block.sync
            def _(sp):
                sp.dma_start(ws[:, :], shared).then_inc(s["weights"], 16)
                sp.dma_start(wr[:, :, :], router).then_inc(s["weights"], 16)
                if rms:
                    sp.dma_start(nw[:, :], norm_w).then_inc(s["weights"], 16)

                def step(st):
                    if st.on(0):
                        t, r, _ = st.tile(0)
                        sp.wait_ge(s["xn"], ready(t))
                        sp.dma_start(at(core.rows, t), pipe.src[r][:, :]).then_inc(kept[r], 16)
                pipeline(sp, NT, step, 0)
                for r in range(4):
                    sp.wait_ge(kept[r], 16 * NT // 4)

            @block.tensor
            def _(pe):
                pipe.open_tensor(pe)
                pe.wait_ge(s["weights"], 48 if rms else 32)

                def source(pe, t, r, m):
                    pe.wait_ge(s["xn"], ready(t))

                def after_gate(pe, t, r):
                    pe.wait_ge(s["logits"], free(t, 2))
                    pe.wait_ge(pipe.s["ht"], free(t, 2))
                    for k in range(KH):
                        ins = nc.tensor.matmul(pipe.psH[r % 2][:, I:I + E], pipe.xt[r % 2][:, k, :], wr[:, k, :],
                                               start=k == 0, stop=k == KH - 1)
                    ins.then_inc(pipe.s["pg"], 1)

                def step(st):
                    pipe.tensor(pe, st, source, lambda pe, t, part: lambda a, n: ws[:, a:a + n], after_gate)
                pipeline(pe, NT, step, 3)

            @block.scalar
            def _(act):
                pipe.open_scalar(act)
                nc.scalar.preload_act_table(ACT.Silu)
                pipeline(act, NT, lambda st: pipe.scalar(act, st), 1)

            @block.gpsimd
            def _(pool):
                pipe.open_pool(pool)
                if pipe.clip:
                    pipeline(pool, NT, lambda st: pipe.pool(pool, st), 1)

            @block.vector
            def _(dve):
                pipe.open_vector(dve)
                open_sems(dve, s["xn"], s["norm"], s["logits"])
                if rms:
                    dve.wait_ge(s["weights"], 48)

                def take(t, r, m):
                    return nc.vector.tensor_tensor(at(x, t), at(x, t), pipe.psO[r % 2][:, 0:H], ALU.add)

                def step(st):
                    if st.on(0):
                        t, r, m = st.tile(0)
                        dve.wait_ge(pipe.s["turned"], free(t, 4))
                        if not isinstance(m, int) or m:
                            dve.wait_ge(kept[r], 16 * m)
                        rstd, nmr = (core.rstd2, core.nmr2) if rms else (core.rstd, core.nmr)
                        ins = nc.vector.tensor_scalar(pipe.src[r][:, :], at(x, t), col(rstd, t), col(nmr, t),
                                                      ALU.mult, ALU.add)
                        if rms:
                            ins.then_inc(s["norm"], 1)
                            dve.wait_ge(s["norm"], ready(2 * t))
                            nc.vector.tensor_tensor(pipe.src[r][:, :], pipe.src[r][:, :], nw[:, :],
                                                    ALU.mult).then_inc(s["xn"], 1)
                            nc.vector.tensor_scalar(at(x, t), at(x, t), col(core.rstd1, t), col(core.nmr, t),
                                                    ALU.mult, ALU.add).then_inc(s["norm"], 1)
                        else:
                            ins.then_inc(s["xn"], 1)
                    if st.on(1):
                        t, r, _ = st.tile(1)
                        dve.wait_ge(pipe.s["pg"], ready(t))
                        nc.vector.tensor_copy(at(logits, t), pipe.psH[r % 2][:, I:I + E]).then_inc(s["logits"], 1)
                    if rms and st.on(3):
                        dve.wait_ge(s["norm"], ready(2 * st.tile(3)[0] + 1))
                    pipe.vector(dve, st, take)
                pipeline(dve, NT, step, 3)


def moe_route(moe, logits, expert_bias, out):
    core, nc, E, name = moe.core, moe.core.nc, moe.E, moe.name
    NE = moe.tiles
    with ExitStack() as ctx:
        sb, ps = scratch(nc, ctx)
        score = sb(f"{name}_score", [P, NT, E])
        sel = sb(f"{name}_sel", [P, NT, E])
        tmp = sb(f"{name}_tmp", [P, NT, E])
        tmp2 = sb(f"{name}_tmp2", [P, NT, E])
        bias = sb(f"{name}_bias", [P, E])
        top = sb(f"{name}_top", [P, NT, 8])
        idx = sb(f"{name}_idx", [P, NT, 8], U32)
        idxf = sb(f"{name}_idxf", [P, NT, TOPK])
        hot = sb(f"{name}_hot", [P, NT, TOPK, E])
        prod = sb(f"{name}_prod", [P, NT, TOPK, E])
        mask = sb(f"{name}_mask", [P, NT, E], BF16)
        before = sb(f"{name}_before", [P, NT + 1, E], BF16)
        row = sb(f"{name}_row", [P, 8, NT])
        count = sb(f"{name}_count", [P, 4, E])
        counti = sb(f"{name}_counti", [P, E], I32)
        slot = sb(f"{name}_slot", [P, NT, TOPK])
        sloti = sb(f"{name}_sloti", [P, 2, NT, TOPK], I32)
        hi = sb(f"{name}_hi", [P, NT * TOPK])
        lo = sb(f"{name}_lo", [P, NT * TOPK])
        eid = sb(f"{name}_eid", [P, 1])
        ge = sb(f"{name}_ge", [P, E])
        inv = sb(f"{name}_inv", [P, NE])
        pick = [sb(f"{name}_pick{i}", [P, TOPK, P], BF16) for i in range(2)]
        place = [sb(f"{name}_place{i}", [P, TOPK, 2, NE], BF16) for i in range(2)]
        psR = ps(f"{name}_psR", [P, NT, E])
        psC = ps(f"{name}_psC", [P, E])
        psE = ps(f"{name}_psE", [P, P])
        psI = ps(f"{name}_psI", [P, 2, NE])
        s = core.sems(name + "r", "bias chain act acted mask ranks eid row picks used")

        def bc(ap, shape):
            return ap.to_broadcast(shape) if False else ap.broadcast_to(shape)

        with nc.Block() as block:
            @block.sync
            def _(sp):
                if expert_bias is not None:
                    sp.dma_start(bias[:, :], expert_bias).then_inc(s["bias"], 16)

            @block.scalar
            def _(act):
                if moe.kind == "sigmoid":
                    nc.scalar.activation(score[:, :, :], logits[:, :, :], ACT.Sigmoid).then_inc(s["acted"], 1)
                elif moe.kind == "softmax":
                    act.wait_ge(s["act"], 1)
                    nc.scalar.activation(tmp[:, :, :], tmp2[:, :, :], ACT.Exp).then_inc(s["acted"], 1)
                else:
                    act.wait_ge(s["act"], 1)
                    nc.scalar.activation(tmp[:, :, :], tmp2[:, :, :], ACT.Exp).then_inc(s["acted"], 1)
                    act.wait_ge(s["act"], 2)
                    nc.scalar.activation(score[:, :, :], tmp2[:, :, :], ACT.Ln).then_inc(s["acted"], 1)
                    act.wait_ge(s["act"], 3)
                    nc.scalar.activation(score[:, :, :], tmp[:, :, :], ACT.Sqrt).then_inc(s["acted"], 1)

            @block.vector
            def _(dve):
                do = Chain(dve, s["chain"])
                V = nc.vector
                dve.wait_ge(s["acted"], 1) if moe.kind == "sigmoid" else None
                if moe.kind == "softmax":
                    rmax, rsum = row[:, 0, :], row[:, 1, :]
                    do(V.tensor_reduce(rmax, logits[:, :, :], AX.X, ALU.max))
                    V.tensor_tensor(tmp2[:, :, :], logits[:, :, :], rmax.unsqueeze(2).broadcast_to([P, NT, E]),
                                    ALU.subtract).then_inc(s["act"], 1)
                    dve.wait_ge(s["acted"], 1)
                    do(V.tensor_reduce(rsum, tmp[:, :, :], AX.X, ALU.add))
                    do(V.reciprocal(rsum, rsum))
                    do(V.tensor_tensor(score[:, :, :], tmp[:, :, :], rsum.unsqueeze(2).broadcast_to([P, NT, E]),
                                       ALU.mult))
                if moe.kind == "softplus":
                    do(V.tensor_scalar(tmp2[:, :, :], logits[:, :, :], -1.0, None, ALU.mult))
                    V.tensor_tensor(tmp2[:, :, :], tmp2[:, :, :], logits[:, :, :], ALU.min).then_inc(s["act"], 1)
                    dve.wait_ge(s["acted"], 1)
                    V.tensor_scalar(tmp2[:, :, :], tmp[:, :, :], 1.0, None, ALU.add).then_inc(s["act"], 1)
                    dve.wait_ge(s["act"], 2)
                    dve.wait_ge(s["acted"], 2)
                    do(V.tensor_scalar(tmp2[:, :, :], tmp2[:, :, :], -1.0, None, ALU.add))
                    do(V.tensor_scalar(sel[:, :, :], tmp2[:, :, :], 0.0, None, ALU.is_equal))
                    do(V.tensor_tensor(tmp2[:, :, :], tmp2[:, :, :], sel[:, :, :], ALU.add))
                    do(V.tensor_tensor(sel[:, :, :], score[:, :, :], sel[:, :, :], ALU.add))
                    do(V.reciprocal(tmp2[:, :, :], tmp2[:, :, :]))
                    do(V.tensor_tensor(sel[:, :, :], sel[:, :, :], tmp2[:, :, :], ALU.mult))
                    do(V.tensor_tensor(tmp[:, :, :], tmp[:, :, :], sel[:, :, :], ALU.mult))
                    V.scalar_tensor_tensor(tmp[:, :, :], logits[:, :, :], 0.0, tmp[:, :, :], ALU.max,
                                           ALU.add).then_inc(s["act"], 1)
                    dve.wait_ge(s["act"], 3)
                    dve.wait_ge(s["acted"], 3)
                choose = score
                if expert_bias is not None:
                    dve.wait_ge(s["bias"], 16)
                    do(V.tensor_tensor(sel[:, :, :], score[:, :, :], bias[:, :].unsqueeze(1).broadcast_to([P, NT, E]),
                                       ALU.add))
                    choose = sel
                for t in range(NT):
                    V.max(top[:, t, :], choose[:, t, :]).then_inc(s["chain"], 1)
                do.n += NT
                dve.wait_ge(s["chain"], do.n)
                for t in range(NT):
                    V.max_index(idx[:, t, :], top[:, t, :], choose[:, t, :]).then_inc(s["chain"], 1)
                do.n += NT
                dve.wait_ge(s["chain"], do.n)
                do(V.tensor_copy(idxf[:, :, :], idx[:, :, 0:TOPK]))
                for k in range(TOPK):
                    V.tensor_tensor(hot[:, :, k, :], core.iota[:, 0:E].unsqueeze(1).broadcast_to([P, NT, E]),
                                    idxf[:, :, k:k + 1].broadcast_to([P, NT, E]), ALU.is_equal).then_inc(s["chain"], 1)
                do.n += TOPK
                dve.wait_ge(s["chain"], do.n)
                V.tensor_tensor(tmp[:, :, :], hot[:, :, 0, :], hot[:, :, 1, :], ALU.add).then_inc(s["chain"], 1)
                V.tensor_tensor(tmp2[:, :, :], hot[:, :, 2, :], hot[:, :, 3, :], ALU.add).then_inc(s["chain"], 1)
                do.n += 2
                dve.wait_ge(s["chain"], do.n)
                do(V.tensor_tensor(mask[:, :, :], tmp[:, :, :], tmp2[:, :, :], ALU.add))
                do(V.memset(before[:, 0, :], 0.0))
                for t in range(NT):
                    ins = V.tensor_tensor(before[:, t + 1, :], before[:, t, :], mask[:, t, :], ALU.add)
                    if t < NT - 1:
                        do(ins)
                    else:
                        ins.then_inc(s["mask"], 1)

                def chosen(dst, values):
                    for k in range(TOPK):
                        V.tensor_tensor(prod[:, :, k, :], hot[:, :, k, :], values, ALU.mult).then_inc(s["chain"], 1)
                    do.n += TOPK
                    dve.wait_ge(s["chain"], do.n)
                    do(V.tensor_reduce(dst, prod[:, :, :, :], AX.X, ALU.add))
                chosen(out["weight"][:, :, :], score[:, :, :])
                total = row[:, 2, :]
                do(V.tensor_reduce(total, out["weight"][:, :, :], AX.X, ALU.add))
                if moe.kind == "softplus":
                    do(V.tensor_scalar(total, total, 1e-20, None, ALU.add))
                do(V.reciprocal(total, total))
                do(V.tensor_tensor(out["weight"][:, :, :], out["weight"][:, :, :],
                                   total.unsqueeze(2).broadcast_to([P, NT, TOPK]), ALU.mult))

                cnt, need, end, start = (count[:, i, :] for i in range(4))
                dve.wait_ge(s["ranks"], 1)
                do(V.tensor_scalar(cnt, psC[:, :], float(P - 1), None, ALU.add))
                do(V.tensor_copy(counti[:, :], cnt))
                do(V.tensor_scalar(counti[:, :], counti[:, :], 7, None, ALU.arith_shift_right))
                do(V.tensor_copy(need, counti[:, :]))
                do(V.tensor_tensor_scan(end, core.onesf[:, 0:E], need, 0.0, ALU.mult, ALU.add))
                do(V.tensor_tensor(start, end, need, ALU.subtract))
                do(V.tensor_scalar(ge[:, :], end, core.part[:, 0:1], None, ALU.is_le))
                do(V.tensor_reduce(eid[:, :], ge[:, :], AX.X, ALU.add))
                V.tensor_scalar(eid[:, :], eid[:, :], float(E - 1), None, ALU.min).then_inc(s["eid"], 1)
                do(V.tensor_scalar(start, start, float(P), None, ALU.mult))
                if moe.kind == "softmax":
                    do(V.tensor_scalar(tmp[:, :, :], psR[:, :, :], float(2 * T * TOPK // E - 1), None, ALU.min))
                    do(V.tensor_tensor(tmp[:, :, :], tmp[:, :, :], start.unsqueeze(1).broadcast_to([P, NT, E]),
                                       ALU.add))
                    chosen(slot[:, :, :], tmp[:, :, :])
                    do(V.tensor_copy(out["read"][:, :, :], slot[:, :, :]))
                do(V.tensor_tensor(tmp[:, :, :], psR[:, :, :], start.unsqueeze(1).broadcast_to([P, NT, E]), ALU.add))
                chosen(slot[:, :, :], tmp[:, :, :])
                if moe.kind != "softmax":
                    do(V.tensor_copy(out["read"][:, :, :], slot[:, :, :]))
                do(V.tensor_copy(sloti[:, 0, :, :], slot[:, :, :]))
                do(V.tensor_scalar(sloti[:, 1, :, :], sloti[:, 0, :, :], 7, None, ALU.arith_shift_right))
                do(V.tensor_copy(hi[:, :], sloti[:, 1, :, :].rearrange("p a b -> p (a b)")))
                do(V.scalar_tensor_tensor(lo[:, :], hi[:, :], -float(P), slot[:, :, :].rearrange("p a b -> p (a b)"),
                                          ALU.mult, ALU.add))
                with dve.Fori(0, NT // 2) as n:
                    for par in range(2):
                        t = 2 * n + par
                        dve.wait_ge(s["used"], free(t, 2))
                        for k in range(TOPK):
                            V.tensor_scalar(pick[par][:, k, :], core.iotab[:, :], col(lo, 4 * t + k), None, ALU.is_equal)
                            V.tensor_scalar(place[par][:, k, 0, :], core.iotab[:, 0:NE], col(hi, 4 * t + k),
                                            core.part[:, 0:1], ALU.is_equal, ALU.mult)
                            ins = V.tensor_scalar(place[par][:, k, 1, :], core.iotab[:, 0:NE], col(hi, 4 * t + k),
                                                  col(core.iota, t), ALU.is_equal, ALU.mult)
                        ins.then_inc(s["picks"], 1)
                dve.wait_ge(s["used"], ready(NT - 1))
                do(V.tensor_copy(inv[:, :], psI[:, 0, :]))
                do(V.scalar_tensor_tensor(inv[:, :], psI[:, 1, :], float(P), inv[:, :], ALU.mult, ALU.add))
                do(V.tensor_copy(out["token"][:, 0:NE], inv[:, :]))
                dve.wait_ge(s["row"], 1)
                do(V.tensor_copy(out["expert"][0:1, 0:P], psE[0:1, :]))

            @block.tensor
            def _(pe):
                open_sems(pe, s["used"])
                pe.wait_ge(s["mask"], 1)
                fr = psR[:, :, :].rearrange("p a b -> p (a b)")
                nc.tensor.matmul(fr, core.earlier[:, :], mask[:, :, :].rearrange("p a b -> p (a b)"),
                                 start=True, stop=False)
                nc.tensor.matmul(fr, core.onesb[:, :], before[:, 0:NT, :].rearrange("p a b -> p (a b)"),
                                 start=False, stop=True)
                nc.tensor.matmul(psC[:, :], core.onesb[:, :], before[:, NT, :], start=True,
                                 stop=True).then_inc(s["ranks"], 1)
                pe.wait_ge(s["eid"], 1)
                nc.tensor.matmul(psE[0:1, :], eid[:, 0:1], core.ident[:, :], start=True, stop=True).then_inc(s["row"], 1)
                for t in range(NT):
                    pe.wait_ge(s["picks"], t + 1)
                    for k in range(TOPK):
                        ins = nc.tensor.matmul(flat(psI[:, :, :]), pick[t % 2][:, k, :], flat(place[t % 2][:, k, :, :]),
                                               start=t + k == 0, stop=t * k == (NT - 1) * (TOPK - 1))
                    ins.then_inc(s["used"], 1)


def moe_experts(moe, out):
    core, nc = moe.core, moe.core.nc
    stage, N = moe.name + "e", moe.tiles
    with ExitStack() as ctx:
        sb, ps = scratch(nc, ctx)
        pipe = FfnPipe(core, stage, sb, ps, moe.kind == "softplus")
        tok = [sb(f"{stage}_tok{i}", [P, 1], I32) for i in range(4)]
        y = [sb(f"{stage}_y{i}", [P, H]) for i in range(4)]
        s = core.sems(stage, "tok")
        got = [core.sem(f"{stage}_got{i}") for i in range(4)]
        kept = [core.sem(f"{stage}_kept{i}") for i in range(4)]
        w3 = moe.w

        with nc.Block() as block:
            @block.gpsimd
            def _(pool):
                pipe.open_pool(pool)
                open_sems(pool, s["tok"])

                def step(st):
                    if st.on(0):
                        t, r, m = st.tile(0)
                        if not isinstance(m, int) or m:
                            pool.wait_ge(got[r], 16 * m)
                        settle(pool)
                        nc.gpsimd.tensor_copy(tok[r][:, :], col(out["token"], t)).then_inc(s["tok"], 1)
                        pool.wait_ge(s["tok"], ready(t))
                        pool.wait_ge(pipe.s["turned"], free(t, 4))
                        settle(pool)
                        pool.indirect_dma_start(pipe.src[r][:, :], None, core.rows_flat,
                                                bass.IndirectOffsetOnAxis(ap=tok[r][:, 0:1].bitcast(U32), axis=0)
                                                ).then_inc(got[r], 16)
                    if pipe.clip and st.on(3):
                        t, r, _ = st.tile(3)
                        pool.wait_ge(pipe.s["act"], ready(t))
                        pool.wait_ge(pipe.s["ph"], free(t, 2))
                        nc.gpsimd.tensor_tensor(pipe.h[r % 2][:, :], pipe.gu[r % 2][:, I:2 * I],
                                                pipe.act[r % 2][:, :], ALU.mult).then_inc(pipe.s["h"], 1)
                pipeline(pool, N, step, 3)

            @block.sync
            def _(sp):
                def step(st):
                    if st.on(3):
                        t, r, _ = st.tile(3)
                        sp.wait_ge(pipe.s["out"], ready(t))
                        sp.dma_start(at(core.results, t), y[r][:, :]).then_inc(kept[r], 16)
                pipeline(sp, N, step, 3)
                for r in range(4):
                    sp.wait_ge(kept[r], 16 * N // 4)

            @block.tensor
            def _(pe):
                pipe.open_tensor(pe)
                for loaded in moe.loaded:
                    pe.wait_ge(loaded, 16)

                def source(pe, t, r, m):
                    pe.wait_ge(got[r], 16 * (m + 1))

                def weights(pe, t, part):
                    e = pe.value_load(out["expert"][0:1, t:t + 1] if isinstance(t, int)
                                      else out["expert"][0:1, bass.ds(t, 1)], min_val=0, max_val=moe.E - 1)
                    return lambda a, n: w3[:, bass.ds(e, 1), a:a + n].rearrange("p a c -> p (a c)")
                pipeline(pe, N, lambda st: pipe.tensor(pe, st, source, weights), 3)

            @block.scalar
            def _(act):
                pipe.open_scalar(act)
                nc.scalar.preload_act_table(ACT.Silu)
                pipeline(act, N, lambda st: pipe.scalar(act, st), 1)

            @block.vector
            def _(dve):
                pipe.open_vector(dve)

                def take(t, r, m):
                    if not isinstance(m, int) or m:
                        dve.wait_ge(kept[r], 16 * m)
                    return nc.vector.tensor_copy(y[r][:, :], pipe.psO[r % 2][:, 0:H])
                pipeline(dve, N, lambda st: pipe.vector(dve, st, take), 3)


def moe_combine(moe, out):
    core, nc = moe.core, moe.core.nc
    stage = moe.name + "c"
    with ExitStack() as ctx:
        sb, _ = scratch(nc, ctx)
        at_slot = [[sb(f"{stage}_at{i}{k}", [P, 1], I32) for k in range(TOPK)] for i in range(2)]
        got_rows = [[sb(f"{stage}_g{i}{k}", [P, H]) for k in range(TOPK)] for i in range(2)]
        s = core.sems(stage, "slots summed")
        got = [[core.sem(f"{stage}_got{i}{k}") for k in range(TOPK)] for i in range(2)]

        with nc.Block() as block:
            @block.gpsimd
            def _(pool):
                open_sems(pool, s["slots"])
                with pool.Fori(0, NT // 2) as n:
                    for par in range(2):
                        t = 2 * n + par
                        pool.wait_ge(s["summed"], ready(TOPK * t - 2 * TOPK + TOPK - 1))
                        settle(pool)
                        for k in range(TOPK):
                            ins = nc.gpsimd.tensor_copy(at_slot[par][k][:, :], col(out["readf"], TOPK * t + k))
                        ins.then_inc(s["slots"], 1)
                        pool.wait_ge(s["slots"], ready(t))
                        settle(pool)
                        for k in range(TOPK):
                            pool.indirect_dma_start(got_rows[par][k][:, :], None, core.results_flat[0:moe.tiles * P, :],
                                                    bass.IndirectOffsetOnAxis(ap=at_slot[par][k][:, 0:1].bitcast(U32),
                                                                              axis=0)).then_inc(got[par][k], 16)

            @block.vector
            def _(dve):
                open_sems(dve, s["summed"])
                with dve.Fori(0, NT // 2) as n:
                    for par in range(2):
                        t = 2 * n + par
                        for k in range(TOPK):
                            e = TOPK * t + k
                            dve.wait_ge(got[par][k], 16 * n + 16)
                            dve.wait_ge(s["summed"], free(e, 1))
                            nc.vector.scalar_tensor_tensor(at(core.x, t), got_rows[par][k][:, :],
                                                           col(out["weightf"], e), at(core.x, t),
                                                           ALU.mult, ALU.add).then_inc(s["summed"], 1)


def moe_layer(moe, shared, router, expert_bias, norm_w=None):
    core, nc, E, name = moe.core, moe.core.nc, moe.E, moe.name
    with ExitStack() as ctx:
        sb, _ = scratch(nc, ctx)
        weight = sb(f"{name}_weight", [P, NT, TOPK])
        read = sb(f"{name}_read", [P, NT, TOPK], I32)
        out = {"weight": weight, "weightf": weight[:, :, :].rearrange("p a b -> p (a b)"),
               "read": read, "readf": read[:, :, :].rearrange("p a b -> p (a b)"),
               "token": sb(f"{name}_token", [P, moe.tiles], I32), "expert": sb(f"{name}_expert", [1, P], I32)}
        with ExitStack() as inner:
            logits = inner.enter_context(nc.sbuf_tensor(f"{name}_logits", [P, NT, E], F32))
            moe_dense(moe, shared, router, norm_w, logits)
            moe_route(moe, logits, expert_bias, out)
        moe_experts(moe, out)
        moe_combine(moe, out)



def layer1_attention(core, shift, gate, gamma, beta, kv, time_decay, time_first, w_out):
    nc, x = core.nc, core.x
    norm_stats(core, "n1", x)
    with ExitStack() as ctx:
        sb, _ = scratch(nc, ctx)
        shifted = sb("a1_shifted", [P, NT, H])
        states = sb("a1_states", [P, S])
        layer1_shift(core, shift, gate, shifted)
        norm_stats(core, "n1s", shifted)
        layer1_scan(core, gamma, beta, kv, time_decay, time_first, shifted, states)
        layer1_out(core, w_out, states)


def layer1_shift(core, shift, gate, shifted):
    nc, x = core.nc, core.x
    with ExitStack() as ctx:
        sb, ps = scratch(nc, ctx)
        w = sb("a1_w", [P, KH, H])
        g_new, g_old = sb("a1_gnew", [P, H]), sb("a1_gold", [P, H])
        xn = [sb(f"a1_xn{q}", [P, H]) for q in range(4)]
        xt = [sb(f"a1_xt{q}", [P, KH, P]) for q in range(2)]
        new = [sb(f"a1_new{q}", [P, H]) for q in range(2)]
        old = [sb(f"a1_old{q}", [P, H]) for q in range(2)]
        psT = [ps(f"a1_pT{q}", [P, CH]) for q in range(2)]
        psS = [ps(f"a1_pS{q}", [P, CH]) for q in range(2)]
        s = core.sems("a1", "weights gate gates xn turned xt ps new old mixed")

        with nc.Block() as block:
            @block.sync
            def _(sp):
                sp.dma_start(w[:, :, :], shift).then_inc(s["weights"], 16)
                sp.dma_start(g_new[:, :], gate).then_inc(s["weights"], 16)

            @block.scalar
            def _(act):
                open_sems(act, s["xt"])
                act.wait_ge(s["weights"], 32)
                nc.scalar.activation(g_new[:, :], g_new[:, :], ACT.Sigmoid).then_inc(s["gate"], 1)
                with act.Fori(0, 4) as n:
                    for q in range(4):
                        e = 4 * n + q
                        act.wait_ge(s["turned"], ready(e))
                        act.wait_ge(s["ps"], free(e, 2))
                        nc.scalar.activation(flat(xt[q % 2][:, :, :]), psT[q % 2][:, 0:H],
                                             ACT.Copy).then_inc(s["xt"], 1)

            @block.tensor
            def _(pe):
                open_sems(pe, s["turned"], s["ps"])
                pe.wait_ge(s["weights"], 32)
                with pe.Fori(0, 4) as n:
                    for q in range(4):
                        e = 4 * n + q
                        pe.wait_ge(s["xn"], ready(e))
                        pe.wait_ge(s["xt"], free(e, 2))
                        for k in range(KH):
                            ins = nc.tensor.transpose(psT[q % 2][:, k * P:(k + 1) * P], xn[q][:, k * P:(k + 1) * P],
                                                      core.ident[:, :])
                        ins.then_inc(s["turned"], 1)
                        pe.wait_ge(s["xt"], ready(e))
                        pe.wait_ge(s["new"], free(e, 2))
                        for k in range(KH):
                            ins = nc.tensor.matmul(psS[q % 2][:, 0:H], xt[q % 2][:, k, :], w[:, k, :],
                                                   start=k == 0, stop=k == KH - 1)
                        ins.then_inc(s["ps"], 1)

            @block.gpsimd
            def _(pool):
                open_sems(pool, s["old"])
                pool.wait_ge(s["gates"], 1)
                with pool.Fori(0, 4) as n:
                    for q in range(4):
                        e = 4 * n + q
                        pool.wait_ge(s["xn"], ready(4 * n + (q | 1)))
                        pool.wait_ge(s["mixed"], free(e, 2))
                        nc.gpsimd.tensor_tensor(old[q % 2][:, :], xn[q ^ 1][:, :], g_old[:, :],
                                                ALU.mult).then_inc(s["old"], 1)

            @block.vector
            def _(dve):
                open_sems(dve, s["xn"], s["new"], s["mixed"])
                dve.wait_ge(s["gate"], 1)
                nc.vector.tensor_scalar(g_old[:, :], g_new[:, :], -1.0, 1.0, ALU.mult, ALU.add).then_inc(s["gates"], 1)
                with dve.Fori(0, 4) as n:
                    for q in range(4):
                        e = 4 * n + q
                        t = 4 * q + n
                        dve.wait_ge(s["turned"], free(e, 4))
                        dve.wait_ge(s["old"], ready(4 * n - 4 + (q ^ 1)))
                        nc.vector.tensor_scalar(xn[q][:, :], at(x, t), col(core.rstd, t), col(core.nmr, t),
                                                ALU.mult, ALU.add).then_inc(s["xn"], 1)
                    for q in range(4):
                        e = 4 * n + q
                        dve.wait_ge(s["ps"], ready(e))
                        dve.wait_ge(s["mixed"], free(e, 2))
                        nc.vector.tensor_tensor(new[q % 2][:, :], psS[q % 2][:, 0:H], g_new[:, :],
                                                ALU.mult).then_inc(s["new"], 1)
                        dve.wait_ge(s["new"], ready(e))
                        dve.wait_ge(s["old"], ready(e))
                        nc.vector.tensor_tensor(at(shifted, 4 * (q ^ 1) + n), new[q % 2][:, :], old[q % 2][:, :],
                                                ALU.add).then_inc(s["mixed"], 1)


def layer1_scan(core, gamma, beta, kv, time_decay, time_first, shifted, states):
    nc = core.nc
    with ExitStack() as ctx:
        sb, ps = scratch(nc, ctx)
        w = sb("a1_wkv", [P, KH, 2 * NS])
        gam, bet = sb("a1_gamma", [P, H]), sb("a1_beta", [P, H])
        dec, first = sb("a1_dec", [P, 1]), sb("a1_first", [P, 1])
        decays = sb("a1_decays", [P, S])
        sig, gain = sb("a1_sig", [P, CH]), sb("a1_gain", [P, CH])
        wkv = sb("a1_wkvs", [P, S])
        psT = [ps(f"a1_kT{q}", [P, CH]) for q in range(2)]
        psK, psV = ps("a1_pK", [P, CH]), ps("a1_pV", [P, CH])
        s = core.sems("a1k", "weights exps ready scaled gained pk sig gain wkv scan")
        front = Front(core, "a1k", sb, psT, shifted, lambda act, c: act.wait_ge(s["pk"], ready(c - 2)))

        with nc.Block() as block:
            @block.sync
            def _(sp):
                for dst, src in ((w[:, :, :], kv), (gam[:, :], gamma), (bet[:, :], beta), (dec[:, :], time_decay),
                                 (first[:, :], time_first)):
                    sp.dma_start(dst, src).then_inc(s["weights"], 16)

            @block.scalar
            def _(act):
                front.open(act, "xt")
                open_sems(act, s["sig"], s["gain"])
                act.wait_ge(s["weights"], 80)
                nc.scalar.activation(dec[:, :], dec[:, :], ACT.Exp).then_inc(s["exps"], 1)
                nc.scalar.activation(first[:, :], first[:, :], ACT.Exp).then_inc(s["exps"], 1)
                act.wait_ge(s["ready"], 2)
                with act.Fori(0, 2) as cc:
                    for b in range(B):
                        front.scalar(act, 2 * cc + b, b)
                    act.wait_ge(s["pk"], ready(2 * cc + 1))
                    nc.scalar.activation(sig[:, :], psK[:, :], ACT.Sigmoid).then_inc(s["sig"], 1)
                    act.wait_ge(s["sig"], ready(cc))
                    act.wait_ge(s["wkv"], free(cc, 1))
                    nc.scalar.activation(gain[:, :], sig[:, :], ACT.Exp, scale=first[:, 0:1]).then_inc(s["gain"], 1)

            @block.tensor
            def _(pe):
                front.open(pe, "turned")
                open_sems(pe, s["pk"])
                pe.wait_ge(s["weights"], 80)
                with pe.Fori(0, 2) as cc:
                    for b in range(B):
                        c = 2 * cc + b
                        front.tensor(pe, c)
                        pe.wait_ge(front.s["xt"], ready(SUB * c + SUB - 1))
                        if b == 0:
                            pe.wait_ge(s["wkv"], free(cc, 1))
                        for i, dst in ((0, psK), (1, psV)):
                            for k in range(KH):
                                ins = nc.tensor.matmul(dst[NS * b:NS * (b + 1), :], w[:, k, NS * i:NS * (i + 1)],
                                                       front.xt[b][:, k, :], start=k == 0, stop=k == KH - 1)
                        ins.then_inc(s["pk"], 1)

            @block.gpsimd
            def _(pool):
                front.open(pool, "xn")
                open_sems(pool, s["gained"])
                pool.wait_ge(s["weights"], 80)
                with pool.Fori(0, 2) as cc:
                    for q in range(B * SUB):
                        t = B * SUB * cc + q
                        pool.wait_ge(s["scaled"], ready(t))
                        nc.gpsimd.tensor_tensor(front.xn[q % 4][:, :], front.xn[q % 4][:, :], gam[:, :],
                                                ALU.mult).then_inc(s["gained"], 1)
                        pool.wait_ge(s["gained"], ready(t))
                        nc.gpsimd.tensor_tensor(front.xn[q % 4][:, :], front.xn[q % 4][:, :], bet[:, :],
                                                ALU.add).then_inc(front.s["xn"], 1)

            @block.vector
            def _(dve):
                open_sems(dve, s["scaled"], s["wkv"])
                nc.vector.memset(decays[:, :], 1.0).then_inc(s["scan"], 1)
                dve.wait_ge(s["exps"], 2)
                dve.wait_ge(s["scan"], 1)
                nc.vector.tensor_scalar(decays[:, :], decays[:, :], dec[:, 0:1], None, ALU.mult).then_inc(s["ready"], 1)
                nc.vector.tensor_scalar(first[:, :], first[:, :], -1.0, None, ALU.mult).then_inc(s["ready"], 1)
                with dve.Fori(0, 2) as cc:
                    for b in range(B):
                        front.vector(dve, 2 * cc + b, 2 * b + cc, s["scaled"])
                    dve.wait_ge(s["gain"], ready(cc))
                    nc.vector.tensor_tensor(wkv[:, bass.ds(CH * cc, CH)], psV[:, :], gain[:, :],
                                            ALU.mult).then_inc(s["wkv"], 1)
                dve.wait_ge(s["wkv"], ready(1))
                dve.wait_ge(s["ready"], 2)
                nc.vector.tensor_tensor_scan(states[:, :], decays[:, :], wkv[:, :], 0.0, ALU.mult,
                                             ALU.add).then_inc(s["scan"], 1)


def layer1_out(core, w_out, states):
    nc, x = core.nc, core.x
    with ExitStack() as ctx:
        sb, ps = scratch(nc, ctx)
        w = sb("a1_wo", [P, H])
        psO = [ps(f"a1_pO{q}", [P, CH]) for q in range(4)]
        s = core.sems("a1o", "weights po added")

        with nc.Block() as block:
            @block.sync
            def _(sp):
                sp.dma_start(w[:, :], w_out).then_inc(s["weights"], 16)

            @block.tensor
            def _(pe):
                open_sems(pe, s["po"])
                pe.wait_ge(s["weights"], 16)
                for t in range(NT):
                    b, j = divmod(t, KT)
                    pe.wait_ge(s["added"], free(t, 4))
                    nc.tensor.matmul(psO[t % 4][:, 0:H], states[NS * b:NS * (b + 1), j * P:(j + 1) * P],
                                     w[NS * b:NS * (b + 1), :], start=True, stop=True).then_inc(s["po"], 1)

            @block.vector
            def _(dve):
                open_sems(dve, s["added"])
                with dve.Fori(0, NT // 4) as m:
                    for r in range(4):
                        t = 4 * m + r
                        dve.wait_ge(s["po"], ready(t))
                        nc.vector.tensor_tensor(at(x, t), at(x, t), psO[r][:, 0:H], ALU.add).then_inc(s["added"], 1)



SPLITS = {"q": ((0, 3, 0, False), (3, 2, 0, False), (5, 1, 0, False)),
          "k": ((0, 3, 0, True), (3, 2, 1, True), (5, 1, 2, True))}


def softmax_attention(core, name, w_qkv, w_out, rope):
    with ExitStack() as ctx:
        sb, _ = scratch(core.nc, ctx)
        v = sb(f"{name}_v", [P, BH, KT, VD])
        norm_stats(core, name + "n", core.x)
        attention_project(core, name, w_qkv, rope, v)
        mixed = sb(f"{name}_mixed", [P, BH // 4, KT * 4 * D])
        attention_heads(core, name, v, mixed)
        attention_out(core, name, w_out, mixed)


def attention_project(core, name, w_qkv, rope, v):
    nc, x = core.nc, core.x
    stage = name + "p"
    with ExitStack() as ctx:
        sb, ps = scratch(nc, ctx)
        w = sb(f"{stage}_w", [P, KH, 5 if rope else 3, H])
        parts = [sb(f"{stage}_parts{i}", [P, 3, CH], BF16) for i in range(2)]
        rest = [sb(f"{stage}_rest{i}", [P, CH]) for i in range(2)]
        psT = [ps(f"{stage}_pT{i}", [P, CH]) for i in range(2)]
        psV = [ps(f"{stage}_pV{i}", [P, CH]) for i in range(2)]
        psJ = [ps(f"{stage}_pJ{i}", [P, CH]) for i in range(2)]
        if rope:
            psW = [ps(f"{stage}_pW{i}", [P, CH]) for i in range(2)]
            cos, sin = sb(f"{stage}_cos", [P, S]), sb(f"{stage}_sin", [P, S])
            turn_a = [sb(f"{stage}_ta{i}", [P, CH]) for i in range(2)]
            turn_b = [sb(f"{stage}_tb{i}", [P, CH]) for i in range(2)]
        s = core.sems(stage, "weights ones pj turns roped first rest second third written flushed pv v")
        front = Front(core, stage, sb, psT, x, lambda act, c: act.wait_ge(s["pv"], ready(SUB * (c - 2) + SUB - 1)))
        n_weights = 48 if rope else 16
        UNITS = (("q", 0), ("q", 1), ("k", 0), ("k", 1))

        with nc.Block() as block:
            @block.sync
            def _(sp):
                sp.dma_start(w[:, :, :, :], w_qkv).then_inc(s["weights"], 16)
                if rope:
                    sp.dma_start(cos[:, :], rope[0]).then_inc(s["weights"], 16)
                    sp.dma_start(sin[:, :], rope[1]).then_inc(s["weights"], 16)
                open_sems(sp, s["flushed"])
                with sp.Fori(0, B) as b:
                    for cc in range(2):
                        for u, (which, half) in enumerate(UNITS):
                            e = 4 * (2 * b + cc) + u
                            sp.wait_ge(s["third"], ready(e))
                            dram = core.stack[which]
                            for seg, count, part, same in SPLITS[which]:
                                src = parts[u % 2][:, part:part + (1 if same else count), :]
                                if same and count > 1:
                                    src = src.broadcast_to([P, count, CH])
                                dst = dram[bass.ds(b * H + half * P, P), seg:seg + count, cc * CH:(cc + 1) * CH]
                                sp.dma_start(dst, src).then_inc(s["written"], 16)
                            sp.wait_ge(s["written"], 48 * e + 48)
                            sp.sem_inc(s["flushed"], 1)

            @block.tensor
            def _(pe):
                front.open(pe, "turned")
                open_sems(pe, s["pj"], s["pv"])
                pe.wait_ge(s["weights"], n_weights)
                with pe.Fori(0, B) as b:
                    for cc in range(2):
                        c = 2 * b + cc
                        front.tensor(pe, c)
                        pe.wait_ge(front.s["xt"], ready(SUB * c + SUB - 1))
                        for u, (which, half) in enumerate(UNITS):
                            e = 4 * c + u
                            pe.wait_ge(s["turns" if rope else "rest"], free(e, 2))
                            i = "qk".index(which)
                            for dst, j in ((psJ[u % 2], i), (psW[u % 2] if rope else None, 3 + i)):
                                if dst is not None:
                                    for k in range(KH):
                                        ins = nc.tensor.matmul(dst[:, :], w[:, k, j, half * P:(half + 1) * P],
                                                               front.xt[cc][:, k, :], start=k == 0, stop=k == KH - 1)
                            ins.then_inc(s["pj"], 1)
                        for sub in range(SUB):
                            t = SUB * c + sub
                            pe.wait_ge(s["v"], free(t, 2))
                            for k in range(KH):
                                ins = nc.tensor.matmul(psV[sub % 2][:, 0:H], front.xt[cc][:, k, sub * P:(sub + 1) * P],
                                                       w[:, k, 2, :], start=k == 0, stop=k == KH - 1)
                            ins.then_inc(s["pv"], 1)

            @block.scalar
            def _(act):
                front.open(act, "xt")
                open_sems(act, s["first"], s["second"])
                with act.Fori(0, B) as b:
                    for cc in range(2):
                        c = 2 * b + cc
                        front.scalar(act, c, cc)
                        for u in range(4):
                            e = 4 * c + u
                            value = turn_a[u % 2][:, :] if rope else psJ[u % 2][:, :]
                            act.wait_ge(s["roped" if rope else "pj"], ready(e))
                            act.wait_ge(s["flushed"], free(e, 2))
                            nc.scalar.activation(parts[u % 2][:, 0, :], value, ACT.Copy).then_inc(s["first"], 1)
                            act.wait_ge(s["rest"], ready(e))
                            nc.scalar.activation(parts[u % 2][:, 1, :], rest[u % 2][:, :],
                                                 ACT.Copy).then_inc(s["second"], 1)

            @block.gpsimd
            def _(pool):
                open_sems(pool, s["third"], s["roped"])
                with pool.Fori(0, B) as b:
                    for cc in range(2):
                        for u in range(4):
                            e = 4 * (2 * b + cc) + u
                            if rope:
                                pool.wait_ge(s["turns"], ready(e))
                                nc.gpsimd.tensor_tensor(turn_a[u % 2][:, :], turn_a[u % 2][:, :], turn_b[u % 2][:, :],
                                                        ALU.add).then_inc(s["roped"], 1)
                            pool.wait_ge(s["second"], ready(e))
                            nc.gpsimd.tensor_tensor(parts[u % 2][:, 2, :], rest[u % 2][:, :], parts[u % 2][:, 1, :],
                                                    ALU.subtract).then_inc(s["third"], 1)

            @block.vector
            def _(dve):
                front.open(dve, "xn")
                open_sems(dve, s["rest"], s["turns"], s["v"])
                nc.vector.memset(v[:, :, :, D:VD], 1.0).then_inc(s["ones"], 1)
                dve.wait_ge(s["weights"], n_weights)
                with dve.Fori(0, B) as b:
                    for cc in range(2):
                        c = 2 * b + cc
                        front.vector(dve, c)
                        for u in range(4):
                            e = 4 * c + u
                            value = psJ[u % 2][:, :]
                            if rope:
                                dve.wait_ge(s["pj"], ready(e))
                                dve.wait_ge(s["rest"], free(e, 2))
                                pos = slice(cc * CH, (cc + 1) * CH)
                                nc.vector.tensor_tensor(turn_b[u % 2][:, :], psW[u % 2][:, :], sin[:, pos], ALU.mult)
                                nc.vector.tensor_tensor(turn_a[u % 2][:, :], psJ[u % 2][:, :], cos[:, pos],
                                                        ALU.mult).then_inc(s["turns"], 1)
                                value = turn_a[u % 2][:, :]
                            dve.wait_ge(s["first"], ready(e))
                            dve.wait_ge(s["third"], free(e, 2))
                            nc.vector.tensor_tensor(rest[u % 2][:, :], value, parts[u % 2][:, 0, :],
                                                    ALU.subtract).then_inc(s["rest"], 1)
                        for sub in range(SUB):
                            t = SUB * c + sub
                            dve.wait_ge(s["pv"], ready(t))
                            heads = v[:, bass.ds(b * HEADS, HEADS), cc * SUB + sub, 0:D]
                            nc.vector.tensor_copy(heads, psV[sub % 2][:, 0:H].rearrange("p (h d) -> p h d", d=D)
                                                  ).then_inc(s["v"], 1)


def attention_heads(core, name, v, mixed):
    nc = core.nc
    stage = name + "h"
    GROUPS = BH // 4
    HALF = CH // P
    PIECES = [(0, 0), (0, 1), (0, 2), (0, 3), (1, 0), (1, 5), (1, 6), (1, 7), (1, 4), (1, 1), (1, 2), (1, 3)]
    NP = len(PIECES)
    last_of = [HALF - 1, NP - 1]
    TURNS = list(range(10)) + ["maximum 0", "maximum 1"] + [10, 11]
    NU = len(TURNS)
    PROBS = 6
    MAXIMA = list(range(KT))[::-1]
    MAXIMA_AT = {0: (0, 1), 1: (2,), 2: (3,), 3: (4,), 4: (5, 6), 5: (7,)}
    OUTPUTS_AT = 8
    with ExitStack() as ctx:
        sb, ps = scratch(nc, ctx)
        R3 = ROWS + 3
        q_rows = [sb(f"{stage}_q{i}", [R3, S], BF16) for i in range(4)]
        k_rows = [sb(f"{stage}_k{i}", [R3, S], BF16) for i in range(4)]
        neg = sb(f"{stage}_neg", [P, KT])
        left = sb(f"{stage}_left", [P, KT])
        neg3 = [sb(f"{stage}_neg3{i}", [P, KT, 3], BF16) for i in range(2)]
        probs = [sb(f"{stage}_probs{i}", [P, CH]) for i in range(PROBS)]
        values = [sb(f"{stage}_values{i}", [P, KT, VD]) for i in range(4)]
        turned = sb(f"{stage}_turned", [P, S])
        rden = sb(f"{stage}_rden", [P, HALF, 4])
        psM = [ps(f"{stage}_pM{i}", [P, S]) for i in range(2)]
        psX = [ps(f"{stage}_pX{i}", [P, CH]) for i in range(2)]
        psV = [ps(f"{stage}_pV{i}", [P, CH]) for i in range(2)]
        s = core.sems(stage, "ones clear pm max split neg3 px ex values pv copied rden")
        loaded = [core.sem(f"{stage}_loaded{i}") for i in range(4)]

        def groups(eng, body):
            body(0)
            with eng.Fori(1, GROUPS - 1) as g:
                body(g)
            body(GROUPS - 1)

        def final(t):
            return isinstance(t, int) and t == BH - 1

        def turns(t):
            return [j for j in range(NU) if not (final(t) and isinstance(TURNS[j], str))]

        def bank_use(t, j):
            n = 2 + NU * t + j
            return n - 2 if final(t) and j > TURNS.index("maximum 1") else n

        def rows_use(g, r, i):
            if isinstance(g, int) and g == r == 0:
                return i
            return bank_use(4 * g + r - 1, TURNS.index("maximum 0") + i)

        def maximum_use(g, r, p):
            return KT + (34 * g + KT * r + p) - (2 if r == 0 and not (isinstance(g, int) and g == 0) else 0)

        def output_use(g, c):
            if isinstance(g, int) and g == GROUPS - 1:
                return KT + 34 * g + 3 * KT + c
            return KT + 34 * (g + 1) + KT - 2 + c

        with nc.Block() as block:
            @block.sync
            def _(sp):
                def fetch(t, r):
                    for which, dst in (("q", q_rows[r]), ("k", k_rows[r])):
                        sp.dma_start(dst[0:ROWS, :], core.stack_rows[which][bass.ds(t * ROWS, ROWS), :]
                                     ).then_inc(loaded[r], 16)
                for r in range(4):
                    fetch(r, r)
                with sp.Fori(1, GROUPS) as g:
                    for r in range(4):
                        sp.wait_ge(s["pv"], ready(NP * (4 * g + r - 4) + NP - 1))
                        fetch(4 * g + r, r)

            @block.gpsimd
            def _(pool):
                open_sems(pool, s["values"])

                def take(g):
                    for r in range(4):
                        t = 4 * g + r
                        if not (isinstance(g, int) and g == 0):
                            pool.wait_ge(s["pv"], ready(NP * (t - 4) + NP - 1))
                            settle(pool)
                        nc.gpsimd.tensor_copy(flat(values[r][:, :, :]), v[:, bass.ds(t, 1), :, :].rearrange(
                            "p a k d -> p (a k d)")).then_inc(s["values"], 1)
                groups(pool, take)

            @block.tensor
            def _(pe):
                open_sems(pe, s["pm"], s["px"], s["pv"])
                pe.wait_ge(s["ones"], 4)

                def maximum(g, slot, use, p):
                    u = MAXIMA[p]
                    if p == 0:
                        pe.wait_ge(loaded[slot], 32 * (g + 1))
                    pe.wait_ge(s["max"], free(use, 2))
                    n = (u + 1) * P
                    for a in range(0, n, CH):
                        b = min(a + CH, n)
                        nc.tensor.matmul(psM[p % 2][:, a:b], q_rows[slot][0:ROWS, u * P:(u + 1) * P],
                                         k_rows[slot][0:ROWS, a:b], start=True, stop=b < n)
                    nc.tensor.matmul(psM[p % 2][:, u * P:n], core.identb[:, :], core.mask_q[:, :],
                                     start=False, stop=True).then_inc(s["pm"], 1)

                def maximum_rows(g, r, i):
                    use = rows_use(g, r, i)
                    if i == 0:
                        pe.wait_ge(s["neg3"], ready(4 * g + r))
                    pe.wait_ge(s["ex"], free(use, 2))
                    for j in range(HALF):
                        ins = nc.tensor.matmul(psX[i][ROWS:R3, j * P:(j + 1) * P], neg3[r % 2][:, i * HALF + j, :],
                                               core.identb[:, :], start=True, stop=True)
                    ins.then_inc(s["px"], 1)

                def scores(t, slot, j):
                    c, kt = PIECES[TURNS[j]]
                    off = max(0, kt * P - c * CH)
                    pe.wait_ge(s["ex"], free(bank_use(t, j), 2))
                    diag = kt * P >= c * CH
                    ins = nc.tensor.matmul(psX[j % 2][:, off:CH], k_rows[slot][0:R3, kt * P:(kt + 1) * P],
                                           q_rows[slot][0:R3, c * CH + off:(c + 1) * CH], start=True, stop=not diag)
                    if diag:
                        ins = nc.tensor.matmul(psX[j % 2][:, off:off + P], core.identb[:, :], core.mask_k[:, :],
                                               start=False, stop=True)
                    ins.then_inc(s["px"], 1)

                def weighted(g, r, j):
                    t, i = 4 * g + r, TURNS[j]
                    c, kt = PIECES[i]
                    off = max(0, kt * P - c * CH)
                    if i == 0:
                        pe.wait_ge(s["values"], ready(t))
                    if r == 0 and kt == 0:
                        if isinstance(g, int) and g == 0:
                            pe.wait_ge(s["clear"], 2)
                        else:
                            pe.wait_ge(s["copied"], ready(2 * (g - 1) + c))
                    pe.wait_ge(s["ex"], ready(bank_use(t, j)))
                    nc.tensor.matmul(psV[c][32 * r:32 * r + VD, off:CH], values[r][:, kt, :],
                                     probs[i % PROBS][:, off:CH], start=kt == 0, stop=i == last_of[c]).then_inc(s["pv"], 1)

                def outputs(g):
                    for c in range(2):
                        pe.wait_ge(s["copied"], ready(2 * g + c))
                        pe.wait_ge(s["max"], free(output_use(g, c), 2))
                        for j in range(HALF):
                            ins = nc.tensor.transpose(psM[c][:, j * P:(j + 1) * P],
                                                      turned[:, (c * HALF + j) * P:(c * HALF + j + 1) * P], core.ident[:, :])
                        ins.then_inc(s["pm"], 1)

                def head(g, r):
                    t = 4 * g + r
                    order = turns(t)
                    for n, j in enumerate(order):
                        if n + 2 < len(order):
                            ahead = order[n + 2]
                            if isinstance(TURNS[ahead], int):
                                scores(t, r, ahead)
                            else:
                                maximum_rows(g if r < 3 else g + 1, (r + 1) % 4, ahead - TURNS.index("maximum 0"))
                        elif not final(t):
                            scores(t + 1, (r + 1) % 4, n + 2 - NU)
                        if not final(t):
                            for p in MAXIMA_AT.get(n, ()):
                                maximum(g if r < 3 else g + 1, (r + 1) % 4, maximum_use(g, r, p), p)
                        if isinstance(TURNS[j], int):
                            weighted(g, r, j)
                        if n == OUTPUTS_AT and r == 0 and not (isinstance(g, int) and g == 0):
                            outputs(g - 1)

                for p in range(KT):
                    maximum(0, 0, p, p)
                for i in range(2):
                    maximum_rows(0, 0, i)
                pe.wait_ge(s["ex"], ready(1))
                scores(0, 0, 0)
                scores(0, 0, 1)

                def body(g):
                    for r in range(4):
                        head(g, r)
                groups(pe, body)
                outputs(GROUPS - 1)

            @block.scalar
            def _(act):
                open_sems(act, s["ex"], s["copied"])
                nc.scalar.preload_act_table(ACT.Exp)

                def rows(g, r, i):
                    act.wait_ge(s["px"], ready(rows_use(g, r, i)))
                    nc.scalar.activation(q_rows[r][ROWS:R3, i * CH:(i + 1) * CH], psX[i % 2][ROWS:R3, :],
                                         ACT.Copy).then_inc(s["ex"], 1)

                def copy(g, c):
                    act.wait_ge(s["pv"], ready(NP * (4 * g + 3) + last_of[c]))
                    if not (isinstance(g, int) and g == 0):
                        act.wait_ge(s["max"], ready(output_use(g - 1, c)))
                    nc.scalar.activation(turned[:, c * CH:(c + 1) * CH], psV[c][:, :], ACT.Copy).then_inc(s["copied"], 1)

                def body(g):
                    for r in range(4):
                        t = 4 * g + r
                        for j in turns(t):
                            if isinstance(TURNS[j], str):
                                rows(g if r < 3 else g + 1, (r + 1) % 4, j - TURNS.index("maximum 0"))
                                continue
                            i = TURNS[j]
                            c, kt = PIECES[i]
                            off = max(0, kt * P - c * CH)
                            act.wait_ge(s["px"], ready(bank_use(t, j)))
                            act.wait_ge(s["pv"], free(NP * t + i, PROBS))
                            nc.scalar.activation(probs[i % PROBS][:, off:CH], psX[j % 2][:, off:CH], ACT.Exp,
                                                 scale=float(D) ** -0.5).then_inc(s["ex"], 1)
                            if r == 3 and i == HALF + 2:
                                copy(g, 0)
                            if r == 0 and i == 1 and not (isinstance(g, int) and g == 0):
                                copy(g - 1, 1)
                for i in range(2):
                    rows(0, 0, i)
                groups(act, body)
                copy(GROUPS - 1, 1)

            @block.vector
            def _(dve):
                open_sems(dve, *(s[n] for n in ("max", "split", "neg3", "rden")))
                for i in range(4):
                    nc.vector.memset(k_rows[i][ROWS:R3, :], 1.0).then_inc(s["ones"], 1)
                for c in range(2):
                    nc.vector.memset(psV[c][:, :], 0.0).then_inc(s["clear"], 1)

                def maxima(t, use, r):
                    for p, u in enumerate(MAXIMA):
                        dve.wait_ge(s["pm"], ready(use(p)))
                        nc.vector.tensor_reduce(neg[:, u:u + 1], psM[p % 2][:, 0:(u + 1) * P], AX.X, ALU.max,
                                                negate=True).then_inc(s["max"], 1)
                    dve.wait_ge(s["max"], ready(use(KT - 1)))
                    parts = neg3[r % 2]
                    nc.vector.tensor_copy(parts[:, :, 0], neg[:, :]).then_inc(s["split"], 1)
                    dve.wait_ge(s["split"], ready(3 * t))
                    nc.vector.tensor_tensor(left[:, :], neg[:, :], parts[:, :, 0], ALU.subtract).then_inc(s["split"], 1)
                    dve.wait_ge(s["split"], ready(3 * t + 1))
                    nc.vector.tensor_copy(parts[:, :, 1], left[:, :]).then_inc(s["split"], 1)
                    dve.wait_ge(s["split"], ready(3 * t + 2))
                    nc.vector.tensor_tensor(parts[:, :, 2], left[:, :], parts[:, :, 1],
                                            ALU.subtract).then_inc(s["neg3"], 1)
                    dve.wait_ge(s["neg3"], ready(t))

                def divide(g):
                    for c in range(2):
                        dve.wait_ge(s["pm"], ready(output_use(g, c)))
                        if c:
                            dve.wait_ge(s["max"], ready(output_use(g, 0)))
                        elif not (isinstance(g, int) and g == 0):
                            dve.wait_ge(s["max"], ready(output_use(g - 1, 1)))
                        out = psM[c][:, 0:CH].rearrange("p (q r w) -> p q r w", q=HALF, r=4)
                        nc.vector.reciprocal(rden[:, :, :], out[:, :, :, D]).then_inc(s["rden"], 1)
                        dve.wait_ge(s["rden"], ready(2 * g + c))
                        dst = at(mixed, g)[:, c * HALF * 4 * D:(c + 1) * HALF * 4 * D].rearrange(
                            "p (q r d) -> p q r d", q=HALF, r=4)
                        nc.vector.tensor_tensor(dst, out[:, :, :, 0:D],
                                                rden[:, :, :].unsqueeze(3).broadcast_to([P, HALF, 4, D]),
                                                ALU.mult).then_inc(s["max"], 1)

                def body(g):
                    for r in range(4):
                        if not final(4 * g + r):
                            maxima(4 * g + r + 1, lambda p: maximum_use(g, r, p), (r + 1) % 4)
                        if r == 0 and not (isinstance(g, int) and g == 0):
                            divide(g - 1)
                maxima(0, lambda p: p, 0)
                groups(dve, body)
                divide(GROUPS - 1)


def attention_out(core, name, w_out, mixed):
    nc, x = core.nc, core.x
    stage = name + "o"
    with ExitStack() as ctx:
        sb, ps = scratch(nc, ctx)
        w = sb(f"{stage}_w", [P, KH, H])
        row = [sb(f"{stage}_row{i}", [P, H]) for i in range(4)]
        xt = [sb(f"{stage}_xt{i}", [P, KH, P]) for i in range(2)]
        psT = [ps(f"{stage}_pT{i}", [P, CH]) for i in range(2)]
        psO = [ps(f"{stage}_pO{i}", [P, CH]) for i in range(2)]
        s = core.sems(stage, "weights row turned xt po added")
        groups = HEADS // 4

        with nc.Block() as block:
            @block.sync
            def _(sp):
                sp.dma_start(w[:, :, :], w_out).then_inc(s["weights"], 16)

            @block.gpsimd
            def _(pool):
                open_sems(pool, s["row"])
                with pool.Fori(0, B) as b:
                    for q in range(KT):
                        pool.wait_ge(s["turned"], free(KT * b + q, 4))
                        settle(pool)
                        src = mixed[:, bass.ds(b * groups, groups), q * 4 * D:(q + 1) * 4 * D]
                        nc.gpsimd.tensor_copy(row[q % 4][:, :].rearrange("p (g c) -> p g c", g=groups),
                                              src).then_inc(s["row"], 1)

            @block.tensor
            def _(pe):
                open_sems(pe, s["turned"], s["po"])
                pe.wait_ge(s["weights"], 16)

                def product(t, q):
                    pe.wait_ge(s["xt"], ready(t))
                    pe.wait_ge(s["added"], free(t, 2))
                    for k in range(KH):
                        ins = nc.tensor.matmul(psO[q % 2][:, 0:H], xt[q % 2][:, k, :], w[:, k, :],
                                               start=k == 0, stop=k == KH - 1)
                    ins.then_inc(s["po"], 1)
                with pe.Fori(0, B) as b:
                    for q in range(KT):
                        t = KT * b + q
                        pe.wait_ge(s["row"], ready(t))
                        pe.wait_ge(s["xt"], free(t, 2))
                        for k in range(KH):
                            ins = nc.tensor.transpose(psT[q % 2][:, k * P:(k + 1) * P], row[q % 4][:, k * P:(k + 1) * P],
                                                      core.ident[:, :])
                        ins.then_inc(s["turned"], 1)
                        if q:
                            product(t - 1, q - 1)
                    product(KT * b + KT - 1, KT - 1)

            @block.scalar
            def _(act):
                open_sems(act, s["xt"])
                with act.Fori(0, B) as b:
                    for q in range(KT):
                        t = KT * b + q
                        act.wait_ge(s["turned"], ready(t))
                        act.wait_ge(s["po"], free(t, 2))
                        nc.scalar.activation(flat(xt[q % 2][:, :, :]), psT[q % 2][:, 0:H], ACT.Copy).then_inc(s["xt"], 1)

            @block.vector
            def _(dve):
                open_sems(dve, s["added"])
                with dve.Fori(0, B) as b:
                    for q in range(KT):
                        t = KT * b + q
                        dve.wait_ge(s["po"], ready(t))
                        nc.vector.tensor_tensor(at(x, t), at(x, t), psO[q % 2][:, 0:H], ALU.add).then_inc(s["added"], 1)



def last_ffn(core, w_gu, w_down, w_down_last, scales, down_scale):
    nc, x = core.nc, core.x
    norm_stats(core, "fn", x)
    with ExitStack() as ctx:
        sb, ps = scratch(nc, ctx)
        NI = -(-FI // P)
        width = [min(P, FI - i * P) for i in range(NI)]
        w = sb("f_wgu", [P, KH, 2 * FI])
        wd = sb("f_wd", [P, NI, H])
        sc = {n: sb(f"f_{n}", [P, NI]) for n in ("gs", "us")}
        ds = sb("f_ds", [P, H])
        act_g = [sb(f"f_act{i}", [P, CH]) for i in range(2)]
        hid = sb("f_hid", [P, NI, CH])
        res = [sb(f"f_res{i}", [P, H]) for i in range(2)]
        psT = [ps(f"f_pT{i}", [P, CH]) for i in range(2)]
        psG = [ps(f"f_pG{i}", [P, CH]) for i in range(2)]
        psU = [ps(f"f_pU{i}", [P, CH]) for i in range(2)]
        psO = [ps(f"f_pO{i}", [P, CH]) for i in range(2)]
        s = core.sems("f", "weights pu act hid po res added")
        front = Front(core, "f", sb, psT, x, lambda act, c: act.wait_ge(s["pu"], ready(NI * (c - 1) - 1)))

        with nc.Block() as block:
            @block.sync
            def _(sp):
                last = width[-1]
                loads = [(w[:, :, :], w_gu), (wd[:, 0:NI - 1, :], w_down), (wd[0:last, NI - 1, :], w_down_last),
                         (ds[:, :], down_scale)]
                for n in ("gs", "us"):
                    loads += [(sc[n][:, 0:NI - 1], scales[n][0]), (sc[n][0:last, NI - 1:NI], scales[n][1])]
                for dst, src in loads:
                    sp.dma_start(dst, src).then_inc(s["weights"], 16)

            @block.tensor
            def _(pe):
                front.open(pe, "turned")
                open_sems(pe, s["pu"], s["po"])
                pe.wait_ge(s["weights"], 8 * 16)
                with pe.Fori(0, NC // 2) as b:
                    for cc in range(2):
                        c = 2 * b + cc
                        front.tensor(pe, c)
                        pe.wait_ge(front.s["xt"], ready(SUB * c + SUB - 1))
                        for i in range(NI):
                            pe.wait_ge(s["hid"], free(NI * c + i, 2))
                            for dst, base in ((psG[i % 2], 0), (psU[i % 2], FI)):
                                for k in range(KH):
                                    ins = nc.tensor.matmul(dst[0:width[i], :],
                                                           w[:, k, base + i * P:base + i * P + width[i]],
                                                           front.xt[cc][:, k, :], start=k == 0, stop=k == KH - 1)
                            ins.then_inc(s["pu"], 1)
                        pe.wait_ge(s["hid"], ready(NI * c + NI - 1))
                        for sub in range(SUB):
                            pe.wait_ge(s["res"], free(SUB * c + sub, 2))
                            for i in range(NI):
                                ins = nc.tensor.matmul(psO[sub % 2][:, 0:H], hid[0:width[i], i, sub * P:(sub + 1) * P],
                                                       wd[0:width[i], i, :], start=i == 0, stop=i == NI - 1)
                            ins.then_inc(s["po"], 1)

            @block.scalar
            def _(act):
                front.open(act, "xt")
                open_sems(act, s["act"])
                nc.scalar.preload_act_table(ACT.Silu)
                act.wait_ge(s["weights"], 8 * 16)
                with act.Fori(0, NC // 2) as b:
                    for cc in range(2):
                        c = 2 * b + cc
                        front.scalar(act, c, cc)
                        for i in range(NI):
                            act.wait_ge(s["pu"], ready(NI * c + i))
                            act.wait_ge(s["hid"], free(NI * c + i, 2))
                            nc.scalar.activation(act_g[i % 2][0:width[i], :], psG[i % 2][0:width[i], :], ACT.Silu,
                                                 scale=sc["gs"][0:width[i], i:i + 1]).then_inc(s["act"], 1)

            @block.vector
            def _(dve):
                front.open(dve, "xn")
                open_sems(dve, s["hid"], s["res"], s["added"])
                dve.wait_ge(s["weights"], 8 * 16)
                with dve.Fori(0, NC // 2) as b:
                    for cc in range(2):
                        c = 2 * b + cc
                        front.vector(dve, c)
                        dve.wait_ge(s["po"], ready(SUB * (c - 1) + SUB - 1))
                        for i in range(NI):
                            dve.wait_ge(s["act"], ready(NI * c + i))
                            nc.vector.scalar_tensor_tensor(hid[0:width[i], i, :], psU[i % 2][0:width[i], :],
                                                           sc["us"][0:width[i], i:i + 1], act_g[i % 2][0:width[i], :],
                                                           ALU.mult, ALU.mult).then_inc(s["hid"], 1)
                        for sub in range(SUB):
                            t = SUB * c + sub
                            dve.wait_ge(s["po"], ready(t))
                            dve.wait_ge(s["added"], free(t, 2))
                            nc.vector.tensor_tensor(res[sub % 2][:, :], psO[sub % 2][:, 0:H], ds[:, :],
                                                    ALU.mult).then_inc(s["res"], 1)
                            dve.wait_ge(s["res"], ready(t))
                            nc.vector.tensor_tensor(at(x, t), at(x, t), res[sub % 2][:, :],
                                                    ALU.add).then_inc(s["added"], 1)



def constants(core):
    nc = core.nc
    s = core.sems("const", "iota chain")
    with nc.Block() as block:
        @block.gpsimd
        def _(pool):
            nc.gpsimd.iota(core.iota[:, :], [[1, P]], base=0, channel_multiplier=0,
                           allow_small_or_imprecise_dtypes=True).then_inc(s["iota"], 1)
            nc.gpsimd.iota(core.part[:, :], [[0, 1]], base=0, channel_multiplier=1,
                           allow_small_or_imprecise_dtypes=True).then_inc(s["iota"], 1)

        @block.vector
        def _(dve):
            dve.wait_ge(s["iota"], 2)
            do = Chain(dve, s["chain"])
            V, part = nc.vector, core.part[:, 0:1]
            do(V.tensor_scalar(core.ident[:, :], core.iota[:, :], part, None, ALU.is_equal))
            do(V.tensor_scalar(core.identb[:, :], core.iota[:, :], part, None, ALU.is_equal))
            do(V.tensor_copy(core.iotab[:, :], core.iota[:, :]))
            do(V.tensor_scalar(core.earlier[:, :], core.iota[:, :], part, None, ALU.is_gt))
            do(V.tensor_scalar(core.mask_q[:, :], core.iota[:, :], part, NEG, ALU.is_gt, ALU.mult))
            do(V.tensor_scalar(core.mask_k[:, :], core.iota[:, :], part, NEG, ALU.is_lt, ALU.mult))
            do(V.memset(core.onesb[:, :], 1.0))
            do(V.memset(core.onesf[:, :], 1.0))


def load(core, sem, dst, src):
    with core.nc.Block() as block:
        @block.sync
        def _(sp):
            sp.dma_start(dst, src).then_inc(sem, 16)


def program(nc, a, out):
    x_in = a["x"].rearrange("(t p) h -> p t h", p=P)
    x_out = out.rearrange("(t p) h -> p t h", p=P)
    with ExitStack() as ctx:
        core = Core(nc)
        sb, _ = scratch(nc, ctx)
        core.x = sb("x", [P, NT, H])
        core.rstd, core.nmr = sb("rstd", [P, NT]), sb("nmr", [P, NT])
        core.rstd1, core.rstd2, core.nmr2 = (sb(n, [P, NT]) for n in ("rstd1", "rstd2", "nmr2"))
        core.iota, core.part = sb("iota", [P, P]), sb("part", [P, 1])
        core.ident, core.identb = sb("ident", [P, P]), sb("identb", [P, P], BF16)
        core.iotab, core.earlier = sb("iotab", [P, P], BF16), sb("earlier", [P, P], BF16)
        core.mask_q, core.mask_k = sb("mask_q", [P, P], BF16), sb("mask_k", [P, P], BF16)
        core.onesb, core.onesf = sb("onesb", [P, P], BF16), sb("onesf", [P, 32])
        big = sb("experts", [P, 32, WE])
        rows = nc.dram_tensor("rows", (T, H), F32, kind="Internal").ap()
        results = nc.dram_tensor("results", (96 * P, H), F32, kind="Internal").ap()
        core.rows_flat, core.results_flat = rows, results
        core.rows = rows.rearrange("(t p) h -> p t h", p=P)
        core.results = results.rearrange("(t p) h -> p t h", p=P)
        core.stack = {w: nc.dram_tensor(f"stack_{w}", (B * H, SEGS, S), BF16, kind="Internal").ap() for w in "qk"}
        core.stack_rows = {w: ap.rearrange("c g s -> (c g) s") for w, ap in core.stack.items()}
        x_loaded, load0, load1a, load1b, load2, stored = (core.sem(n) for n in (
            "x_loaded", "load0", "load1a", "load1b", "load2", "stored"))

        with nc.Block() as block:
            @block.sync
            def _(sp):
                sp.dma_start(core.x[:, :, :], x_in).then_inc(x_loaded, 16)
                sp.wait_ge(x_loaded, 16)
        constants(core)

        def experts(name, E, kind, *loaded):
            m = Moe(core, name, E, kind, big)
            m.loaded = loaded
            return m

        half = 16
        load(core, load0, big[:, 0:half, :], a["m0_w"])
        load(core, load1b, big[:, half:, :], a["m1_w"][:, half:, :])
        with core.layer():
            layer0_attention(core, a["a0_wv"], a["a0_wg"], a["a0_bg"], a["a0_wq"], a["a0_bq"], a["a0_wo"])
        with core.layer():
            moe_layer(experts("m0", 16, "sigmoid", load0), a["m0_ws"], a["m0_wr"], a["m0_bias"])
        load(core, load1a, big[:, 0:half, :], a["m1_w"][:, 0:half, :])
        with core.layer():
            layer1_attention(core, a["a1_shift"], a["a1_gate"], a["a1_gamma"], a["a1_beta"], a["a1_kv"],
                         a["a1_decay"], a["a1_first"], a["a1_out"])
        with core.layer():
            moe_layer(experts("m1", 32, "softplus", load1a, load1b), a["m1_ws"], a["m1_wr"], a["m1_bias"])
        load(core, load2, big[:, :, :], a["m2_w"])
        with core.layer():
            softmax_attention(core, "a2", a["a2_w"], a["a2_out"], None)
        with core.layer():
            moe_layer(experts("m2", 32, "softmax", load2), a["m2_ws"], a["m2_wr"], None, a["m2_norm"])
        with core.layer():
            softmax_attention(core, "a3", a["a3_w"], a["a3_out"], (a["rope_cos"], a["rope_sin"]))
        with core.layer():
            last_ffn(core, a["f_gu"], a["f_down"], a["f_down_last"],
                 {n: (a[f"f_{n}"], a[f"f_{n}_last"]) for n in ("gs", "us")}, a["f_ds"])
        with nc.Block() as block:
            @block.sync
            def _(sp):
                sp.dma_start(x_out, core.x[:, :, :]).then_inc(stored, 16)
                sp.wait_ge(stored, 16)



def by_half(w):
    return w.reshape(KH, P, -1).transpose(1, 0, 2)


def wide(v):
    return np.broadcast_to(v.reshape(1, -1), (P, v.size))


def expert_rows(gate_up, down):
    e = gate_up.shape[0]
    gu = gate_up.reshape(e, KH, P, 2 * I).transpose(2, 0, 1, 3).reshape(P, e, KH * 2 * I)
    return np.concatenate([gu, down.transpose(1, 0, 2)], axis=2)


def swiglu(gate, up, down):
    return expert_rows(np.concatenate([gate, up], axis=1).transpose(0, 2, 1), down.transpose(0, 2, 1))


def heads_columns(w):
    return w.reshape(KH, P, 3, H).transpose(1, 0, 2, 3)


def rope_tables():
    inv = (1.0 / np.float32(10000.0) ** (np.arange(0, D, 2, dtype=np.float32) / np.float32(D))).astype(np.float32)
    ang = np.outer(np.arange(S, dtype=np.float32), inv).astype(np.float32)
    ang = np.concatenate([ang, ang], axis=1)
    sign = np.where(np.arange(D) % 2 == 0, -1.0, 1.0)
    return (np.tile(np.cos(ang.astype(np.float64)).T, (P // D, 1)).astype(np.float32),
            np.tile((np.sin(ang.astype(np.float64)) * sign).T, (P // D, 1)).astype(np.float32))


def layouts(i):
    a = {"x": i["L0_attn_x"].reshape(T, H)}
    for n in "vgqo":
        a[f"a0_w{n}"] = by_half(i[f"L0_attn_W{n}"])
    for n in "gq":
        a[f"a0_b{n}"] = i[f"L0_attn_b{n}"].reshape(KH, P).T
    a["m0_w"] = swiglu(i["L0_ffn_w_gate"], i["L0_ffn_w_up"], i["L0_ffn_w_down"])
    a["m0_ws"] = swiglu(i["L0_ffn_sw_gate"][None], i["L0_ffn_sw_up"][None], i["L0_ffn_sw_down"][None])[:, 0]
    a["m0_wr"] = by_half(i["L0_ffn_gate_w"].T)
    a["m0_bias"] = wide(i["L0_ffn_expert_bias"])
    a["a1_shift"] = by_half(i["L1_attn_W_shift"].T)
    a["a1_gate"] = wide(i["L1_attn_gate"])
    a["a1_gamma"] = wide(i["L1_attn_ln_gamma"])
    a["a1_beta"] = wide(i["L1_attn_ln_beta"])
    a["a1_kv"] = np.concatenate([by_half(i["L1_attn_W_key"].T), by_half(i["L1_attn_W_value"].T)], axis=2)
    a["a1_decay"] = np.tile(i["L1_attn_time_decay"].reshape(NS, 1), (B, 1))
    a["a1_first"] = np.tile(i["L1_attn_time_first"].reshape(NS, 1), (B, 1))
    a["a1_out"] = np.tile(i["L1_attn_W_output"].T, (B, 1))
    a["m1_w"] = swiglu(i["L1_ffn_gate_w"], i["L1_ffn_up_w"], i["L1_ffn_down_w"])
    a["m1_ws"] = swiglu(i["L1_ffn_shared_gate_w"][None], i["L1_ffn_shared_up_w"][None],
                        i["L1_ffn_shared_down_w"][None])[:, 0]
    a["m1_wr"] = by_half(i["L1_ffn_router_w"].T)
    a["m1_bias"] = wide(i["L1_ffn_expert_bias"])
    a["a2_w"] = heads_columns(i["L2_attn_w_qkv"])
    a["a2_out"] = by_half(i["L2_attn_w_out"])
    a["m2_w"] = expert_rows(i["L2_ffn_w13"], i["L2_ffn_w2"])
    a["m2_ws"] = expert_rows(np.concatenate([i["L2_ffn_shared_gate_w"], i["L2_ffn_shared_up_w"]], axis=1)[None],
                             i["L2_ffn_shared_down_w"][None])[:, 0]
    a["m2_wr"] = by_half(i["L2_ffn_gate_w"].T)
    a["m2_norm"] = wide(i["L2_ffn_norm_w"])
    w = heads_columns(i["L3_attn_Wqkv"].T)
    swap = np.arange(H) ^ 1
    a["a3_w"] = np.concatenate([w, w[:, :, 0:2][:, :, :, swap]], axis=2)
    a["a3_out"] = by_half(i["L3_attn_Wout"].T)
    a["rope_cos"], a["rope_sin"] = rope_tables()
    a["f_gu"] = np.concatenate([by_half(i["L3_ffn_gate_w"].T), by_half(i["L3_ffn_up_w"].T)], axis=2)
    down = i["L3_ffn_down_w"].T
    full = FI // P
    a["f_down"] = down[:full * P].reshape(full, P, H).transpose(1, 0, 2)
    a["f_down_last"] = down[full * P:]
    for n, key in (("gs", "gate_s"), ("us", "up_s")):
        v = i[f"L3_ffn_{key}"]
        a[f"f_{n}"] = v[:full * P].reshape(full, P).T
        a[f"f_{n}_last"] = v[full * P:].reshape(-1, 1)
    a["f_ds"] = wide(i["L3_ffn_down_s"])
    return a


def kernel(**inputs):
    import concourse.bacc as bacc
    from concourse.bass_utils import run_bass_kernel_spmd as run

    nc = bacc.Bacc("TRN2", target_bir_lowering=False, num_devices=1)
    arrays, args = {}, {}
    for name, value in layouts({k: np.asarray(v) for k, v in inputs.items()}).items():
        value = np.ascontiguousarray(value)
        arrays["in_" + name] = value
        args[name] = nc.dram_tensor("in_" + name, value.shape, mybir.dt.from_np(value.dtype), kind="ExternalInput").ap()
    out = nc.dram_tensor("out_0", (T, H), F32, kind="ExternalOutput").ap()
    program(nc, args, out)
    result = run(nc, [arrays], core_ids=[0])
    return result.results[0]["out_0"].reshape(B, S, H)
```

```python
from contextlib import ExitStack, contextmanager

import numpy as np

import concourse.bass as bass
from concourse import mybir

F32 = mybir.dt.float32
BF16 = mybir.dt.bfloat16
FP16 = mybir.dt.float16
I32 = mybir.dt.int32
U32 = mybir.dt.uint32
ALU = mybir.AluOpType
ACT = mybir.ActivationFunctionType
AX = mybir.AxisListType

P = 128
B, S, H = 2, 1024, 256
T = B * S
NT = T // P
KH = H // P
CH = 512
NC = T // CH
SUB = CH // P
TOPK = 4
I = 128
WE = 2 * KH * I + H
HEADS, D = 16, 16
BH = B * HEADS
KT = S // P
SEGS = 6
ROWS = SEGS * D
VD = D + 1
NS = 64
FI = 704
DECAY = 0.95
LN_EPS = 1e-5
RMS_EPS = 1e-6
CLIP = 7.0
NEG = -1e30

BASE = 8


def ready(t):
    return t + BASE + 1


def free(t, ring):
    return t + BASE + 1 - ring


def at(tensor, i):
    if isinstance(i, int):
        return tensor[:, i, :]
    return tensor[:, bass.ds(i, 1), :].rearrange("p a h -> p (a h)")


def col(tensor, i):
    if isinstance(i, int):
        return tensor[:, i:i + 1]
    return tensor[:, bass.ds(i, 1)]


def flat(ap):
    return ap.rearrange("p a b -> p (a b)")


class Step:

    def __init__(self, m, r, n):
        self.m, self.r, self.n = m, r, n

    def on(self, lag):
        return not isinstance(self.m, int) or 0 <= 4 * self.m + self.r - lag < self.n

    def behind(self, steps):
        return Step(self.m, self.r - steps, self.n)

    def tile(self, lag):
        q = self.r - lag
        return 4 * self.m + q, q % 4, self.m + q // 4


def pipeline(eng, n, step, lags, peel=2):
    for m in range(n // 4):
        for r in range(4):
            step(Step(m, r, n))
    for r in range(lags):
        step(Step(n // 4, r, n))


def settle(eng):
    eng.nop(nofuse=True)


class Chain:

    def __init__(self, eng, sem):
        self.eng, self.sem, self.n = eng, sem, 0

    def __call__(self, ins):
        self.n += 1
        ins.then_inc(self.sem, 1)
        self.eng.wait_ge(self.sem, self.n)


class Core:

    def __init__(self, nc):
        self.nc, self.open = nc, []
        self.behind = []

    def start_loads(self, sp):
        for dst, src, sem in self.behind:
            sp.dma_start(dst, src).then_inc(sem, 16)
        self.behind = []

    def sem(self, name):
        self.open.append(self.nc.alloc_semaphore(name=name))
        return self.open[-1]

    @contextmanager
    def layer(self):
        outer, self.open = self.open, []
        yield
        self.nc.clear_and_free_semaphores(self.open)
        self.nc.all_engine_barrier()
        self.open = outer

    def sems(self, stage, names):
        return {n: self.sem(f"{stage}_{n}") for n in names.split()}


def scratch(nc, ctx):
    def sb(name, shape, dt=F32):
        return ctx.enter_context(nc.sbuf_tensor(name, shape, dt))

    def ps(name, shape, dt=F32):
        return ctx.enter_context(nc.psum_tensor(name, shape, dt))
    return sb, ps


def open_sems(eng, *sems):
    for s in sems:
        eng.sem_inc(s, BASE)



def norm_stats(core, stage, src, rms=False, fetch=None):
    nc = core.nc
    with ExitStack() as ctx:
        sb, _ = scratch(nc, ctx)
        st = sb(f"{stage}_st", [P, NT, 6])
        work = sb(f"{stage}_work", [P, 6, NT])
        mean, dev, var, root, ysq, tmp = (work[:, i, :] for i in range(6))
        s = core.sems(stage, "stats chain var root")
        rstd, nmr = core.rstd, core.nmr

        with nc.Block() as block:
            @block.sync
            def _(sp):
                if fetch:
                    fetch(sp)

            @block.vector
            def _(dve):
                for t in range(NT):
                    nc.vector.bn_stats(at(st, t), at(src, t)).then_inc(s["stats"], 1)
                dve.wait_ge(s["stats"], NT)
                do = Chain(dve, s["chain"])

                def inverse_root(out, value):
                    nc.vector.tensor_copy(tmp, value).then_inc(s["var"], 1)
                    inverse_root.n += 1
                    dve.wait_ge(s["root"], inverse_root.n)
                    do(nc.vector.reciprocal(out, root))
                    do(nc.vector.tensor_tensor(ysq, out, out, ALU.mult))
                    do(nc.vector.tensor_tensor(ysq, ysq, tmp, ALU.mult))
                    do(nc.vector.tensor_scalar(ysq, ysq, -0.5, 1.5, ALU.mult, ALU.add))
                    do(nc.vector.tensor_tensor(out, out, ysq, ALU.mult))
                inverse_root.n = 0

                do(nc.vector.tensor_tensor(mean, st[:, :, 1], st[:, :, 4], ALU.add))
                do(nc.vector.tensor_tensor(dev, st[:, :, 1], st[:, :, 4], ALU.subtract))
                do(nc.vector.tensor_scalar(mean, mean, 0.5, None, ALU.mult))
                do(nc.vector.tensor_scalar(dev, dev, 0.5, None, ALU.mult))
                do(nc.vector.tensor_tensor(dev, dev, dev, ALU.mult))
                do(nc.vector.tensor_tensor(var, st[:, :, 2], st[:, :, 5], ALU.add))
                do(nc.vector.scalar_tensor_tensor(var, var, 1.0 / H, dev, ALU.mult, ALU.add))
                do(nc.vector.tensor_scalar(dev, var, LN_EPS, None, ALU.add))
                inverse_root(rstd[:, :], dev)
                do(nc.vector.scalar_tensor_tensor(nmr[:, :], mean, -1.0, rstd[:, :], ALU.mult, ALU.mult))
                if rms:
                    do(nc.vector.tensor_tensor(var, var, rstd[:, :], ALU.mult))
                    do(nc.vector.tensor_tensor(var, var, rstd[:, :], ALU.mult))
                    do(nc.vector.tensor_scalar(var, var, RMS_EPS, None, ALU.add))
                    inverse_root(core.rstd2[:, :], var)
                    do(nc.vector.tensor_tensor(core.rstd2[:, :], core.rstd2[:, :], rstd[:, :], ALU.mult))
                    do(nc.vector.scalar_tensor_tensor(core.nmr2[:, :], mean, -1.0, core.rstd2[:, :],
                                                      ALU.mult, ALU.mult))
                    do(nc.vector.tensor_scalar(core.rstd1[:, :], rstd[:, :], 1.0, None, ALU.add))

            @block.scalar
            def _(act):
                for n in range(2 if rms else 1):
                    act.wait_ge(s["var"], n + 1)
                    nc.scalar.activation(root, tmp, ACT.Sqrt).then_inc(s["root"], 1)



class Front:

    def __init__(self, core, stage, sb, psT, src, wait_used):
        self.core, self.nc, self.src = core, core.nc, src
        self.xn = [sb(f"{stage}_xn{i}", [P, H]) for i in range(4)]
        self.xt = [sb(f"{stage}_xt{i}", [P, KH, CH]) for i in range(2)]
        self.psT = psT
        self.s = core.sems(stage, "xn turned xt")
        self.wait_used = wait_used

    def open(self, eng, name):
        open_sems(eng, self.s[name])

    def vector(self, dve, c, group=None, done=None):
        for sub in range(SUB):
            t = SUB * c + sub
            g = SUB * (c if group is None else group) + sub
            dve.wait_ge(self.s["turned"], free(t, 4))
            ins = self.nc.vector.tensor_scalar(self.xn[sub][:, :], at(self.src, g), col(self.core.rstd, g),
                                               col(self.core.nmr, g), ALU.mult, ALU.add)
            ins.then_inc(done or self.s["xn"], 1)

    def tensor(self, pe, c):
        for sub in range(SUB):
            t = SUB * c + sub
            pe.wait_ge(self.s["xn"], ready(t))
            pe.wait_ge(self.s["xt"], free(t, 2))
            for k in range(KH):
                ins = self.nc.tensor.transpose(self.psT[sub % 2][:, k * P:(k + 1) * P],
                                               self.xn[sub][:, k * P:(k + 1) * P], self.core.ident[:, :])
            ins.then_inc(self.s["turned"], 1)

    def scalar(self, act, c, slot):
        self.wait_used(act, c)
        for sub in range(SUB):
            t = SUB * c + sub
            act.wait_ge(self.s["turned"], ready(t))
            self.nc.scalar.activation(self.xt[slot][:, :, sub * P:(sub + 1) * P],
                                      self.psT[sub % 2][:, 0:H].rearrange("p (k c) -> p k c", k=KH),
                                      ACT.Copy).then_inc(self.s["xt"], 1)



def layer0_attention(core, wv, wg, bg, wq, bq, wo):
    nc, x = core.nc, core.x
    with ExitStack() as ctx:
        sb, ps = scratch(nc, ctx)
        w = {n: sb(f"a0_w{n}", [P, KH, H]) for n in "vgqo"}
        bias = {n: sb(f"a0_b{n}", [P, KH]) for n in "gq"}
        decay = sb("a0_decay", [P, CH])
        sig_g = [sb(f"a0_sg{m}", [P, CH]) for m in range(KH)]
        sig_q = [sb(f"a0_sq{m}", [P, CH]) for m in range(KH)]
        store = [sb(f"a0_st{m}", [P, CH]) for m in range(KH)]
        mem = [[sb(f"a0_m{c}{m}", [P, CH]) for m in range(KH)] for c in range(2)]
        load = [[sb(f"a0_l{c}{m}", [P, CH]) for m in range(KH)] for c in range(2)]
        psT = [ps(f"a0_pT{i}", [P, CH]) for i in range(2)]
        psO = [ps(f"a0_pO{i}", [P, CH]) for i in range(2)]
        psG, psQ = ps("a0_pG", [P, CH]), ps("a0_pQ", [P, CH])
        psV = [ps(f"a0_pV{i}", [P, CH]) for i in range(2)]
        s = core.sems("a0", "weights decay pg pv pq sg sq store mem load po added")
        front = Front(core, "a0", sb, psT, x, lambda act, c: act.wait_ge(s["pq"], ready(KH * (c - 2) + KH - 1)))
        scale2 = float(np.float32(np.sqrt(1.0 - DECAY))) ** 2

        def fetch(sp):
            for n, src in (("v", wv), ("g", wg), ("q", wq), ("o", wo)):
                sp.dma_start(w[n][:, :, :], src).then_inc(s["weights"], 16)
            for n, src in (("g", bg), ("q", bq)):
                sp.dma_start(bias[n][:, :], src).then_inc(s["weights"], 16)
            core.start_loads(sp)
        norm_stats(core, "n0", x, fetch=fetch)

        with nc.Block() as block:
            @block.tensor
            def _(pe):
                front.open(pe, "turned")
                open_sems(pe, s["pg"], s["pv"], s["pq"], s["po"])
                pe.wait_ge(s["weights"], 96)

                def products(c):
                    pe.wait_ge(front.s["xt"], ready(SUB * c + SUB - 1))
                    for m in range(KH):
                        e = 2 * c + m
                        for name, dst, ring, freed, done in (("g", psG, 1, "sg", "pg"), ("v", psV[m], 2, "store", "pv"),
                                                             ("q", psQ, 1, "sq", "pq")):
                            pe.wait_ge(s[freed], free(e, ring))
                            for k in range(KH):
                                ins = nc.tensor.matmul(dst[:, :], w[name][:, k, m * P:(m + 1) * P],
                                                       front.xt[c % 2][:, k, :], start=k == 0, stop=k == KH - 1)
                            ins.then_inc(s[done], 1)

                def outputs(c):
                    pe.wait_ge(s["load"], ready(2 * c + 1))
                    for sub in range(SUB):
                        pe.wait_ge(s["added"], free(SUB * c + sub, 2))
                        for m in range(KH):
                            ins = nc.tensor.matmul(psO[sub % 2][:, 0:H], load[c % 2][m][:, sub * P:(sub + 1) * P],
                                                   w["o"][:, m, :], start=m == 0, stop=m == KH - 1)
                        ins.then_inc(s["po"], 1)
                front.tensor(pe, 0)
                for c in range(NC):
                    products(c)
                    if c < NC - 1:
                        front.tensor(pe, c + 1)
                    if c:
                        outputs(c - 1)
                outputs(NC - 1)

            @block.scalar
            def _(act):
                front.open(act, "xt")
                open_sems(act, s["sg"], s["sq"])
                nc.scalar.preload_act_table(ACT.Sigmoid)
                act.wait_ge(s["weights"], 96)
                front.scalar(act, 0, 0)
                for c in range(NC):
                    for m in range(KH):
                        e = 2 * c + m
                        act.wait_ge(s["pg"], ready(e))
                        act.wait_ge(s["store"], free(e, 2))
                        nc.scalar.activation(sig_g[m][:, :], psG[:, :], ACT.Sigmoid,
                                             bias=bias["g"][:, m:m + 1]).then_inc(s["sg"], 1)
                        act.wait_ge(s["pq"], ready(e))
                        act.wait_ge(s["load"], free(e, 2))
                        nc.scalar.activation(sig_q[m][:, :], psQ[:, :], ACT.Sigmoid,
                                             bias=bias["q"][:, m:m + 1]).then_inc(s["sq"], 1)
                    if c < NC - 1:
                        front.scalar(act, c + 1, (c + 1) % 2)

            @block.vector
            def _(dve):
                front.open(dve, "xn")
                open_sems(dve, s["store"], s["mem"], s["load"], s["added"])
                nc.vector.memset(decay[:, :], DECAY).then_inc(s["decay"], 1)
                dve.wait_ge(s["decay"], 1)

                def memory(c):
                    cc = c % 2
                    for m in range(KH):
                        e = 2 * c + m
                        dve.wait_ge(s["sg"], ready(e))
                        dve.wait_ge(s["pv"], ready(e))
                        dve.wait_ge(s["mem"], free(e, 2))
                        nc.vector.tensor_tensor(store[m][:, :], psV[m][:, :], sig_g[m][:, :],
                                                ALU.mult).then_inc(s["store"], 1)
                        dve.wait_ge(s["store"], ready(e))
                        nc.vector.tensor_tensor_scan(mem[cc][m][:, :], decay[:, :], store[m][:, :],
                                                     mem[0][m][:, CH - 1:CH] if cc else 0.0,
                                                     ALU.mult, ALU.add).then_inc(s["mem"], 1)
                        dve.wait_ge(s["mem"], ready(e))
                        dve.wait_ge(s["sq"], ready(e))
                        if c > 1:
                            dve.wait_ge(s["po"], ready(SUB * (c - 2) + SUB - 1))
                        nc.vector.scalar_tensor_tensor(load[cc][m][:, :], mem[cc][m][:, :], scale2, sig_q[m][:, :],
                                                       ALU.mult, ALU.mult).then_inc(s["load"], 1)

                def add(c):
                    for sub in range(SUB):
                        t = SUB * c + sub
                        dve.wait_ge(s["po"], ready(t))
                        nc.vector.tensor_tensor(at(x, t), at(x, t), psO[sub % 2][:, 0:H],
                                                ALU.add).then_inc(s["added"], 1)
                front.vector(dve, 0)
                for c in range(NC):
                    if c < NC - 1:
                        front.vector(dve, c + 1)
                    memory(c)
                    if c:
                        add(c - 1)
                add(NC - 1)



class Moe:

    def __init__(self, core, name, experts, kind, weights):
        self.core, self.name, self.E, self.kind, self.w = core, name, experts, kind, weights
        most = (T * TOPK - experts) // P + experts
        self.tiles = -(-most // 4) * 4


class FfnPipe:

    def __init__(self, core, stage, sb, ps, clip):
        self.core, self.nc, self.clip = core, core.nc, clip
        self.turn = 3 if clip else 2
        self.down = self.turn + 1
        self.src = [sb(f"{stage}_src{i}", [P, H]) for i in range(4)]
        self.xt = [sb(f"{stage}_xt{i}", [P, KH, P]) for i in range(2)]
        self.gu = [sb(f"{stage}_gu{i}", [P, 2 * I]) for i in range(2)]
        self.act = [sb(f"{stage}_act{i}", [P, I]) for i in range(2)]
        self.h = [sb(f"{stage}_h{i}", [P, I]) for i in range(2)]
        self.ht = [sb(f"{stage}_ht{i}", [P, I]) for i in range(2)]
        self.psT = [ps(f"{stage}_pT{i}", [P, CH]) for i in range(2)]
        self.psG = [ps(f"{stage}_pG{i}", [P, CH]) for i in range(2)]
        self.psH = [ps(f"{stage}_pH{i}", [P, CH]) for i in range(2)]
        self.psO = [ps(f"{stage}_pO{i}", [P, CH]) for i in range(2)]
        self.s = core.sems(stage, "turned xt pg clip act h ph ht po out")

    def open_tensor(self, pe):
        open_sems(pe, *(self.s[n] for n in ("turned", "pg", "ph", "po")))

    def open_scalar(self, act):
        open_sems(act, *(self.s[n] for n in ("xt", "act")))

    def open_vector(self, dve):
        open_sems(dve, *(self.s[n] for n in ("clip", "h", "ht", "out")))

    def tensor(self, pe, st, wait_source, weights, after_gate=None):
        nc, s = self.nc, self.s
        if st.on(0):
            t, r, m = st.tile(0)
            wait_source(pe, t, r, m)
            pe.wait_ge(s["xt"], free(t, 2))
            for k in range(KH):
                ins = nc.tensor.transpose(self.psT[r % 2][:, k * P:(k + 1) * P],
                                          self.src[r][:, k * P:(k + 1) * P], self.core.ident[:, :])
            ins.then_inc(s["turned"], 1)
        if st.on(1):
            t, r, _ = st.tile(1)
            w = weights(pe, t, 0)
            pe.wait_ge(s["xt"], ready(t))
            pe.wait_ge(s["clip" if self.clip else "h"], free(t, 2))
            for k in range(KH):
                ins = nc.tensor.matmul(self.psG[r % 2][:, 0:2 * I], self.xt[r % 2][:, k, :], w(k * 2 * I, 2 * I),
                                       start=k == 0, stop=k == KH - 1)
            if after_gate:
                after_gate(pe, t, r)
            else:
                ins.then_inc(s["pg"], 1)
        if st.on(self.turn):
            t, r, _ = st.tile(self.turn)
            pe.wait_ge(s["h"], ready(t))
            pe.wait_ge(s["ht"], free(t, 2))
            nc.tensor.transpose(self.psH[r % 2][:, 0:I], self.h[r % 2][:, :],
                                self.core.ident[:, :]).then_inc(s["ph"], 1)
        if st.on(self.down):
            t, r, _ = st.tile(self.down)
            w = weights(pe, t, 1)
            pe.wait_ge(s["ht"], ready(t))
            pe.wait_ge(s["out"], free(t, 2))
            nc.tensor.matmul(self.psO[r % 2][:, 0:H], self.ht[r % 2][:, :], w(2 * KH * I, H),
                             start=True, stop=True).then_inc(s["po"], 1)

    def scalar(self, act, st):
        nc, s = self.nc, self.s
        if st.on(0):
            t, r, _ = st.tile(0)
            act.wait_ge(s["turned"], ready(t))
            act.wait_ge(s["pg"], free(t, 2))
            nc.scalar.activation(flat(self.xt[r % 2][:, :, :]), self.psT[r % 2][:, 0:H],
                                 ACT.Copy).then_inc(s["xt"], 1)
        if st.on(1):
            t, r, _ = st.tile(1)
            act.wait_ge(s["clip" if self.clip else "pg"], ready(t))
            act.wait_ge(s["h"], free(t, 2))
            gate = self.gu[r % 2][:, 0:I] if self.clip else self.psG[r % 2][:, 0:I]
            nc.scalar.activation(self.act[r % 2][:, :], gate, ACT.Silu).then_inc(s["act"], 1)

    def vector(self, dve, st, take):
        nc, s = self.nc, self.s
        if st.on(1):
            t, r, _ = st.tile(1)
            if self.clip:
                dve.wait_ge(s["pg"], ready(t))
                dve.wait_ge(s["h"], free(t, 2))
                nc.vector.tensor_scalar(self.gu[r % 2][:, :], self.psG[r % 2][:, 0:2 * I], -CLIP, CLIP,
                                        ALU.max, ALU.min).then_inc(s["clip"], 1)
            else:
                dve.wait_ge(s["act"], ready(t))
                dve.wait_ge(s["ph"], free(t, 2))
                nc.vector.tensor_tensor(self.h[r % 2][:, :], self.psG[r % 2][:, I:2 * I], self.act[r % 2][:, :],
                                        ALU.mult).then_inc(s["h"], 1)
        if st.on(self.turn):
            t, r, _ = st.tile(self.turn)
            dve.wait_ge(s["ph"], ready(t))
            dve.wait_ge(s["po"], free(t, 2))
            nc.vector.tensor_copy(self.ht[r % 2][:, :], self.psH[r % 2][:, 0:I]).then_inc(s["ht"], 1)
        if st.on(self.down):
            t, r, m = st.tile(self.down)
            dve.wait_ge(s["po"], ready(t))
            take(t, r, m).then_inc(s["out"], 1)
        if st.on(1) and self.clip:
            t, r, _ = st.tile(1)
            dve.wait_ge(s["act"], ready(t))
            dve.wait_ge(s["ph"], free(t, 2))
            nc.vector.tensor_tensor(self.h[r % 2][:, :], self.gu[r % 2][:, I:2 * I], self.act[r % 2][:, :],
                                    ALU.mult).then_inc(s["h"], 1)


def moe_dense(moe, shared, router, norm_w, logits):
    core, nc, E = moe.core, moe.core.nc, moe.E
    x = core.x
    stage = moe.name + "d"
    rms = norm_w is not None
    AHEAD = 2
    with ExitStack() as ctx:
        sb, ps = scratch(nc, ctx)
        pipe = FfnPipe(core, stage, sb, ps, moe.kind == "softplus")
        ws = sb(f"{stage}_ws", [P, WE])
        wr = sb(f"{stage}_wr", [P, KH, E])
        nw = sb(f"{stage}_nw", [P, H]) if rms else None
        s = core.sems(stage, "weights norm xn logits")
        kept = [core.sem(f"{stage}_kept{i}") for i in range(4)]

        def fetch(sp):
            sp.dma_start(ws[:, :], shared).then_inc(s["weights"], 16)
            sp.dma_start(wr[:, :, :], router).then_inc(s["weights"], 16)
            if rms:
                sp.dma_start(nw[:, :], norm_w).then_inc(s["weights"], 16)
        norm_stats(core, moe.name + "n", x, rms, fetch)

        with nc.Block() as block:
            @block.sync
            def _(sp):
                def step(st):
                    if st.on(0):
                        t, r, _ = st.tile(0)
                        sp.wait_ge(s["xn"], ready(t))
                        sp.dma_start(at(core.rows, t), pipe.src[r][:, :]).then_inc(kept[r], 16)
                pipeline(sp, NT, step, 0)
                for r in range(4):
                    sp.wait_ge(kept[r], 16 * NT // 4)

            @block.tensor
            def _(pe):
                pipe.open_tensor(pe)
                pe.wait_ge(s["weights"], 48 if rms else 32)

                def source(pe, t, r, m):
                    pe.wait_ge(s["xn"], ready(t))

                def after_gate(pe, t, r):
                    pe.wait_ge(s["logits"], free(t, 2))
                    for k in range(KH):
                        ins = nc.tensor.matmul(pipe.psG[r % 2][:, 2 * I:2 * I + E], pipe.xt[r % 2][:, k, :], wr[:, k, :],
                                               start=k == 0, stop=k == KH - 1)
                    ins.then_inc(pipe.s["pg"], 1)

                def step(st):
                    pipe.tensor(pe, st, source, lambda pe, t, part: lambda a, n: ws[:, a:a + n], after_gate)
                pipeline(pe, NT, step, pipe.down)

            @block.scalar
            def _(act):
                pipe.open_scalar(act)
                nc.scalar.preload_act_table(ACT.Silu)
                if not pipe.clip:
                    open_sems(act, s["logits"])

                def step(st):
                    if st.on(1) and not pipe.clip:
                        t, r, _ = st.tile(1)
                        act.wait_ge(pipe.s["pg"], ready(t))
                        nc.scalar.activation(at(logits, t), pipe.psG[r % 2][:, 2 * I:2 * I + E],
                                             ACT.Copy).then_inc(s["logits"], 1)
                    pipe.scalar(act, st)
                pipeline(act, NT, step, 1)

            @block.vector
            def _(dve):
                pipe.open_vector(dve)
                open_sems(dve, s["xn"], s["norm"])
                if pipe.clip:
                    open_sems(dve, s["logits"])
                if rms:
                    dve.wait_ge(s["weights"], 48)

                def take(t, r, m):
                    return nc.vector.tensor_tensor(at(x, t), at(x, t), pipe.psO[r % 2][:, 0:H], ALU.add)

                def step(st):
                    if st.on(0):
                        t, r, m = st.tile(0)
                        dve.wait_ge(pipe.s["turned"], free(t, 4))
                        if not isinstance(m, int) or m:
                            dve.wait_ge(kept[r], 16 * m)
                        rstd, nmr = (core.rstd2, core.nmr2) if rms else (core.rstd, core.nmr)
                        ins = nc.vector.tensor_scalar(pipe.src[r][:, :], at(x, t), col(rstd, t), col(nmr, t),
                                                      ALU.mult, ALU.add)
                        if rms:
                            ins.then_inc(s["norm"], 1)
                            dve.wait_ge(s["norm"], ready(2 * t))
                            nc.vector.tensor_tensor(pipe.src[r][:, :], pipe.src[r][:, :], nw[:, :],
                                                    ALU.mult).then_inc(s["xn"], 1)
                            nc.vector.tensor_scalar(at(x, t), at(x, t), col(core.rstd1, t), col(core.nmr, t),
                                                    ALU.mult, ALU.add).then_inc(s["norm"], 1)
                        else:
                            ins.then_inc(s["xn"], 1)
                    st = st.behind(AHEAD)
                    if st.on(1) and pipe.clip:
                        t, r, _ = st.tile(1)
                        dve.wait_ge(pipe.s["pg"], ready(t))
                        nc.vector.tensor_copy(at(logits, t), pipe.psG[r % 2][:, 2 * I:2 * I + E]
                                              ).then_inc(s["logits"], 1)
                    if rms and st.on(pipe.down):
                        dve.wait_ge(s["norm"], ready(2 * st.tile(pipe.down)[0] + 1))
                    pipe.vector(dve, st, take)
                pipeline(dve, NT, step, pipe.down + AHEAD)


def moe_route(moe, logits, expert_bias, out):
    core, nc, E, name = moe.core, moe.core.nc, moe.E, moe.name
    NE = moe.tiles
    with ExitStack() as ctx:
        sb, ps = scratch(nc, ctx)
        score = sb(f"{name}_score", [P, NT, E])
        sel = sb(f"{name}_sel", [P, NT, E])
        tmp = sb(f"{name}_tmp", [P, NT, E])
        tmp2 = sb(f"{name}_tmp2", [P, NT, E])
        bias = sb(f"{name}_bias", [P, E])
        top = sb(f"{name}_top", [P, NT, 8])
        idx = sb(f"{name}_idx", [P, NT, 8], U32)
        idxf = sb(f"{name}_idxf", [P, NT, TOPK])
        hot = sb(f"{name}_hot", [P, NT, TOPK, E])
        prod = sb(f"{name}_prod", [P, NT, TOPK, E])
        mask = sb(f"{name}_mask", [P, NT, E], BF16)
        before = sb(f"{name}_before", [P, NT + 1, E], BF16)
        row = sb(f"{name}_row", [P, 8, NT])
        count = sb(f"{name}_count", [P, 4, E])
        counti = sb(f"{name}_counti", [P, E], I32)
        slot = sb(f"{name}_slot", [P, NT, TOPK])
        sloti = sb(f"{name}_sloti", [P, 2, NT, TOPK], I32)
        hi = sb(f"{name}_hi", [P, NT * TOPK])
        lo = sb(f"{name}_lo", [P, NT * TOPK])
        eid = sb(f"{name}_eid", [P, 1])
        ge = sb(f"{name}_ge", [P, E])
        pick = [sb(f"{name}_pick{i}", [P, TOPK, P], FP16) for i in range(2)]
        place = [sb(f"{name}_place{i}", [P, TOPK, NE], FP16) for i in range(2)]
        psR = ps(f"{name}_psR", [P, NT, E])
        psC = ps(f"{name}_psC", [P, E])
        psE = ps(f"{name}_psE", [P, P])
        psI = ps(f"{name}_psI", [P, NE])
        s = core.sems(name + "r", "bias chain act acted mask ranks eid row picks used")

        def bc(ap, shape):
            return ap.to_broadcast(shape) if False else ap.broadcast_to(shape)

        with nc.Block() as block:
            @block.sync
            def _(sp):
                if expert_bias is not None:
                    sp.dma_start(bias[:, :], expert_bias).then_inc(s["bias"], 16)

            @block.scalar
            def _(act):
                if moe.kind == "sigmoid":
                    nc.scalar.activation(score[:, :, :], logits[:, :, :], ACT.Sigmoid).then_inc(s["acted"], 1)
                elif moe.kind == "softmax":
                    act.wait_ge(s["act"], 1)
                    nc.scalar.activation(tmp[:, :, :], tmp2[:, :, :], ACT.Exp).then_inc(s["acted"], 1)
                else:
                    act.wait_ge(s["act"], 1)
                    nc.scalar.activation(tmp[:, :, :], tmp2[:, :, :], ACT.Exp).then_inc(s["acted"], 1)
                    act.wait_ge(s["act"], 2)
                    nc.scalar.activation(score[:, :, :], tmp2[:, :, :], ACT.Ln).then_inc(s["acted"], 1)
                    act.wait_ge(s["act"], 3)
                    nc.scalar.activation(score[:, :, :], tmp[:, :, :], ACT.Sqrt).then_inc(s["acted"], 1)

            @block.vector
            def _(dve):
                do = Chain(dve, s["chain"])
                V = nc.vector
                dve.wait_ge(s["acted"], 1) if moe.kind == "sigmoid" else None
                if moe.kind == "softmax":
                    rmax, rsum = row[:, 0, :], row[:, 1, :]
                    do(V.tensor_reduce(rmax, logits[:, :, :], AX.X, ALU.max))
                    V.tensor_tensor(tmp2[:, :, :], logits[:, :, :], rmax.unsqueeze(2).broadcast_to([P, NT, E]),
                                    ALU.subtract).then_inc(s["act"], 1)
                    dve.wait_ge(s["acted"], 1)
                    do(V.tensor_reduce(rsum, tmp[:, :, :], AX.X, ALU.add))
                    do(V.reciprocal(rsum, rsum))
                    do(V.tensor_tensor(score[:, :, :], tmp[:, :, :], rsum.unsqueeze(2).broadcast_to([P, NT, E]),
                                       ALU.mult))
                if moe.kind == "softplus":
                    do(V.tensor_scalar(tmp2[:, :, :], logits[:, :, :], -1.0, None, ALU.mult))
                    V.tensor_tensor(tmp2[:, :, :], tmp2[:, :, :], logits[:, :, :], ALU.min).then_inc(s["act"], 1)
                    dve.wait_ge(s["acted"], 1)
                    V.tensor_scalar(tmp2[:, :, :], tmp[:, :, :], 1.0, None, ALU.add).then_inc(s["act"], 1)
                    dve.wait_ge(s["act"], 2)
                    dve.wait_ge(s["acted"], 2)
                    do(V.tensor_scalar(tmp2[:, :, :], tmp2[:, :, :], -1.0, None, ALU.add))
                    do(V.tensor_scalar(sel[:, :, :], tmp2[:, :, :], 0.0, None, ALU.is_equal))
                    do(V.tensor_tensor(tmp2[:, :, :], tmp2[:, :, :], sel[:, :, :], ALU.add))
                    do(V.tensor_tensor(sel[:, :, :], score[:, :, :], sel[:, :, :], ALU.add))
                    do(V.reciprocal(tmp2[:, :, :], tmp2[:, :, :]))
                    do(V.tensor_tensor(sel[:, :, :], sel[:, :, :], tmp2[:, :, :], ALU.mult))
                    do(V.tensor_tensor(tmp[:, :, :], tmp[:, :, :], sel[:, :, :], ALU.mult))
                    V.scalar_tensor_tensor(tmp[:, :, :], logits[:, :, :], 0.0, tmp[:, :, :], ALU.max,
                                           ALU.add).then_inc(s["act"], 1)
                    dve.wait_ge(s["act"], 3)
                    dve.wait_ge(s["acted"], 3)
                choose = score
                if expert_bias is not None:
                    dve.wait_ge(s["bias"], 16)
                    do(V.tensor_tensor(sel[:, :, :], score[:, :, :], bias[:, :].unsqueeze(1).broadcast_to([P, NT, E]),
                                       ALU.add))
                    choose = sel
                for t in range(NT):
                    V.max(top[:, t, :], choose[:, t, :]).then_inc(s["chain"], 1)
                do.n += NT
                dve.wait_ge(s["chain"], do.n)
                for t in range(NT):
                    V.max_index(idx[:, t, :], top[:, t, :], choose[:, t, :]).then_inc(s["chain"], 1)
                do.n += NT
                dve.wait_ge(s["chain"], do.n)
                do(V.tensor_copy(idxf[:, :, :], idx[:, :, 0:TOPK]))
                for k in range(TOPK):
                    V.tensor_tensor(hot[:, :, k, :], core.iota[:, 0:E].unsqueeze(1).broadcast_to([P, NT, E]),
                                    idxf[:, :, k:k + 1].broadcast_to([P, NT, E]), ALU.is_equal).then_inc(s["chain"], 1)
                do.n += TOPK
                dve.wait_ge(s["chain"], do.n)
                V.tensor_tensor(tmp[:, :, :], hot[:, :, 0, :], hot[:, :, 1, :], ALU.add).then_inc(s["chain"], 1)
                V.tensor_tensor(tmp2[:, :, :], hot[:, :, 2, :], hot[:, :, 3, :], ALU.add).then_inc(s["chain"], 1)
                do.n += 2
                dve.wait_ge(s["chain"], do.n)
                do(V.tensor_tensor(mask[:, :, :], tmp[:, :, :], tmp2[:, :, :], ALU.add))
                do(V.memset(before[:, 0, :], 0.0))
                for t in range(NT):
                    ins = V.tensor_tensor(before[:, t + 1, :], before[:, t, :], mask[:, t, :], ALU.add)
                    if t < NT - 1:
                        do(ins)
                    else:
                        ins.then_inc(s["mask"], 1)

                def chosen(dst, values):
                    for k in range(TOPK):
                        V.tensor_tensor(prod[:, :, k, :], hot[:, :, k, :], values, ALU.mult).then_inc(s["chain"], 1)
                    do.n += TOPK
                    dve.wait_ge(s["chain"], do.n)
                    do(V.tensor_reduce(dst, prod[:, :, :, :], AX.X, ALU.add))
                if choose is score:
                    do(V.tensor_copy(out["weight"][:, :, :], top[:, :, 0:TOPK]))
                else:
                    chosen(out["weight"][:, :, :], score[:, :, :])
                total = row[:, 2, :]
                do(V.tensor_reduce(total, out["weight"][:, :, :], AX.X, ALU.add))
                if moe.kind == "softplus":
                    do(V.tensor_scalar(total, total, 1e-20, None, ALU.add))
                do(V.reciprocal(total, total))
                do(V.tensor_tensor(out["weight"][:, :, :], out["weight"][:, :, :],
                                   total.unsqueeze(2).broadcast_to([P, NT, TOPK]), ALU.mult))

                cnt, need, end, start = (count[:, i, :] for i in range(4))
                dve.wait_ge(s["ranks"], 1)
                do(V.tensor_scalar(cnt, psC[:, :], float(P - 1), None, ALU.add))
                do(V.tensor_copy(counti[:, :], cnt))
                do(V.tensor_scalar(counti[:, :], counti[:, :], 7, None, ALU.arith_shift_right))
                do(V.tensor_copy(need, counti[:, :]))
                do(V.tensor_tensor_scan(end, core.onesf[:, 0:E], need, 0.0, ALU.mult, ALU.add))
                do(V.tensor_tensor(start, end, need, ALU.subtract))
                do(V.tensor_scalar(ge[:, :], end, core.part[:, 0:1], None, ALU.is_le))
                do(V.tensor_reduce(eid[:, :], ge[:, :], AX.X, ALU.add))
                V.tensor_scalar(eid[:, :], eid[:, :], float(E - 1), None, ALU.min).then_inc(s["eid"], 1)
                do(V.tensor_scalar(start, start, float(P), None, ALU.mult))
                if moe.kind == "softmax":
                    do(V.tensor_scalar(tmp[:, :, :], psR[:, :, :], float(2 * T * TOPK // E - 1), None, ALU.min))
                    do(V.tensor_tensor(tmp[:, :, :], tmp[:, :, :], start.unsqueeze(1).broadcast_to([P, NT, E]),
                                       ALU.add))
                    chosen(slot[:, :, :], tmp[:, :, :])
                    do(V.tensor_copy(out["read"][:, :, :], slot[:, :, :]))
                do(V.tensor_tensor(tmp[:, :, :], psR[:, :, :], start.unsqueeze(1).broadcast_to([P, NT, E]), ALU.add))
                chosen(slot[:, :, :], tmp[:, :, :])
                if moe.kind != "softmax":
                    do(V.tensor_copy(out["read"][:, :, :], slot[:, :, :]))
                do(V.tensor_copy(sloti[:, 0, :, :], slot[:, :, :]))
                do(V.tensor_scalar(sloti[:, 1, :, :], sloti[:, 0, :, :], 7, None, ALU.arith_shift_right))
                do(V.tensor_copy(hi[:, :], sloti[:, 1, :, :].rearrange("p a b -> p (a b)")))
                do(V.scalar_tensor_tensor(lo[:, :], hi[:, :], -float(P), slot[:, :, :].rearrange("p a b -> p (a b)"),
                                          ALU.mult, ALU.add))
                with dve.Fori(0, NT // 2) as n:
                    for par in range(2):
                        t = 2 * n + par
                        dve.wait_ge(s["used"], free(t, 2))
                        for k in range(TOPK):
                            V.tensor_scalar(pick[par][:, k, :], core.iotab[:, :], col(lo, 4 * t + k), None, ALU.is_equal)
                            ins = V.tensor_scalar(place[par][:, k, :], core.iotab[:, 0:NE], col(hi, 4 * t + k),
                                                  col(core.number, t), ALU.is_equal, ALU.mult)
                        ins.then_inc(s["picks"], 1)
                dve.wait_ge(s["used"], ready(NT - 1))
                do(V.tensor_copy(out["token"][:, 0:NE], psI[:, :]))
                dve.wait_ge(s["row"], 1)
                do(V.tensor_copy(out["expert"][0:1, 0:P], psE[0:1, :]))

            @block.tensor
            def _(pe):
                open_sems(pe, s["used"])
                pe.wait_ge(s["mask"], 1)
                fr = psR[:, :, :].rearrange("p a b -> p (a b)")
                nc.tensor.matmul(fr, core.earlier[:, :], mask[:, :, :].rearrange("p a b -> p (a b)"),
                                 start=True, stop=False)
                nc.tensor.matmul(fr, core.onesb[:, :], before[:, 0:NT, :].rearrange("p a b -> p (a b)"),
                                 start=False, stop=True)
                nc.tensor.matmul(psC[:, :], core.onesb[:, :], before[:, NT, :], start=True,
                                 stop=True).then_inc(s["ranks"], 1)
                pe.wait_ge(s["eid"], 1)
                nc.tensor.matmul(psE[0:1, :], eid[:, 0:1], core.ident[:, :], start=True, stop=True).then_inc(s["row"], 1)
                for t in range(NT):
                    pe.wait_ge(s["picks"], t + 1)
                    for k in range(TOPK):
                        ins = nc.tensor.matmul(psI[:, :], pick[t % 2][:, k, :], place[t % 2][:, k, :],
                                               start=t + k == 0, stop=t * k == (NT - 1) * (TOPK - 1))
                    ins.then_inc(s["used"], 1)


def moe_experts(moe, out):
    core, nc = moe.core, moe.core.nc
    stage, N = moe.name + "e", moe.tiles
    with ExitStack() as ctx:
        sb, ps = scratch(nc, ctx)
        pipe = FfnPipe(core, stage, sb, ps, moe.kind == "softplus")
        tok = [sb(f"{stage}_tok{i}", [P, 1], I32) for i in range(4)]
        y = [sb(f"{stage}_y{i}", [P, H]) for i in range(4)]
        s = core.sems(stage, "tok")
        got = [core.sem(f"{stage}_got{i}") for i in range(4)]
        kept = [core.sem(f"{stage}_kept{i}") for i in range(4)]
        w3 = moe.w

        with nc.Block() as block:
            @block.gpsimd
            def _(pool):
                open_sems(pool, s["tok"])

                def step(st):
                    if st.on(0):
                        t, r, m = st.tile(0)
                        if not isinstance(m, int) or m:
                            pool.wait_ge(got[r], 16 * m)
                        settle(pool)
                        nc.gpsimd.tensor_copy(tok[r][:, :], col(out["token"], t)).then_inc(s["tok"], 1)
                        pool.wait_ge(s["tok"], ready(t))
                        pool.wait_ge(pipe.s["turned"], free(t, 4))
                        settle(pool)
                        pool.indirect_dma_start(pipe.src[r][:, :], None, core.rows_flat,
                                                bass.IndirectOffsetOnAxis(ap=tok[r][:, 0:1].bitcast(U32), axis=0)
                                                ).then_inc(got[r], 16)
                pipeline(pool, N, step, 0)

            @block.sync
            def _(sp):
                def step(st):
                    if st.on(3):
                        t, r, _ = st.tile(3)
                        sp.wait_ge(pipe.s["out"], ready(t))
                        sp.dma_start(at(core.results, t), y[r][:, :]).then_inc(kept[r], 16)
                pipeline(sp, N, step, 3)
                for r in range(4):
                    sp.wait_ge(kept[r], 16 * N // 4)

            @block.tensor
            def _(pe):
                pipe.open_tensor(pe)
                for loaded in moe.loaded:
                    pe.wait_ge(loaded, 16)

                def source(pe, t, r, m):
                    pe.wait_ge(got[r], 16 * (m + 1))

                expert = {}

                def weights(pe, t, part):
                    if t not in expert:
                        expert[t] = pe.value_load(out["expert"][0:1, t:t + 1], min_val=0, max_val=moe.E - 1)
                        e = expert[t]
                    else:
                        e = expert.pop(t)
                    return lambda a, n: w3[:, bass.ds(e, 1), a:a + n].rearrange("p a c -> p (a c)")
                pipeline(pe, N, lambda st: pipe.tensor(pe, st, source, weights), pipe.down)

            @block.scalar
            def _(act):
                pipe.open_scalar(act)
                nc.scalar.preload_act_table(ACT.Silu)
                pipeline(act, N, lambda st: pipe.scalar(act, st), 1)

            @block.vector
            def _(dve):
                pipe.open_vector(dve)

                def take(t, r, m):
                    if not isinstance(m, int) or m:
                        dve.wait_ge(kept[r], 16 * m)
                    return nc.vector.tensor_copy(y[r][:, :], pipe.psO[r % 2][:, 0:H])
                pipeline(dve, N, lambda st: pipe.vector(dve, st, take), pipe.down)


def moe_combine(moe, out):
    core, nc = moe.core, moe.core.nc
    stage = moe.name + "c"
    with ExitStack() as ctx:
        sb, _ = scratch(nc, ctx)
        at_slot = [[sb(f"{stage}_at{i}{k}", [P, 1], I32) for k in range(TOPK)] for i in range(2)]
        got_rows = [[sb(f"{stage}_g{i}{k}", [P, H]) for k in range(TOPK)] for i in range(2)]
        s = core.sems(stage, "slots summed")
        got = [[core.sem(f"{stage}_got{i}{k}") for k in range(TOPK)] for i in range(2)]

        with nc.Block() as block:
            @block.gpsimd
            def _(pool):
                open_sems(pool, s["slots"])
                with pool.Fori(0, NT // 2) as n:
                    for par in range(2):
                        t = 2 * n + par
                        pool.wait_ge(s["summed"], ready(TOPK * t - 2 * TOPK + TOPK - 1))
                        settle(pool)
                        for k in range(TOPK):
                            ins = nc.gpsimd.tensor_copy(at_slot[par][k][:, :], col(out["readf"], TOPK * t + k))
                        ins.then_inc(s["slots"], 1)
                        pool.wait_ge(s["slots"], ready(t))
                        settle(pool)
                        for k in range(TOPK):
                            pool.indirect_dma_start(got_rows[par][k][:, :], None, core.results_flat[0:moe.tiles * P, :],
                                                    bass.IndirectOffsetOnAxis(ap=at_slot[par][k][:, 0:1].bitcast(U32),
                                                                              axis=0)).then_inc(got[par][k], 16)

            @block.vector
            def _(dve):
                open_sems(dve, s["summed"])
                with dve.Fori(0, NT // 2) as n:
                    for par in range(2):
                        t = 2 * n + par
                        for k in range(TOPK):
                            e = TOPK * t + k
                            dve.wait_ge(got[par][k], 16 * n + 16)
                            dve.wait_ge(s["summed"], free(e, 1))
                            nc.vector.scalar_tensor_tensor(at(core.x, t), got_rows[par][k][:, :],
                                                           col(out["weightf"], e), at(core.x, t),
                                                           ALU.mult, ALU.add).then_inc(s["summed"], 1)


def moe_layer(moe, shared, router, expert_bias, norm_w=None):
    core, nc, E, name = moe.core, moe.core.nc, moe.E, moe.name
    with ExitStack() as ctx:
        sb, _ = scratch(nc, ctx)
        weight = sb(f"{name}_weight", [P, NT, TOPK])
        read = sb(f"{name}_read", [P, NT, TOPK], I32)
        out = {"weight": weight, "weightf": weight[:, :, :].rearrange("p a b -> p (a b)"),
               "read": read, "readf": read[:, :, :].rearrange("p a b -> p (a b)"),
               "token": sb(f"{name}_token", [P, moe.tiles], I32), "expert": sb(f"{name}_expert", [1, P], I32)}
        with ExitStack() as inner:
            logits = inner.enter_context(nc.sbuf_tensor(f"{name}_logits", [P, NT, E], F32))
            moe_dense(moe, shared, router, norm_w, logits)
            moe_route(moe, logits, expert_bias, out)
        moe_experts(moe, out)
        moe_combine(moe, out)



def layer1_attention(core, shift, gate, gamma, beta, kv, time_decay, time_first, w_out):
    nc, x = core.nc, core.x
    with ExitStack() as ctx:
        sb, _ = scratch(nc, ctx)
        shifted = sb("a1_shifted", [P, NT, H])
        states = sb("a1_states", [P, S])
        layer1_shift(core, shift, gate, shifted)
        layer1_scan(core, gamma, beta, kv, time_decay, time_first, shifted, states)
        layer1_out(core, w_out, states)


def layer1_shift(core, shift, gate, shifted):
    nc, x = core.nc, core.x
    with ExitStack() as ctx:
        sb, ps = scratch(nc, ctx)
        w = sb("a1_w", [P, KH, H])
        g_new, g_old = sb("a1_gnew", [P, H]), sb("a1_gold", [P, H])
        xn = [sb(f"a1_xn{q}", [P, H]) for q in range(4)]
        xt = [sb(f"a1_xt{q}", [P, KH, P]) for q in range(2)]
        new = [sb(f"a1_new{q}", [P, H]) for q in range(2)]
        old = [sb(f"a1_old{q}", [P, H]) for q in range(2)]
        psT = [ps(f"a1_pT{q}", [P, CH]) for q in range(2)]
        psS = [ps(f"a1_pS{q}", [P, CH]) for q in range(2)]
        s = core.sems("a1", "weights gate gates xn turned xt ps new old mixed")

        def fetch(sp):
            sp.dma_start(w[:, :, :], shift).then_inc(s["weights"], 16)
            sp.dma_start(g_new[:, :], gate).then_inc(s["weights"], 16)
            core.start_loads(sp)
        norm_stats(core, "n1", x, fetch=fetch)

        with nc.Block() as block:
            @block.scalar
            def _(act):
                open_sems(act, s["xt"])
                act.wait_ge(s["weights"], 32)
                nc.scalar.activation(g_new[:, :], g_new[:, :], ACT.Sigmoid).then_inc(s["gate"], 1)
                with act.Fori(0, 4) as n:
                    for q in range(4):
                        e = 4 * n + q
                        act.wait_ge(s["turned"], ready(e))
                        act.wait_ge(s["ps"], free(e, 2))
                        nc.scalar.activation(flat(xt[q % 2][:, :, :]), psT[q % 2][:, 0:H],
                                             ACT.Copy).then_inc(s["xt"], 1)

            @block.tensor
            def _(pe):
                open_sems(pe, s["turned"], s["ps"])
                pe.wait_ge(s["weights"], 32)
                with pe.Fori(0, 4) as n:
                    for q in range(4):
                        e = 4 * n + q
                        pe.wait_ge(s["xn"], ready(e))
                        pe.wait_ge(s["xt"], free(e, 2))
                        for k in range(KH):
                            ins = nc.tensor.transpose(psT[q % 2][:, k * P:(k + 1) * P], xn[q][:, k * P:(k + 1) * P],
                                                      core.ident[:, :])
                        ins.then_inc(s["turned"], 1)
                        pe.wait_ge(s["xt"], ready(e))
                        pe.wait_ge(s["new"], free(e, 2))
                        for k in range(KH):
                            ins = nc.tensor.matmul(psS[q % 2][:, 0:H], xt[q % 2][:, k, :], w[:, k, :],
                                                   start=k == 0, stop=k == KH - 1)
                        ins.then_inc(s["ps"], 1)

            @block.gpsimd
            def _(pool):
                open_sems(pool, s["old"])
                pool.wait_ge(s["gates"], 1)
                with pool.Fori(0, 4) as n:
                    for q in range(4):
                        e = 4 * n + q
                        pool.wait_ge(s["xn"], ready(4 * n + (q | 1)))
                        pool.wait_ge(s["mixed"], free(e, 2))
                        nc.gpsimd.tensor_tensor(old[q % 2][:, :], xn[q ^ 1][:, :], g_old[:, :],
                                                ALU.mult).then_inc(s["old"], 1)

            @block.vector
            def _(dve):
                open_sems(dve, s["xn"], s["new"], s["mixed"])
                dve.wait_ge(s["gate"], 1)
                nc.vector.tensor_scalar(g_old[:, :], g_new[:, :], -1.0, 1.0, ALU.mult, ALU.add).then_inc(s["gates"], 1)
                with dve.Fori(0, 4) as n:
                    for q in range(4):
                        e = 4 * n + q
                        t = 4 * q + n
                        dve.wait_ge(s["turned"], free(e, 4))
                        dve.wait_ge(s["old"], ready(4 * n - 4 + (q ^ 1)))
                        nc.vector.tensor_scalar(xn[q][:, :], at(x, t), col(core.rstd, t), col(core.nmr, t),
                                                ALU.mult, ALU.add).then_inc(s["xn"], 1)
                    for q in range(4):
                        e = 4 * n + q
                        dve.wait_ge(s["ps"], ready(e))
                        dve.wait_ge(s["mixed"], free(e, 2))
                        nc.vector.tensor_tensor(new[q % 2][:, :], psS[q % 2][:, 0:H], g_new[:, :],
                                                ALU.mult).then_inc(s["new"], 1)
                        dve.wait_ge(s["new"], ready(e))
                        dve.wait_ge(s["old"], ready(e))
                        nc.vector.tensor_tensor(at(shifted, 4 * (q ^ 1) + n), new[q % 2][:, :], old[q % 2][:, :],
                                                ALU.add).then_inc(s["mixed"], 1)


def layer1_scan(core, gamma, beta, kv, time_decay, time_first, shifted, states):
    nc = core.nc
    with ExitStack() as ctx:
        sb, ps = scratch(nc, ctx)
        w = sb("a1_wkv", [P, KH, 2 * NS])
        gam, bet = sb("a1_gamma", [P, H]), sb("a1_beta", [P, H])
        dec, first = sb("a1_dec", [P, 1]), sb("a1_first", [P, 1])
        decays = sb("a1_decays", [P, S])
        sig, gain = sb("a1_sig", [P, CH]), sb("a1_gain", [P, CH])
        wkv = sb("a1_wkvs", [P, S])
        psT = [ps(f"a1_kT{q}", [P, CH]) for q in range(2)]
        psK, psV = ps("a1_pK", [P, CH]), ps("a1_pV", [P, CH])
        s = core.sems("a1k", "weights exps ready scaled gained pk sig gain wkv scan")
        front = Front(core, "a1k", sb, psT, shifted, lambda act, c: act.wait_ge(s["pk"], ready(c - 2)))

        def fetch(sp):
                for dst, src in ((w[:, :, :], kv), (gam[:, :], gamma), (bet[:, :], beta), (dec[:, :], time_decay),
                                 (first[:, :], time_first)):
                    sp.dma_start(dst, src).then_inc(s["weights"], 16)
        norm_stats(core, "n1s", shifted, fetch=fetch)

        with nc.Block() as block:
            @block.scalar
            def _(act):
                front.open(act, "xt")
                open_sems(act, s["sig"], s["gain"])
                act.wait_ge(s["weights"], 80)
                nc.scalar.activation(dec[:, :], dec[:, :], ACT.Exp).then_inc(s["exps"], 1)
                nc.scalar.activation(first[:, :], first[:, :], ACT.Exp).then_inc(s["exps"], 1)
                act.wait_ge(s["ready"], 2)
                with act.Fori(0, 2) as cc:
                    for b in range(B):
                        front.scalar(act, 2 * cc + b, b)
                    act.wait_ge(s["pk"], ready(2 * cc + 1))
                    nc.scalar.activation(sig[:, :], psK[:, :], ACT.Sigmoid).then_inc(s["sig"], 1)
                    act.wait_ge(s["sig"], ready(cc))
                    act.wait_ge(s["wkv"], free(cc, 1))
                    nc.scalar.activation(gain[:, :], sig[:, :], ACT.Exp, scale=first[:, 0:1]).then_inc(s["gain"], 1)

            @block.tensor
            def _(pe):
                front.open(pe, "turned")
                open_sems(pe, s["pk"])
                pe.wait_ge(s["weights"], 80)
                with pe.Fori(0, 2) as cc:
                    for b in range(B):
                        c = 2 * cc + b
                        front.tensor(pe, c)
                        pe.wait_ge(front.s["xt"], ready(SUB * c + SUB - 1))
                        if b == 0:
                            pe.wait_ge(s["wkv"], free(cc, 1))
                        for i, dst in ((0, psK), (1, psV)):
                            for k in range(KH):
                                ins = nc.tensor.matmul(dst[NS * b:NS * (b + 1), :], w[:, k, NS * i:NS * (i + 1)],
                                                       front.xt[b][:, k, :], start=k == 0, stop=k == KH - 1)
                        ins.then_inc(s["pk"], 1)

            @block.gpsimd
            def _(pool):
                front.open(pool, "xn")
                open_sems(pool, s["gained"])
                pool.wait_ge(s["weights"], 80)
                with pool.Fori(0, 2) as cc:
                    for q in range(B * SUB):
                        t = B * SUB * cc + q
                        pool.wait_ge(s["scaled"], ready(t))
                        nc.gpsimd.tensor_tensor(front.xn[q % 4][:, :], front.xn[q % 4][:, :], gam[:, :],
                                                ALU.mult).then_inc(s["gained"], 1)
                        pool.wait_ge(s["gained"], ready(t))
                        nc.gpsimd.tensor_tensor(front.xn[q % 4][:, :], front.xn[q % 4][:, :], bet[:, :],
                                                ALU.add).then_inc(front.s["xn"], 1)

            @block.vector
            def _(dve):
                open_sems(dve, s["scaled"], s["wkv"])
                nc.vector.memset(decays[:, :], 1.0).then_inc(s["scan"], 1)
                dve.wait_ge(s["exps"], 2)
                dve.wait_ge(s["scan"], 1)
                nc.vector.tensor_scalar(decays[:, :], decays[:, :], dec[:, 0:1], None, ALU.mult).then_inc(s["ready"], 1)
                nc.vector.tensor_scalar(first[:, :], first[:, :], -1.0, None, ALU.mult).then_inc(s["ready"], 1)
                with dve.Fori(0, 2) as cc:
                    for b in range(B):
                        front.vector(dve, 2 * cc + b, 2 * b + cc, s["scaled"])
                    dve.wait_ge(s["gain"], ready(cc))
                    nc.vector.tensor_tensor(wkv[:, bass.ds(CH * cc, CH)], psV[:, :], gain[:, :],
                                            ALU.mult).then_inc(s["wkv"], 1)
                dve.wait_ge(s["wkv"], ready(1))
                dve.wait_ge(s["ready"], 2)
                nc.vector.tensor_tensor_scan(states[:, :], decays[:, :], wkv[:, :], 0.0, ALU.mult,
                                             ALU.add).then_inc(s["scan"], 1)


def layer1_out(core, w_out, states):
    nc, x = core.nc, core.x
    with ExitStack() as ctx:
        sb, ps = scratch(nc, ctx)
        w = sb("a1_wo", [P, H])
        psO = [ps(f"a1_pO{q}", [P, CH]) for q in range(4)]
        s = core.sems("a1o", "weights po added")

        with nc.Block() as block:
            @block.sync
            def _(sp):
                sp.dma_start(w[:, :], w_out).then_inc(s["weights"], 16)

            @block.tensor
            def _(pe):
                open_sems(pe, s["po"])
                pe.wait_ge(s["weights"], 16)
                for t in range(NT):
                    b, j = divmod(t, KT)
                    pe.wait_ge(s["added"], free(t, 4))
                    nc.tensor.matmul(psO[t % 4][:, 0:H], states[NS * b:NS * (b + 1), j * P:(j + 1) * P],
                                     w[NS * b:NS * (b + 1), :], start=True, stop=True).then_inc(s["po"], 1)

            @block.vector
            def _(dve):
                open_sems(dve, s["added"])
                with dve.Fori(0, NT // 4) as m:
                    for r in range(4):
                        t = 4 * m + r
                        dve.wait_ge(s["po"], ready(t))
                        nc.vector.tensor_tensor(at(x, t), at(x, t), psO[r][:, 0:H], ALU.add).then_inc(s["added"], 1)



SPLITS = {"q": ((0, 3, 0, False), (3, 2, 0, False), (5, 1, 0, False)),
          "k": ((0, 3, 0, True), (3, 2, 1, True), (5, 1, 2, True))}


def softmax_attention(core, name, w_qkv, w_out, rope):
    with ExitStack() as ctx:
        sb, _ = scratch(core.nc, ctx)
        v = sb(f"{name}_v", [P, BH, KT, VD])
        attention_project(core, name, w_qkv, rope, v)
        mixed = sb(f"{name}_mixed", [P, BH // 4, KT * 4 * D])
        attention_heads(core, name, v, mixed)
        attention_out(core, name, w_out, mixed)


def attention_project(core, name, w_qkv, rope, v):
    nc, x = core.nc, core.x
    stage = name + "p"
    with ExitStack() as ctx:
        sb, ps = scratch(nc, ctx)
        w = sb(f"{stage}_w", [P, KH, 5 if rope else 3, H])
        parts = [sb(f"{stage}_parts{i}", [P, 3, CH], BF16) for i in range(4)]
        rest = [sb(f"{stage}_rest{i}", [P, CH]) for i in range(2)]
        psT = [ps(f"{stage}_pT{i}", [P, CH]) for i in range(2)]
        psV = [ps(f"{stage}_pV{i}", [P, CH]) for i in range(2)]
        psJ = [ps(f"{stage}_pJ{i}", [P, CH]) for i in range(2)]
        if rope:
            psW = [ps(f"{stage}_pW{i}", [P, CH]) for i in range(2)]
            cos, sin = sb(f"{stage}_cos", [P, S]), sb(f"{stage}_sin", [P, S])
            turn_a = [sb(f"{stage}_ta{i}", [P, CH]) for i in range(2)]
            turn_b = [sb(f"{stage}_tb{i}", [P, CH]) for i in range(2)]
        s = core.sems(stage, "weights ones pj turns roped first rest second third pv v")
        written = [core.sem(f"{stage}_written{i}") for i in range(4)]
        front = Front(core, stage, sb, psT, x, lambda act, c: act.wait_ge(s["pv"], ready(SUB * (c - 2) + SUB - 1)))
        n_weights = 48 if rope else 16
        UNITS = (("q", 0), ("q", 1), ("k", 0), ("k", 1))
        U = len(UNITS)

        def fetch(sp):
            sp.dma_start(w[:, :, :, :], w_qkv).then_inc(s["weights"], 16)
            if rope:
                sp.dma_start(cos[:, :], rope[0]).then_inc(s["weights"], 16)
                sp.dma_start(sin[:, :], rope[1]).then_inc(s["weights"], 16)
        norm_stats(core, name + "n", x, fetch=fetch)

        with nc.Block() as block:
            @block.sync
            def _(sp):
                for c in range(NC):
                    b, cc = divmod(c, 2)
                    for u, (which, half) in enumerate(UNITS):
                        sp.wait_ge(s["third"], ready(U * c + u))
                        dram = core.stack[which]
                        for seg, count, part, same in SPLITS[which]:
                            src = parts[u][:, part:part + (1 if same else count), :]
                            if same and count > 1:
                                src = src.broadcast_to([P, count, CH])
                            dst = dram[b * H + half * P:b * H + (half + 1) * P, seg:seg + count, cc * CH:(cc + 1) * CH]
                            sp.dma_start(dst, src).then_inc(written[u], 16)
                for u in range(U):
                    sp.wait_ge(written[u], 48 * NC)

            @block.tensor
            def _(pe):
                front.open(pe, "turned")
                open_sems(pe, s["pj"], s["pv"])
                pe.wait_ge(s["weights"], n_weights)

                def value(t):
                    pe.wait_ge(s["v"], free(t, 2))
                    for k in range(KH):
                        ins = nc.tensor.matmul(psV[t % 2][:, 0:H],
                                               front.xt[t // SUB % 2][:, k, t % SUB * P:(t % SUB + 1) * P],
                                               w[:, k, 2, :], start=k == 0, stop=k == KH - 1)
                    ins.then_inc(s["pv"], 1)
                front.tensor(pe, 0)
                for c in range(NC):
                    pe.wait_ge(front.s["xt"], ready(SUB * c + SUB - 1))
                    for u, (which, half) in enumerate(UNITS):
                        e = U * c + u
                        pe.wait_ge(s["turns" if rope else "rest"], free(e, 2))
                        i = "qk".index(which)
                        for dst, j in ((psJ[u % 2], i), (psW[u % 2] if rope else None, 3 + i)):
                            if dst is not None:
                                for k in range(KH):
                                    ins = nc.tensor.matmul(dst[:, :], w[:, k, j, half * P:(half + 1) * P],
                                                           front.xt[c % 2][:, k, :], start=k == 0, stop=k == KH - 1)
                        ins.then_inc(s["pj"], 1)
                        value(SUB * c + u)
                        if u == 2 and c < NC - 1:
                            front.tensor(pe, c + 1)

            @block.scalar
            def _(act):
                front.open(act, "xt")
                open_sems(act, s["first"], s["second"])
                front.scalar(act, 0, 0)
                for c in range(NC):
                    for u in range(U):
                        e = U * c + u
                        value = turn_a[u % 2][:, :] if rope else psJ[u % 2][:, :]
                        act.wait_ge(s["roped" if rope else "pj"], ready(e))
                        if c:
                            act.wait_ge(written[u], 48 * c)
                        nc.scalar.activation(parts[u][:, 0, :], value, ACT.Copy).then_inc(s["first"], 1)
                        act.wait_ge(s["rest"], ready(e))
                        nc.scalar.activation(parts[u][:, 1, :], rest[u % 2][:, :],
                                             ACT.Copy).then_inc(s["second"], 1)
                        if u == 1 and c < NC - 1:
                            front.scalar(act, c + 1, (c + 1) % 2)

            @block.gpsimd
            def _(pool):
                open_sems(pool, s["third"], s["roped"])

                def turn(e):
                    if rope and e < U * NC:
                        pool.wait_ge(s["turns"], ready(e))
                        nc.gpsimd.tensor_tensor(turn_a[e % 2][:, :], turn_a[e % 2][:, :], turn_b[e % 2][:, :],
                                                ALU.add).then_inc(s["roped"], 1)
                turn(0)
                for e in range(U * NC):
                    u = e % U
                    turn(e + 1)
                    pool.wait_ge(s["second"], ready(e))
                    nc.gpsimd.tensor_tensor(parts[u][:, 2, :], rest[u % 2][:, :], parts[u][:, 1, :],
                                            ALU.subtract).then_inc(s["third"], 1)

            @block.vector
            def _(dve):
                front.open(dve, "xn")
                open_sems(dve, s["rest"], s["turns"], s["v"])
                nc.vector.memset(v[:, :, :, D:VD], 1.0).then_inc(s["ones"], 1)
                dve.wait_ge(s["weights"], n_weights)

                def turn(e):
                    u = e % U
                    dve.wait_ge(s["pj"], ready(e))
                    dve.wait_ge(s["rest"], free(e, 2))
                    pos = slice(e // U % 2 * CH, (e // U % 2 + 1) * CH)
                    nc.vector.tensor_tensor(turn_b[u % 2][:, :], psW[u % 2][:, :], sin[:, pos], ALU.mult)
                    nc.vector.tensor_tensor(turn_a[u % 2][:, :], psJ[u % 2][:, :], cos[:, pos],
                                            ALU.mult).then_inc(s["turns"], 1)
                front.vector(dve, 0)
                if rope:
                    turn(0)
                for c in range(NC):
                    if c < NC - 1:
                        front.vector(dve, c + 1)
                    for u in range(U):
                        e = U * c + u
                        if rope and e + 1 < U * NC:
                            turn(e + 1)
                        dve.wait_ge(s["first"], ready(e))
                        dve.wait_ge(s["third"], free(e, 2))
                        nc.vector.tensor_tensor(rest[u % 2][:, :], turn_a[u % 2][:, :] if rope else psJ[u % 2][:, :],
                                                parts[u][:, 0, :], ALU.subtract).then_inc(s["rest"], 1)
                        t = SUB * c + u
                        b, tile = divmod(t, KT)
                        dve.wait_ge(s["pv"], ready(t))
                        nc.vector.tensor_copy(v[:, b * HEADS:(b + 1) * HEADS, tile, 0:D],
                                              psV[t % 2][:, 0:H].rearrange("p (h d) -> p h d", d=D)).then_inc(s["v"], 1)


def attention_heads(core, name, v, mixed):
    nc = core.nc
    stage = name + "h"
    GROUPS = BH // 4
    HALF = CH // P
    PIECES = [(0, 0), (0, 1), (0, 2), (0, 3), (1, 0), (1, 5), (1, 6), (1, 7), (1, 4), (1, 1), (1, 2), (1, 3)]
    NP = len(PIECES)
    last_of = [HALF - 1, NP - 1]
    TURNS = list(range(10)) + ["maximum 0", "maximum 1"] + [10, 11]
    NU = len(TURNS)
    PROBS = 6
    MAXIMA = list(range(KT))[::-1]
    MAXIMA_AT = {0: (0, 1), 1: (2,), 2: (3,), 3: (4,), 4: (5, 6), 5: (7,)}
    OUTPUTS_AT = 8
    with ExitStack() as ctx:
        sb, ps = scratch(nc, ctx)
        R3 = ROWS + 3
        q_rows = [sb(f"{stage}_q{i}", [R3, S], BF16) for i in range(4)]
        k_rows = [sb(f"{stage}_k{i}", [R3, S], BF16) for i in range(4)]
        neg = sb(f"{stage}_neg", [P, KT])
        left = sb(f"{stage}_left", [P, KT])
        neg3 = [sb(f"{stage}_neg3{i}", [P, KT, 3], BF16) for i in range(2)]
        probs = [sb(f"{stage}_probs{i}", [P, CH]) for i in range(PROBS)]
        values = [sb(f"{stage}_values{i}", [P, KT, VD]) for i in range(4)]
        turned = sb(f"{stage}_turned", [P, S])
        rden = sb(f"{stage}_rden", [P, HALF, 4])
        psM = [ps(f"{stage}_pM{i}", [P, S]) for i in range(2)]
        psX = [ps(f"{stage}_pX{i}", [P, CH]) for i in range(2)]
        psV = [ps(f"{stage}_pV{i}", [P, CH]) for i in range(2)]
        s = core.sems(stage, "ones clear pm max split neg3 px ex values pv copied rden")
        loaded = [core.sem(f"{stage}_loaded{i}") for i in range(4)]

        def groups(eng, body):
            body(0)
            with eng.Fori(1, GROUPS - 1) as g:
                body(g)
            body(GROUPS - 1)

        def final(t):
            return isinstance(t, int) and t == BH - 1

        def turns(t):
            return [j for j in range(NU) if not (final(t) and isinstance(TURNS[j], str))]

        def bank_use(t, j):
            n = 2 + NU * t + j
            return n - 2 if final(t) and j > TURNS.index("maximum 1") else n

        def rows_use(g, r, i):
            if isinstance(g, int) and g == r == 0:
                return i
            return bank_use(4 * g + r - 1, TURNS.index("maximum 0") + i)

        def maximum_use(g, r, p):
            return KT + (34 * g + KT * r + p) - (2 if r == 0 and not (isinstance(g, int) and g == 0) else 0)

        def output_use(g, c):
            if isinstance(g, int) and g == GROUPS - 1:
                return KT + 34 * g + 3 * KT + c
            return KT + 34 * (g + 1) + KT - 2 + c

        with nc.Block() as block:
            @block.sync
            def _(sp):
                def fetch(t, r):
                    for which, dst in (("q", q_rows[r]), ("k", k_rows[r])):
                        sp.dma_start(dst[0:ROWS, :], core.stack_rows[which][bass.ds(t * ROWS, ROWS), :]
                                     ).then_inc(loaded[r], 16)
                for r in range(4):
                    fetch(r, r)
                core.start_loads(sp)
                with sp.Fori(1, GROUPS) as g:
                    for r in range(4):
                        sp.wait_ge(s["pv"], ready(NP * (4 * g + r - 4) + NP - 1))
                        fetch(4 * g + r, r)

            @block.gpsimd
            def _(pool):
                open_sems(pool, s["values"])

                def take(g):
                    for r in range(4):
                        t = 4 * g + r
                        if not (isinstance(g, int) and g == 0):
                            pool.wait_ge(s["pv"], ready(NP * (t - 4) + NP - 1))
                            settle(pool)
                        nc.gpsimd.tensor_copy(flat(values[r][:, :, :]), v[:, bass.ds(t, 1), :, :].rearrange(
                            "p a k d -> p (a k d)")).then_inc(s["values"], 1)
                groups(pool, take)

            @block.tensor
            def _(pe):
                open_sems(pe, s["pm"], s["px"], s["pv"])
                pe.wait_ge(s["ones"], 4)

                def maximum(g, slot, use, p):
                    u = MAXIMA[p]
                    if p == 0:
                        pe.wait_ge(loaded[slot], 32 * (g + 1))
                    pe.wait_ge(s["max"], free(use, 2))
                    n = (u + 1) * P
                    for a in range(0, n, CH):
                        b = min(a + CH, n)
                        nc.tensor.matmul(psM[p % 2][:, a:b], q_rows[slot][0:ROWS, u * P:(u + 1) * P],
                                         k_rows[slot][0:ROWS, a:b], start=True, stop=b < n)
                    nc.tensor.matmul(psM[p % 2][:, u * P:n], core.identb[:, :], core.mask_q[:, :],
                                     start=False, stop=True).then_inc(s["pm"], 1)

                def maximum_rows(g, r, i):
                    use = rows_use(g, r, i)
                    if i == 0:
                        pe.wait_ge(s["neg3"], ready(4 * g + r))
                    pe.wait_ge(s["ex"], free(use, 2))
                    for j in range(HALF):
                        ins = nc.tensor.matmul(psX[i][ROWS:R3, j * P:(j + 1) * P], neg3[r % 2][:, i * HALF + j, :],
                                               core.identb[:, :], start=True, stop=True)
                    ins.then_inc(s["px"], 1)

                def scores(t, slot, j):
                    c, kt = PIECES[TURNS[j]]
                    off = max(0, kt * P - c * CH)
                    pe.wait_ge(s["ex"], free(bank_use(t, j), 2))
                    diag = kt * P >= c * CH
                    ins = nc.tensor.matmul(psX[j % 2][:, off:CH], k_rows[slot][0:R3, kt * P:(kt + 1) * P],
                                           q_rows[slot][0:R3, c * CH + off:(c + 1) * CH], start=True, stop=not diag)
                    if diag:
                        ins = nc.tensor.matmul(psX[j % 2][:, off:off + P], core.identb[:, :], core.mask_k[:, :],
                                               start=False, stop=True)
                    ins.then_inc(s["px"], 1)

                def weighted(g, r, j):
                    t, i = 4 * g + r, TURNS[j]
                    c, kt = PIECES[i]
                    off = max(0, kt * P - c * CH)
                    if i == 0:
                        pe.wait_ge(s["values"], ready(t))
                    if r == 0 and kt == 0:
                        if isinstance(g, int) and g == 0:
                            pe.wait_ge(s["clear"], 2)
                        else:
                            pe.wait_ge(s["copied"], ready(2 * (g - 1) + c))
                    pe.wait_ge(s["ex"], ready(bank_use(t, j)))
                    nc.tensor.matmul(psV[c][32 * r:32 * r + VD, off:CH], values[r][:, kt, :],
                                     probs[i % PROBS][:, off:CH], start=kt == 0, stop=i == last_of[c]).then_inc(s["pv"], 1)

                def outputs(g):
                    for c in range(2):
                        pe.wait_ge(s["copied"], ready(2 * g + c))
                        pe.wait_ge(s["max"], free(output_use(g, c), 2))
                        for j in range(HALF):
                            ins = nc.tensor.transpose(psM[c][:, j * P:(j + 1) * P],
                                                      turned[:, (c * HALF + j) * P:(c * HALF + j + 1) * P], core.ident[:, :])
                        ins.then_inc(s["pm"], 1)

                def head(g, r):
                    t = 4 * g + r
                    order = turns(t)
                    for n, j in enumerate(order):
                        if n + 2 < len(order):
                            ahead = order[n + 2]
                            if isinstance(TURNS[ahead], int):
                                scores(t, r, ahead)
                            else:
                                maximum_rows(g if r < 3 else g + 1, (r + 1) % 4, ahead - TURNS.index("maximum 0"))
                        elif not final(t):
                            scores(t + 1, (r + 1) % 4, n + 2 - NU)
                        if not final(t):
                            for p in MAXIMA_AT.get(n, ()):
                                maximum(g if r < 3 else g + 1, (r + 1) % 4, maximum_use(g, r, p), p)
                        if isinstance(TURNS[j], int):
                            weighted(g, r, j)
                        if n == OUTPUTS_AT and r == 0 and not (isinstance(g, int) and g == 0):
                            outputs(g - 1)

                for p in range(KT):
                    maximum(0, 0, p, p)
                for i in range(2):
                    maximum_rows(0, 0, i)
                pe.wait_ge(s["ex"], ready(1))
                scores(0, 0, 0)
                scores(0, 0, 1)

                def body(g):
                    for r in range(4):
                        head(g, r)
                groups(pe, body)
                outputs(GROUPS - 1)

            @block.scalar
            def _(act):
                open_sems(act, s["ex"], s["copied"])
                nc.scalar.preload_act_table(ACT.Exp)

                def rows(g, r, i):
                    act.wait_ge(s["px"], ready(rows_use(g, r, i)))
                    nc.scalar.activation(q_rows[r][ROWS:R3, i * CH:(i + 1) * CH], psX[i % 2][ROWS:R3, :],
                                         ACT.Copy).then_inc(s["ex"], 1)

                def copy(g, c):
                    act.wait_ge(s["pv"], ready(NP * (4 * g + 3) + last_of[c]))
                    if not (isinstance(g, int) and g == 0):
                        act.wait_ge(s["max"], ready(output_use(g - 1, c)))
                    nc.scalar.activation(turned[:, c * CH:(c + 1) * CH], psV[c][:, :], ACT.Copy).then_inc(s["copied"], 1)

                def body(g):
                    for r in range(4):
                        t = 4 * g + r
                        for j in turns(t):
                            if isinstance(TURNS[j], str):
                                rows(g if r < 3 else g + 1, (r + 1) % 4, j - TURNS.index("maximum 0"))
                                continue
                            i = TURNS[j]
                            c, kt = PIECES[i]
                            off = max(0, kt * P - c * CH)
                            act.wait_ge(s["px"], ready(bank_use(t, j)))
                            act.wait_ge(s["pv"], free(NP * t + i, PROBS))
                            nc.scalar.activation(probs[i % PROBS][:, off:CH], psX[j % 2][:, off:CH], ACT.Exp,
                                                 scale=float(D) ** -0.5).then_inc(s["ex"], 1)
                            if r == 3 and i == HALF + 2:
                                copy(g, 0)
                            if r == 0 and i == 1 and not (isinstance(g, int) and g == 0):
                                copy(g - 1, 1)
                for i in range(2):
                    rows(0, 0, i)
                groups(act, body)
                copy(GROUPS - 1, 1)

            @block.vector
            def _(dve):
                open_sems(dve, *(s[n] for n in ("max", "split", "neg3", "rden")))
                for i in range(4):
                    nc.vector.memset(k_rows[i][ROWS:R3, :], 1.0).then_inc(s["ones"], 1)
                for c in range(2):
                    nc.vector.memset(psV[c][:, :], 0.0).then_inc(s["clear"], 1)

                def maxima(t, use, r):
                    for p, u in enumerate(MAXIMA):
                        dve.wait_ge(s["pm"], ready(use(p)))
                        nc.vector.tensor_reduce(neg[:, u:u + 1], psM[p % 2][:, 0:(u + 1) * P], AX.X, ALU.max,
                                                negate=True).then_inc(s["max"], 1)
                    dve.wait_ge(s["max"], ready(use(KT - 1)))
                    parts = neg3[r % 2]
                    nc.vector.tensor_copy(parts[:, :, 0], neg[:, :]).then_inc(s["split"], 1)
                    dve.wait_ge(s["split"], ready(3 * t))
                    nc.vector.tensor_tensor(left[:, :], neg[:, :], parts[:, :, 0], ALU.subtract).then_inc(s["split"], 1)
                    dve.wait_ge(s["split"], ready(3 * t + 1))
                    nc.vector.tensor_copy(parts[:, :, 1], left[:, :]).then_inc(s["split"], 1)
                    dve.wait_ge(s["split"], ready(3 * t + 2))
                    nc.vector.tensor_tensor(parts[:, :, 2], left[:, :], parts[:, :, 1],
                                            ALU.subtract).then_inc(s["neg3"], 1)
                    dve.wait_ge(s["neg3"], ready(t))

                def divide(g):
                    for c in range(2):
                        dve.wait_ge(s["pm"], ready(output_use(g, c)))
                        if c:
                            dve.wait_ge(s["max"], ready(output_use(g, 0)))
                        elif not (isinstance(g, int) and g == 0):
                            dve.wait_ge(s["max"], ready(output_use(g - 1, 1)))
                        out = psM[c][:, 0:CH].rearrange("p (q r w) -> p q r w", q=HALF, r=4)
                        nc.vector.reciprocal(rden[:, :, :], out[:, :, :, D]).then_inc(s["rden"], 1)
                        dve.wait_ge(s["rden"], ready(2 * g + c))
                        dst = at(mixed, g)[:, c * HALF * 4 * D:(c + 1) * HALF * 4 * D].rearrange(
                            "p (q r d) -> p q r d", q=HALF, r=4)
                        nc.vector.tensor_tensor(dst, out[:, :, :, 0:D],
                                                rden[:, :, :].unsqueeze(3).broadcast_to([P, HALF, 4, D]),
                                                ALU.mult).then_inc(s["max"], 1)

                def body(g):
                    for r in range(4):
                        if not final(4 * g + r):
                            maxima(4 * g + r + 1, lambda p: maximum_use(g, r, p), (r + 1) % 4)
                        if r == 0 and not (isinstance(g, int) and g == 0):
                            divide(g - 1)
                maxima(0, lambda p: p, 0)
                groups(dve, body)
                divide(GROUPS - 1)


def attention_out(core, name, w_out, mixed):
    nc, x = core.nc, core.x
    stage = name + "o"
    with ExitStack() as ctx:
        sb, ps = scratch(nc, ctx)
        w = sb(f"{stage}_w", [P, KH, H])
        row = [sb(f"{stage}_row{i}", [P, H]) for i in range(4)]
        xt = [sb(f"{stage}_xt{i}", [P, KH, P]) for i in range(2)]
        psT = [ps(f"{stage}_pT{i}", [P, CH]) for i in range(2)]
        psO = [ps(f"{stage}_pO{i}", [P, CH]) for i in range(2)]
        s = core.sems(stage, "weights row turned xt po added")
        groups = HEADS // 4

        with nc.Block() as block:
            @block.sync
            def _(sp):
                sp.dma_start(w[:, :, :], w_out).then_inc(s["weights"], 16)

            @block.gpsimd
            def _(pool):
                open_sems(pool, s["row"])
                with pool.Fori(0, B) as b:
                    for q in range(KT):
                        pool.wait_ge(s["turned"], free(KT * b + q, 4))
                        settle(pool)
                        src = mixed[:, bass.ds(b * groups, groups), q * 4 * D:(q + 1) * 4 * D]
                        nc.gpsimd.tensor_copy(row[q % 4][:, :].rearrange("p (g c) -> p g c", g=groups),
                                              src).then_inc(s["row"], 1)

            @block.tensor
            def _(pe):
                open_sems(pe, s["turned"], s["po"])
                pe.wait_ge(s["weights"], 16)

                def product(t, q):
                    pe.wait_ge(s["xt"], ready(t))
                    pe.wait_ge(s["added"], free(t, 2))
                    for k in range(KH):
                        ins = nc.tensor.matmul(psO[q % 2][:, 0:H], xt[q % 2][:, k, :], w[:, k, :],
                                               start=k == 0, stop=k == KH - 1)
                    ins.then_inc(s["po"], 1)
                with pe.Fori(0, B) as b:
                    for q in range(KT):
                        t = KT * b + q
                        pe.wait_ge(s["row"], ready(t))
                        pe.wait_ge(s["xt"], free(t, 2))
                        for k in range(KH):
                            ins = nc.tensor.transpose(psT[q % 2][:, k * P:(k + 1) * P], row[q % 4][:, k * P:(k + 1) * P],
                                                      core.ident[:, :])
                        ins.then_inc(s["turned"], 1)
                        if q:
                            product(t - 1, q - 1)
                    product(KT * b + KT - 1, KT - 1)

            @block.scalar
            def _(act):
                open_sems(act, s["xt"])
                with act.Fori(0, B) as b:
                    for q in range(KT):
                        t = KT * b + q
                        act.wait_ge(s["turned"], ready(t))
                        act.wait_ge(s["po"], free(t, 2))
                        nc.scalar.activation(flat(xt[q % 2][:, :, :]), psT[q % 2][:, 0:H], ACT.Copy).then_inc(s["xt"], 1)

            @block.vector
            def _(dve):
                open_sems(dve, s["added"])
                with dve.Fori(0, B) as b:
                    for q in range(KT):
                        t = KT * b + q
                        dve.wait_ge(s["po"], ready(t))
                        nc.vector.tensor_tensor(at(x, t), at(x, t), psO[q % 2][:, 0:H], ALU.add).then_inc(s["added"], 1)



def last_ffn(core, w_gu, w_down, w_down_last, scales, down_scale):
    nc, x = core.nc, core.x
    with ExitStack() as ctx:
        sb, ps = scratch(nc, ctx)
        NI = -(-FI // P)
        width = [min(P, FI - i * P) for i in range(NI)]
        w = sb("f_wgu", [P, KH, 2 * FI])
        wd = sb("f_wd", [P, NI, H])
        sc = {n: sb(f"f_{n}", [P, NI]) for n in ("gs", "us")}
        ds = sb("f_ds", [P, H])
        act_g = [sb(f"f_act{i}", [P, CH]) for i in range(2)]
        hid = [sb(f"f_hid{i}", [P, NI, CH]) for i in range(2)]
        res = [sb(f"f_res{i}", [P, H]) for i in range(2)]
        psT = [ps(f"f_pT{i}", [P, CH]) for i in range(2)]
        psG = [ps(f"f_pG{i}", [P, CH]) for i in range(2)]
        psU = [ps(f"f_pU{i}", [P, CH]) for i in range(2)]
        psO = [ps(f"f_pO{i}", [P, CH]) for i in range(2)]
        s = core.sems("f", "weights pu act hid po res added")
        front = Front(core, "f", sb, psT, x, lambda act, c: act.wait_ge(s["pu"], ready(NI * (c - 1) - 1)))

        def fetch(sp):
            last = width[-1]
            loads = [(w[:, :, :], w_gu), (wd[:, 0:NI - 1, :], w_down), (wd[0:last, NI - 1, :], w_down_last),
                     (ds[:, :], down_scale)]
            for n in ("gs", "us"):
                loads += [(sc[n][:, 0:NI - 1], scales[n][0]), (sc[n][0:last, NI - 1:NI], scales[n][1])]
            for dst, src in loads:
                sp.dma_start(dst, src).then_inc(s["weights"], 16)
        norm_stats(core, "fn", x, fetch=fetch)

        with nc.Block() as block:
            @block.tensor
            def _(pe):
                front.open(pe, "turned")
                open_sems(pe, s["pu"], s["po"])
                pe.wait_ge(s["weights"], 8 * 16)

                def products(c):
                    pe.wait_ge(front.s["xt"], ready(SUB * c + SUB - 1))
                    for i in range(NI):
                        pe.wait_ge(s["hid"], free(NI * c + i, 2))
                        for dst, base in ((psG[i % 2], 0), (psU[i % 2], FI)):
                            for k in range(KH):
                                ins = nc.tensor.matmul(dst[0:width[i], :],
                                                       w[:, k, base + i * P:base + i * P + width[i]],
                                                       front.xt[c % 2][:, k, :], start=k == 0, stop=k == KH - 1)
                        ins.then_inc(s["pu"], 1)

                def outputs(c):
                    pe.wait_ge(s["hid"], ready(NI * c + NI - 1))
                    for sub in range(SUB):
                        pe.wait_ge(s["res"], free(SUB * c + sub, 2))
                        for i in range(NI):
                            ins = nc.tensor.matmul(psO[sub % 2][:, 0:H],
                                                   hid[c % 2][0:width[i], i, sub * P:(sub + 1) * P],
                                                   wd[0:width[i], i, :], start=i == 0, stop=i == NI - 1)
                        ins.then_inc(s["po"], 1)
                front.tensor(pe, 0)
                for c in range(NC):
                    products(c)
                    if c < NC - 1:
                        front.tensor(pe, c + 1)
                    if c:
                        outputs(c - 1)
                outputs(NC - 1)

            @block.scalar
            def _(act):
                front.open(act, "xt")
                open_sems(act, s["act"])
                nc.scalar.preload_act_table(ACT.Silu)
                act.wait_ge(s["weights"], 8 * 16)
                front.scalar(act, 0, 0)
                for c in range(NC):
                    for i in range(NI):
                        act.wait_ge(s["pu"], ready(NI * c + i))
                        act.wait_ge(s["hid"], free(NI * c + i, 2))
                        nc.scalar.activation(act_g[i % 2][0:width[i], :], psG[i % 2][0:width[i], :], ACT.Silu,
                                             scale=sc["gs"][0:width[i], i:i + 1]).then_inc(s["act"], 1)
                    if c < NC - 1:
                        front.scalar(act, c + 1, (c + 1) % 2)

            @block.vector
            def _(dve):
                front.open(dve, "xn")
                open_sems(dve, s["hid"], s["res"], s["added"])
                dve.wait_ge(s["weights"], 8 * 16)

                def add(c):
                    for sub in range(SUB):
                        t = SUB * c + sub
                        dve.wait_ge(s["po"], ready(t))
                        dve.wait_ge(s["added"], free(t, 2))
                        nc.vector.tensor_tensor(res[sub % 2][:, :], psO[sub % 2][:, 0:H], ds[:, :],
                                                ALU.mult).then_inc(s["res"], 1)
                        dve.wait_ge(s["res"], ready(t))
                        nc.vector.tensor_tensor(at(x, t), at(x, t), res[sub % 2][:, :],
                                                ALU.add).then_inc(s["added"], 1)
                front.vector(dve, 0)
                for c in range(NC):
                    if c < NC - 1:
                        front.vector(dve, c + 1)
                    if c > 1:
                        dve.wait_ge(s["po"], ready(SUB * (c - 2) + SUB - 1))
                    for i in range(NI):
                        dve.wait_ge(s["act"], ready(NI * c + i))
                        nc.vector.scalar_tensor_tensor(hid[c % 2][0:width[i], i, :], psU[i % 2][0:width[i], :],
                                                       sc["us"][0:width[i], i:i + 1], act_g[i % 2][0:width[i], :],
                                                       ALU.mult, ALU.mult).then_inc(s["hid"], 1)
                    if c:
                        add(c - 1)
                add(NC - 1)



def constants(core, x_in, x_loaded):
    nc = core.nc
    s = core.sems("const", "iota chain")
    with nc.Block() as block:
        @block.sync
        def _(sp):
            sp.dma_start(core.x[:, :, :], x_in).then_inc(x_loaded, 16)
            sp.wait_ge(x_loaded, 16)

        @block.gpsimd
        def _(pool):
            nc.gpsimd.iota(core.number[:, :], [[P, NT]], base=0, channel_multiplier=1,
                           allow_small_or_imprecise_dtypes=True).then_inc(s["iota"], 1)
            nc.gpsimd.iota(core.iota[:, :], [[1, P]], base=0, channel_multiplier=0,
                           allow_small_or_imprecise_dtypes=True).then_inc(s["iota"], 1)
            nc.gpsimd.iota(core.part[:, :], [[0, 1]], base=0, channel_multiplier=1,
                           allow_small_or_imprecise_dtypes=True).then_inc(s["iota"], 1)

        @block.vector
        def _(dve):
            dve.wait_ge(s["iota"], 3)
            do = Chain(dve, s["chain"])
            V, part = nc.vector, core.part[:, 0:1]
            do(V.tensor_scalar(core.ident[:, :], core.iota[:, :], part, None, ALU.is_equal))
            do(V.tensor_scalar(core.identb[:, :], core.iota[:, :], part, None, ALU.is_equal))
            do(V.tensor_copy(core.iotab[:, :], core.iota[:, :]))
            do(V.tensor_scalar(core.earlier[:, :], core.iota[:, :], part, None, ALU.is_gt))
            do(V.tensor_scalar(core.mask_q[:, :], core.iota[:, :], part, NEG, ALU.is_gt, ALU.mult))
            do(V.tensor_scalar(core.mask_k[:, :], core.iota[:, :], part, NEG, ALU.is_lt, ALU.mult))
            do(V.memset(core.onesb[:, :], 1.0))
            do(V.memset(core.onesf[:, :], 1.0))


def load(core, sem, dst, src):
    core.behind.append((dst, src, sem))


def program(nc, a, out):
    x_in = a["x"].rearrange("(t p) h -> p t h", p=P)
    x_out = out.rearrange("(t p) h -> p t h", p=P)
    with ExitStack() as ctx:
        core = Core(nc)
        sb, _ = scratch(nc, ctx)
        core.x = sb("x", [P, NT, H])
        core.rstd, core.nmr = sb("rstd", [P, NT]), sb("nmr", [P, NT])
        core.rstd1, core.rstd2, core.nmr2 = (sb(n, [P, NT]) for n in ("rstd1", "rstd2", "nmr2"))
        core.iota, core.part = sb("iota", [P, P]), sb("part", [P, 1])
        core.number = sb("number", [P, NT])
        core.ident, core.identb = sb("ident", [P, P]), sb("identb", [P, P], BF16)
        core.iotab, core.earlier = sb("iotab", [P, P], BF16), sb("earlier", [P, P], BF16)
        core.mask_q, core.mask_k = sb("mask_q", [P, P], BF16), sb("mask_k", [P, P], BF16)
        core.onesb, core.onesf = sb("onesb", [P, P], BF16), sb("onesf", [P, 32])
        big = sb("experts", [P, 32, WE])
        rows = nc.dram_tensor("rows", (T, H), F32, kind="Internal").ap()
        results = nc.dram_tensor("results", (96 * P, H), F32, kind="Internal").ap()
        core.rows_flat, core.results_flat = rows, results
        core.rows = rows.rearrange("(t p) h -> p t h", p=P)
        core.results = results.rearrange("(t p) h -> p t h", p=P)
        core.stack = {w: nc.dram_tensor(f"stack_{w}", (B * H, SEGS, S), BF16, kind="Internal").ap() for w in "qk"}
        core.stack_rows = {w: ap.rearrange("c g s -> (c g) s") for w, ap in core.stack.items()}
        x_loaded, load0, load1a, load1b, load2, stored = (core.sem(n) for n in (
            "x_loaded", "load0", "load1a", "load1b", "load2", "stored"))

        constants(core, x_in, x_loaded)

        def experts(name, E, kind, *loaded):
            m = Moe(core, name, E, kind, big)
            m.loaded = loaded
            return m

        half = 16
        load(core, load0, big[:, 0:half, :], a["m0_w"])
        load(core, load1b, big[:, half:, :], a["m1_w"][:, half:, :])
        with core.layer():
            layer0_attention(core, a["a0_wv"], a["a0_wg"], a["a0_bg"], a["a0_wq"], a["a0_bq"], a["a0_wo"])
        with core.layer():
            moe_layer(experts("m0", 16, "sigmoid", load0), a["m0_ws"], a["m0_wr"], a["m0_bias"])
        load(core, load1a, big[:, 0:half, :], a["m1_w"][:, 0:half, :])
        with core.layer():
            layer1_attention(core, a["a1_shift"], a["a1_gate"], a["a1_gamma"], a["a1_beta"], a["a1_kv"],
                         a["a1_decay"], a["a1_first"], a["a1_out"])
        with core.layer():
            moe_layer(experts("m1", 32, "softplus", load1a, load1b), a["m1_ws"], a["m1_wr"], a["m1_bias"])
        load(core, load2, big[:, :, :], a["m2_w"])
        with core.layer():
            softmax_attention(core, "a2", a["a2_w"], a["a2_out"], None)
        with core.layer():
            moe_layer(experts("m2", 32, "softmax", load2), a["m2_ws"], a["m2_wr"], None, a["m2_norm"])
        with core.layer():
            softmax_attention(core, "a3", a["a3_w"], a["a3_out"], (a["rope_cos"], a["rope_sin"]))
        with core.layer():
            last_ffn(core, a["f_gu"], a["f_down"], a["f_down_last"],
                 {n: (a[f"f_{n}"], a[f"f_{n}_last"]) for n in ("gs", "us")}, a["f_ds"])
        with nc.Block() as block:
            @block.sync
            def _(sp):
                sp.dma_start(x_out, core.x[:, :, :]).then_inc(stored, 16)
                sp.wait_ge(stored, 16)



def by_half(w):
    return w.reshape(KH, P, -1).transpose(1, 0, 2)


def wide(v):
    return np.broadcast_to(v.reshape(1, -1), (P, v.size))


def expert_rows(gate_up, down):
    e = gate_up.shape[0]
    gu = gate_up.reshape(e, KH, P, 2 * I).transpose(2, 0, 1, 3).reshape(P, e, KH * 2 * I)
    return np.concatenate([gu, down.transpose(1, 0, 2)], axis=2)


def swiglu(gate, up, down):
    return expert_rows(np.concatenate([gate, up], axis=1).transpose(0, 2, 1), down.transpose(0, 2, 1))


def heads_columns(w):
    return w.reshape(KH, P, 3, H).transpose(1, 0, 2, 3)


def rope_tables():
    inv = (1.0 / np.float32(10000.0) ** (np.arange(0, D, 2, dtype=np.float32) / np.float32(D))).astype(np.float32)
    ang = np.outer(np.arange(S, dtype=np.float32), inv).astype(np.float32)
    ang = np.concatenate([ang, ang], axis=1)
    sign = np.where(np.arange(D) % 2 == 0, -1.0, 1.0)
    return (np.tile(np.cos(ang.astype(np.float64)).T, (P // D, 1)).astype(np.float32),
            np.tile((np.sin(ang.astype(np.float64)) * sign).T, (P // D, 1)).astype(np.float32))


def layouts(i):
    a = {"x": i["L0_attn_x"].reshape(T, H)}
    for n in "vgqo":
        a[f"a0_w{n}"] = by_half(i[f"L0_attn_W{n}"])
    for n in "gq":
        a[f"a0_b{n}"] = i[f"L0_attn_b{n}"].reshape(KH, P).T
    a["m0_w"] = swiglu(i["L0_ffn_w_gate"], i["L0_ffn_w_up"], i["L0_ffn_w_down"])
    a["m0_ws"] = swiglu(i["L0_ffn_sw_gate"][None], i["L0_ffn_sw_up"][None], i["L0_ffn_sw_down"][None])[:, 0]
    a["m0_wr"] = by_half(i["L0_ffn_gate_w"].T)
    a["m0_bias"] = wide(i["L0_ffn_expert_bias"])
    a["a1_shift"] = by_half(i["L1_attn_W_shift"].T)
    a["a1_gate"] = wide(i["L1_attn_gate"])
    a["a1_gamma"] = wide(i["L1_attn_ln_gamma"])
    a["a1_beta"] = wide(i["L1_attn_ln_beta"])
    a["a1_kv"] = np.concatenate([by_half(i["L1_attn_W_key"].T), by_half(i["L1_attn_W_value"].T)], axis=2)
    a["a1_decay"] = np.tile(i["L1_attn_time_decay"].reshape(NS, 1), (B, 1))
    a["a1_first"] = np.tile(i["L1_attn_time_first"].reshape(NS, 1), (B, 1))
    a["a1_out"] = np.tile(i["L1_attn_W_output"].T, (B, 1))
    a["m1_w"] = swiglu(i["L1_ffn_gate_w"], i["L1_ffn_up_w"], i["L1_ffn_down_w"])
    a["m1_ws"] = swiglu(i["L1_ffn_shared_gate_w"][None], i["L1_ffn_shared_up_w"][None],
                        i["L1_ffn_shared_down_w"][None])[:, 0]
    a["m1_wr"] = by_half(i["L1_ffn_router_w"].T)
    a["m1_bias"] = wide(i["L1_ffn_expert_bias"])
    a["a2_w"] = heads_columns(i["L2_attn_w_qkv"])
    a["a2_out"] = by_half(i["L2_attn_w_out"])
    a["m2_w"] = expert_rows(i["L2_ffn_w13"], i["L2_ffn_w2"])
    a["m2_ws"] = expert_rows(np.concatenate([i["L2_ffn_shared_gate_w"], i["L2_ffn_shared_up_w"]], axis=1)[None],
                             i["L2_ffn_shared_down_w"][None])[:, 0]
    a["m2_wr"] = by_half(i["L2_ffn_gate_w"].T)
    a["m2_norm"] = wide(i["L2_ffn_norm_w"])
    w = heads_columns(i["L3_attn_Wqkv"].T)
    swap = np.arange(H) ^ 1
    a["a3_w"] = np.concatenate([w, w[:, :, 0:2][:, :, :, swap]], axis=2)
    a["a3_out"] = by_half(i["L3_attn_Wout"].T)
    a["rope_cos"], a["rope_sin"] = rope_tables()
    a["f_gu"] = np.concatenate([by_half(i["L3_ffn_gate_w"].T), by_half(i["L3_ffn_up_w"].T)], axis=2)
    down = i["L3_ffn_down_w"].T
    full = FI // P
    a["f_down"] = down[:full * P].reshape(full, P, H).transpose(1, 0, 2)
    a["f_down_last"] = down[full * P:]
    for n, key in (("gs", "gate_s"), ("us", "up_s")):
        v = i[f"L3_ffn_{key}"]
        a[f"f_{n}"] = v[:full * P].reshape(full, P).T
        a[f"f_{n}_last"] = v[full * P:].reshape(-1, 1)
    a["f_ds"] = wide(i["L3_ffn_down_s"])
    return a


def kernel(**inputs):
    import concourse.bacc as bacc
    from concourse.bass_utils import run_bass_kernel_spmd as run

    nc = bacc.Bacc("TRN2", target_bir_lowering=False, num_devices=1)
    arrays, args = {}, {}
    for name, value in layouts({k: np.asarray(v) for k, v in inputs.items()}).items():
        value = np.ascontiguousarray(value)
        arrays["in_" + name] = value
        args[name] = nc.dram_tensor("in_" + name, value.shape, mybir.dt.from_np(value.dtype), kind="ExternalInput").ap()
    out = nc.dram_tensor("out_0", (T, H), F32, kind="ExternalOutput").ap()
    program(nc, args, out)
    result = run(nc, [arrays], core_ids=[0])
    return result.results[0]["out_0"].reshape(B, S, H)
```

```python
from contextlib import ExitStack, contextmanager

import numpy as np

import concourse.bass as bass
from concourse import mybir

F32 = mybir.dt.float32
BF16 = mybir.dt.bfloat16
FP16 = mybir.dt.float16
I32 = mybir.dt.int32
U32 = mybir.dt.uint32
ALU = mybir.AluOpType
ACT = mybir.ActivationFunctionType
AX = mybir.AxisListType

P = 128
B, S, H = 2, 1024, 256
T = B * S
NT = T // P
KH = H // P
CH = 512
NC = T // CH
SUB = CH // P
TOPK = 4
I = 128
WE = 2 * KH * I + H
HEADS, D = 16, 16
BH = B * HEADS
KT = S // P
SEGS = 6
ROWS = SEGS * D
VD = D + 1
NS = 64
FI = 704
DECAY = 0.95
LN_EPS = 1e-5
RMS_EPS = 1e-6
CLIP = 7.0
NEG = -1e30

BASE = 8


def ready(t):
    return t + BASE + 1


def free(t, ring):
    return t + BASE + 1 - ring


def at(tensor, i):
    if isinstance(i, int):
        return tensor[:, i, :]
    return tensor[:, bass.ds(i, 1), :].rearrange("p a h -> p (a h)")


def col(tensor, i):
    if isinstance(i, int):
        return tensor[:, i:i + 1]
    return tensor[:, bass.ds(i, 1)]


def flat(ap):
    return ap.rearrange("p a b -> p (a b)")


class Step:

    def __init__(self, m, r, n):
        self.m, self.r, self.n = m, r, n

    def on(self, lag):
        return not isinstance(self.m, int) or 0 <= 4 * self.m + self.r - lag < self.n

    def behind(self, steps):
        return Step(self.m, self.r - steps, self.n)

    def tile(self, lag):
        q = self.r - lag
        return 4 * self.m + q, q % 4, self.m + q // 4


def pipeline(n, step, lags):
    for m in range(n // 4):
        for r in range(4):
            step(Step(m, r, n))
    for r in range(lags):
        step(Step(n // 4, r, n))


def settle(eng):
    eng.nop(nofuse=True)


class Chain:

    def __init__(self, eng, sem):
        self.eng, self.sem, self.n = eng, sem, 0

    def __call__(self, ins):
        self.n += 1
        ins.then_inc(self.sem, 1)
        self.eng.wait_ge(self.sem, self.n)


class Core:

    def __init__(self, nc):
        self.nc, self.open = nc, []
        self.behind = []

    def start_loads(self, sp):
        for dst, src, sem in self.behind:
            sp.dma_start(dst, src).then_inc(sem, 16)
        self.behind = []

    def sem(self, name):
        self.open.append(self.nc.alloc_semaphore(name=name))
        return self.open[-1]

    @contextmanager
    def layer(self):
        outer, self.open = self.open, []
        yield
        self.nc.clear_and_free_semaphores(self.open)
        self.nc.all_engine_barrier()
        self.open = outer

    def sems(self, stage, names):
        return {n: self.sem(f"{stage}_{n}") for n in names.split()}


def scratch(nc, ctx):
    def sb(name, shape, dt=F32):
        return ctx.enter_context(nc.sbuf_tensor(name, shape, dt))

    def ps(name, shape, dt=F32):
        return ctx.enter_context(nc.psum_tensor(name, shape, dt))
    return sb, ps


def open_sems(eng, *sems):
    for s in sems:
        eng.sem_inc(s, BASE)



class Stats:

    def __init__(self, core, stage, sb, src, rms=False):
        self.core, self.nc, self.src, self.rms = core, core.nc, src, rms
        self.st = sb(f"{stage}_st", [P, NT, 6])
        self.work = sb(f"{stage}_work", [P, 6, NT])
        self.s = core.sems(stage, "stats chain var root")
        self.counted = self.asked = self.answered = 0
        self.do = None

    def vector(self, dve, tiles):
        nc, core, s, st, V = self.nc, self.core, self.s, self.st, self.nc.vector
        mean, dev, var, root, ysq, tmp = (self.work[:, i, tiles] for i in range(6))
        rstd, nmr = core.rstd[:, tiles], core.nmr[:, tiles]
        for t in range(NT)[tiles]:
            V.bn_stats(at(st, t), at(self.src, t)).then_inc(s["stats"], 1)
            self.counted += 1
        dve.wait_ge(s["stats"], self.counted)
        do = self.do = self.do or Chain(dve, s["chain"])

        def inverse_root(out, value):
            V.tensor_copy(tmp, value).then_inc(s["var"], 1)
            self.asked += 1
            dve.wait_ge(s["root"], self.asked)
            do(V.reciprocal(out, root))
            do(V.tensor_tensor(ysq, out, out, ALU.mult))
            do(V.tensor_tensor(ysq, ysq, tmp, ALU.mult))
            do(V.tensor_scalar(ysq, ysq, -0.5, 1.5, ALU.mult, ALU.add))
            do(V.tensor_tensor(out, out, ysq, ALU.mult))

        do(V.tensor_tensor(mean, st[:, tiles, 1], st[:, tiles, 4], ALU.add))
        do(V.tensor_tensor(dev, st[:, tiles, 1], st[:, tiles, 4], ALU.subtract))
        do(V.tensor_scalar(mean, mean, 0.5, None, ALU.mult))
        do(V.tensor_scalar(dev, dev, 0.5, None, ALU.mult))
        do(V.tensor_tensor(dev, dev, dev, ALU.mult))
        do(V.tensor_tensor(var, st[:, tiles, 2], st[:, tiles, 5], ALU.add))
        do(V.scalar_tensor_tensor(var, var, 1.0 / H, dev, ALU.mult, ALU.add))
        do(V.tensor_scalar(dev, var, LN_EPS, None, ALU.add))
        inverse_root(rstd, dev)
        do(V.scalar_tensor_tensor(nmr, mean, -1.0, rstd, ALU.mult, ALU.mult))
        if self.rms:
            rstd2, nmr2 = core.rstd2[:, tiles], core.nmr2[:, tiles]
            do(V.tensor_tensor(var, var, rstd, ALU.mult))
            do(V.tensor_tensor(var, var, rstd, ALU.mult))
            do(V.tensor_scalar(var, var, RMS_EPS, None, ALU.add))
            inverse_root(rstd2, var)
            do(V.tensor_tensor(rstd2, rstd2, rstd, ALU.mult))
            do(V.scalar_tensor_tensor(nmr2, mean, -1.0, rstd2, ALU.mult, ALU.mult))
            do(V.tensor_scalar(core.rstd1[:, tiles], rstd, 1.0, None, ALU.add))

    def scalar(self, act, tiles):
        for _ in range(2 if self.rms else 1):
            self.answered += 1
            act.wait_ge(self.s["var"], self.answered)
            self.nc.scalar.activation(self.work[:, 3, tiles], self.work[:, 5, tiles], ACT.Sqrt
                                      ).then_inc(self.s["root"], 1)


def norm_stats(core, stage, src, rms=False, fetch=None):
    with ExitStack() as ctx:
        sb, _ = scratch(core.nc, ctx)
        stats = Stats(core, stage, sb, src, rms)
        with core.nc.Block() as block:
            @block.sync
            def _(sp):
                if fetch:
                    fetch(sp)

            @block.vector
            def _(dve):
                stats.vector(dve, slice(0, NT))

            @block.scalar
            def _(act):
                stats.scalar(act, slice(0, NT))



class Front:

    def __init__(self, core, stage, sb, psT, src, wait_used):
        self.core, self.nc, self.src = core, core.nc, src
        self.xn = [sb(f"{stage}_xn{i}", [P, H]) for i in range(4)]
        self.xt = [sb(f"{stage}_xt{i}", [P, KH, CH]) for i in range(2)]
        self.psT = psT
        self.s = core.sems(stage, "xn turned xt")
        self.wait_used = wait_used

    def open(self, eng, name):
        open_sems(eng, self.s[name])

    def vector(self, dve, c, group=None, done=None):
        for sub in range(SUB):
            t = SUB * c + sub
            g = SUB * (c if group is None else group) + sub
            dve.wait_ge(self.s["turned"], free(t, 4))
            ins = self.nc.vector.tensor_scalar(self.xn[sub][:, :], at(self.src, g), col(self.core.rstd, g),
                                               col(self.core.nmr, g), ALU.mult, ALU.add)
            ins.then_inc(done or self.s["xn"], 1)

    def tensor(self, pe, c):
        for sub in range(SUB):
            t = SUB * c + sub
            pe.wait_ge(self.s["xn"], ready(t))
            pe.wait_ge(self.s["xt"], free(t, 2))
            for k in range(KH):
                ins = self.nc.tensor.transpose(self.psT[sub % 2][:, k * P:(k + 1) * P],
                                               self.xn[sub][:, k * P:(k + 1) * P], self.core.ident[:, :])
            ins.then_inc(self.s["turned"], 1)

    def scalar(self, act, c, slot):
        self.wait_used(act, c)
        for sub in range(SUB):
            t = SUB * c + sub
            act.wait_ge(self.s["turned"], ready(t))
            self.nc.scalar.activation(self.xt[slot][:, :, sub * P:(sub + 1) * P],
                                      self.psT[sub % 2][:, 0:H].rearrange("p (k c) -> p k c", k=KH),
                                      ACT.Copy).then_inc(self.s["xt"], 1)



def layer0_attention(core, wv, wg, bg, wq, bq, wo):
    nc, x = core.nc, core.x
    with ExitStack() as ctx:
        sb, ps = scratch(nc, ctx)
        w = {n: sb(f"a0_w{n}", [P, KH, H]) for n in "vgqo"}
        bias = {n: sb(f"a0_b{n}", [P, KH]) for n in "gq"}
        decay = sb("a0_decay", [P, CH])
        sig_g = [sb(f"a0_sg{m}", [P, CH]) for m in range(KH)]
        sig_q = [sb(f"a0_sq{m}", [P, CH]) for m in range(KH)]
        store = [sb(f"a0_st{m}", [P, CH]) for m in range(KH)]
        mem = [[sb(f"a0_m{c}{m}", [P, CH]) for m in range(KH)] for c in range(2)]
        load = [[sb(f"a0_l{c}{m}", [P, CH]) for m in range(KH)] for c in range(2)]
        psT = [ps(f"a0_pT{i}", [P, CH]) for i in range(2)]
        psO = [ps(f"a0_pO{i}", [P, CH]) for i in range(2)]
        psG, psQ = ps("a0_pG", [P, CH]), ps("a0_pQ", [P, CH])
        psV = [ps(f"a0_pV{i}", [P, CH]) for i in range(2)]
        s = core.sems("a0", "weights decay pg pv pq sg sq store mem load po added")
        front = Front(core, "a0", sb, psT, x, lambda act, c: act.wait_ge(s["pq"], ready(KH * (c - 2) + KH - 1)))
        scale2 = float(np.float32(np.sqrt(1.0 - DECAY))) ** 2

        def fetch(sp):
            for n, src in (("v", wv), ("g", wg), ("q", wq), ("o", wo)):
                sp.dma_start(w[n][:, :, :], src).then_inc(s["weights"], 16)
            for n, src in (("g", bg), ("q", bq)):
                sp.dma_start(bias[n][:, :], src).then_inc(s["weights"], 16)
            core.start_loads(sp)
        norm_stats(core, "n0", x, fetch=fetch)

        with nc.Block() as block:
            @block.tensor
            def _(pe):
                front.open(pe, "turned")
                open_sems(pe, s["pg"], s["pv"], s["pq"], s["po"])
                pe.wait_ge(s["weights"], 96)

                def products(c):
                    pe.wait_ge(front.s["xt"], ready(SUB * c + SUB - 1))
                    for m in range(KH):
                        e = 2 * c + m
                        for name, dst, ring, freed, done in (("g", psG, 1, "sg", "pg"), ("v", psV[m], 2, "store", "pv"),
                                                             ("q", psQ, 1, "sq", "pq")):
                            pe.wait_ge(s[freed], free(e, ring))
                            for k in range(KH):
                                ins = nc.tensor.matmul(dst[:, :], w[name][:, k, m * P:(m + 1) * P],
                                                       front.xt[c % 2][:, k, :], start=k == 0, stop=k == KH - 1)
                            ins.then_inc(s[done], 1)

                def outputs(c):
                    pe.wait_ge(s["load"], ready(2 * c + 1))
                    for sub in range(SUB):
                        pe.wait_ge(s["added"], free(SUB * c + sub, 2))
                        for m in range(KH):
                            ins = nc.tensor.matmul(psO[sub % 2][:, 0:H], load[c % 2][m][:, sub * P:(sub + 1) * P],
                                                   w["o"][:, m, :], start=m == 0, stop=m == KH - 1)
                        ins.then_inc(s["po"], 1)
                front.tensor(pe, 0)
                for c in range(NC):
                    products(c)
                    if c < NC - 1:
                        front.tensor(pe, c + 1)
                    if c:
                        outputs(c - 1)
                outputs(NC - 1)

            @block.scalar
            def _(act):
                front.open(act, "xt")
                open_sems(act, s["sg"], s["sq"])
                nc.scalar.preload_act_table(ACT.Sigmoid)
                act.wait_ge(s["weights"], 96)
                front.scalar(act, 0, 0)
                for c in range(NC):
                    for m in range(KH):
                        e = 2 * c + m
                        act.wait_ge(s["pg"], ready(e))
                        act.wait_ge(s["store"], free(e, 2))
                        nc.scalar.activation(sig_g[m][:, :], psG[:, :], ACT.Sigmoid,
                                             bias=bias["g"][:, m:m + 1]).then_inc(s["sg"], 1)
                        act.wait_ge(s["pq"], ready(e))
                        act.wait_ge(s["load"], free(e, 2))
                        nc.scalar.activation(sig_q[m][:, :], psQ[:, :], ACT.Sigmoid,
                                             bias=bias["q"][:, m:m + 1]).then_inc(s["sq"], 1)
                    if c < NC - 1:
                        front.scalar(act, c + 1, (c + 1) % 2)

            @block.vector
            def _(dve):
                front.open(dve, "xn")
                open_sems(dve, s["store"], s["mem"], s["load"], s["added"])
                nc.vector.memset(decay[:, :], DECAY).then_inc(s["decay"], 1)
                dve.wait_ge(s["decay"], 1)

                def memory(c):
                    cc = c % 2
                    for m in range(KH):
                        e = 2 * c + m
                        dve.wait_ge(s["sg"], ready(e))
                        dve.wait_ge(s["pv"], ready(e))
                        dve.wait_ge(s["mem"], free(e, 2))
                        nc.vector.tensor_tensor(store[m][:, :], psV[m][:, :], sig_g[m][:, :],
                                                ALU.mult).then_inc(s["store"], 1)
                        dve.wait_ge(s["store"], ready(e))
                        nc.vector.tensor_tensor_scan(mem[cc][m][:, :], decay[:, :], store[m][:, :],
                                                     mem[0][m][:, CH - 1:CH] if cc else 0.0,
                                                     ALU.mult, ALU.add).then_inc(s["mem"], 1)
                        dve.wait_ge(s["mem"], ready(e))
                        dve.wait_ge(s["sq"], ready(e))
                        if c > 1:
                            dve.wait_ge(s["po"], ready(SUB * (c - 2) + SUB - 1))
                        nc.vector.scalar_tensor_tensor(load[cc][m][:, :], mem[cc][m][:, :], scale2, sig_q[m][:, :],
                                                       ALU.mult, ALU.mult).then_inc(s["load"], 1)

                def add(c):
                    for sub in range(SUB):
                        t = SUB * c + sub
                        dve.wait_ge(s["po"], ready(t))
                        nc.vector.tensor_tensor(at(x, t), at(x, t), psO[sub % 2][:, 0:H],
                                                ALU.add).then_inc(s["added"], 1)
                front.vector(dve, 0)
                for c in range(NC):
                    if c < NC - 1:
                        front.vector(dve, c + 1)
                    memory(c)
                    if c:
                        add(c - 1)
                add(NC - 1)



class Moe:

    def __init__(self, core, name, experts, kind, weights):
        self.core, self.name, self.E, self.kind, self.w = core, name, experts, kind, weights
        most = (T * TOPK - experts) // P + experts
        self.tiles = -(-most // 4) * 4


class FfnPipe:

    def __init__(self, core, stage, sb, ps, clip):
        self.core, self.nc, self.clip = core, core.nc, clip
        self.turn = 3 if clip else 2
        self.down = self.turn + 1
        self.src = [sb(f"{stage}_src{i}", [P, H]) for i in range(4)]
        self.xt = [sb(f"{stage}_xt{i}", [P, KH, P]) for i in range(2)]
        self.gu = [sb(f"{stage}_gu{i}", [P, 2 * I]) for i in range(2)]
        self.act = [sb(f"{stage}_act{i}", [P, I]) for i in range(2)]
        self.h = [sb(f"{stage}_h{i}", [P, I]) for i in range(2)]
        self.ht = [sb(f"{stage}_ht{i}", [P, I]) for i in range(2)]
        self.psT = [ps(f"{stage}_pT{i}", [P, CH]) for i in range(2)]
        self.psG = [ps(f"{stage}_pG{i}", [P, CH]) for i in range(2)]
        self.psH = [ps(f"{stage}_pH{i}", [P, CH]) for i in range(2)]
        self.psO = [ps(f"{stage}_pO{i}", [P, CH]) for i in range(2)]
        self.s = core.sems(stage, "turned xt pg clip act h ph ht po out")

    def open_tensor(self, pe):
        open_sems(pe, *(self.s[n] for n in ("turned", "pg", "ph", "po")))

    def open_scalar(self, act):
        open_sems(act, *(self.s[n] for n in ("xt", "act")))

    def open_vector(self, dve):
        open_sems(dve, *(self.s[n] for n in ("clip", "h", "ht", "out")))

    def tensor(self, pe, st, wait_source, weights, after_gate=None):
        nc, s = self.nc, self.s
        if st.on(0):
            t, r, m = st.tile(0)
            wait_source(pe, t, r, m)
            pe.wait_ge(s["xt"], free(t, 2))
            for k in range(KH):
                ins = nc.tensor.transpose(self.psT[r % 2][:, k * P:(k + 1) * P],
                                          self.src[r][:, k * P:(k + 1) * P], self.core.ident[:, :])
            ins.then_inc(s["turned"], 1)
        if st.on(1):
            t, r, _ = st.tile(1)
            w = weights(pe, t, 0)
            pe.wait_ge(s["xt"], ready(t))
            pe.wait_ge(s["clip" if self.clip else "h"], free(t, 2))
            for k in range(KH):
                ins = nc.tensor.matmul(self.psG[r % 2][:, 0:2 * I], self.xt[r % 2][:, k, :], w(k * 2 * I, 2 * I),
                                       start=k == 0, stop=k == KH - 1)
            if after_gate:
                after_gate(pe, t, r)
            else:
                ins.then_inc(s["pg"], 1)
        if st.on(self.turn):
            t, r, _ = st.tile(self.turn)
            pe.wait_ge(s["h"], ready(t))
            pe.wait_ge(s["ht"], free(t, 2))
            nc.tensor.transpose(self.psH[r % 2][:, 0:I], self.h[r % 2][:, :],
                                self.core.ident[:, :]).then_inc(s["ph"], 1)
        if st.on(self.down):
            t, r, _ = st.tile(self.down)
            w = weights(pe, t, 1)
            pe.wait_ge(s["ht"], ready(t))
            pe.wait_ge(s["out"], free(t, 2))
            nc.tensor.matmul(self.psO[r % 2][:, 0:H], self.ht[r % 2][:, :], w(2 * KH * I, H),
                             start=True, stop=True).then_inc(s["po"], 1)

    def scalar(self, act, st):
        nc, s = self.nc, self.s
        if st.on(0):
            t, r, _ = st.tile(0)
            act.wait_ge(s["turned"], ready(t))
            act.wait_ge(s["pg"], free(t, 2))
            nc.scalar.activation(flat(self.xt[r % 2][:, :, :]), self.psT[r % 2][:, 0:H],
                                 ACT.Copy).then_inc(s["xt"], 1)
        if st.on(1):
            t, r, _ = st.tile(1)
            act.wait_ge(s["clip" if self.clip else "pg"], ready(t))
            act.wait_ge(s["h"], free(t, 2))
            gate = self.gu[r % 2][:, 0:I] if self.clip else self.psG[r % 2][:, 0:I]
            nc.scalar.activation(self.act[r % 2][:, :], gate, ACT.Silu).then_inc(s["act"], 1)

    def vector(self, dve, st, take):
        nc, s = self.nc, self.s
        if st.on(1):
            t, r, _ = st.tile(1)
            if self.clip:
                dve.wait_ge(s["pg"], ready(t))
                dve.wait_ge(s["h"], free(t, 2))
                nc.vector.tensor_scalar(self.gu[r % 2][:, :], self.psG[r % 2][:, 0:2 * I], -CLIP, CLIP,
                                        ALU.max, ALU.min).then_inc(s["clip"], 1)
            else:
                dve.wait_ge(s["act"], ready(t))
                dve.wait_ge(s["ph"], free(t, 2))
                nc.vector.tensor_tensor(self.h[r % 2][:, :], self.psG[r % 2][:, I:2 * I], self.act[r % 2][:, :],
                                        ALU.mult).then_inc(s["h"], 1)
        if st.on(self.turn):
            t, r, _ = st.tile(self.turn)
            dve.wait_ge(s["ph"], ready(t))
            dve.wait_ge(s["po"], free(t, 2))
            nc.vector.tensor_copy(self.ht[r % 2][:, :], self.psH[r % 2][:, 0:I]).then_inc(s["ht"], 1)
        if st.on(self.down):
            t, r, m = st.tile(self.down)
            dve.wait_ge(s["po"], ready(t))
            take(t, r, m).then_inc(s["out"], 1)
        if st.on(1) and self.clip:
            t, r, _ = st.tile(1)
            dve.wait_ge(s["act"], ready(t))
            dve.wait_ge(s["ph"], free(t, 2))
            nc.vector.tensor_tensor(self.h[r % 2][:, :], self.gu[r % 2][:, I:2 * I], self.act[r % 2][:, :],
                                    ALU.mult).then_inc(s["h"], 1)


def moe_dense(moe, shared, router, norm_w, logits):
    core, nc, E = moe.core, moe.core.nc, moe.E
    x = core.x
    stage = moe.name + "d"
    rms = norm_w is not None
    AHEAD = 2
    with ExitStack() as ctx:
        sb, ps = scratch(nc, ctx)
        pipe = FfnPipe(core, stage, sb, ps, moe.kind == "softplus")
        ws = sb(f"{stage}_ws", [P, WE])
        wr = sb(f"{stage}_wr", [P, KH, E])
        nw = sb(f"{stage}_nw", [P, H]) if rms else None
        s = core.sems(stage, "weights norm xn logits")
        kept = [core.sem(f"{stage}_kept{i}") for i in range(4)]

        def fetch(sp):
            sp.dma_start(ws[:, :], shared).then_inc(s["weights"], 16)
            sp.dma_start(wr[:, :, :], router).then_inc(s["weights"], 16)
            if rms:
                sp.dma_start(nw[:, :], norm_w).then_inc(s["weights"], 16)
        norm_stats(core, moe.name + "n", x, rms, fetch)

        with nc.Block() as block:
            @block.sync
            def _(sp):
                def step(st):
                    if st.on(0):
                        t, r, _ = st.tile(0)
                        sp.wait_ge(s["xn"], ready(t))
                        sp.dma_start(at(core.rows, t), pipe.src[r][:, :]).then_inc(kept[r], 16)
                pipeline(NT, step, 0)
                for r in range(4):
                    sp.wait_ge(kept[r], 16 * NT // 4)

            @block.tensor
            def _(pe):
                pipe.open_tensor(pe)
                pe.wait_ge(s["weights"], 48 if rms else 32)

                def source(pe, t, r, m):
                    pe.wait_ge(s["xn"], ready(t))

                def after_gate(pe, t, r):
                    pe.wait_ge(s["logits"], free(t, 2))
                    for k in range(KH):
                        ins = nc.tensor.matmul(pipe.psG[r % 2][:, 2 * I:2 * I + E], pipe.xt[r % 2][:, k, :], wr[:, k, :],
                                               start=k == 0, stop=k == KH - 1)
                    ins.then_inc(pipe.s["pg"], 1)

                def step(st):
                    pipe.tensor(pe, st, source, lambda pe, t, part: lambda a, n: ws[:, a:a + n], after_gate)
                pipeline(NT, step, pipe.down)

            @block.scalar
            def _(act):
                pipe.open_scalar(act)
                nc.scalar.preload_act_table(ACT.Silu)
                if not pipe.clip:
                    open_sems(act, s["logits"])

                def step(st):
                    if st.on(1) and not pipe.clip:
                        t, r, _ = st.tile(1)
                        act.wait_ge(pipe.s["pg"], ready(t))
                        nc.scalar.activation(at(logits, t), pipe.psG[r % 2][:, 2 * I:2 * I + E],
                                             ACT.Copy).then_inc(s["logits"], 1)
                    pipe.scalar(act, st)
                pipeline(NT, step, 1)

            @block.vector
            def _(dve):
                pipe.open_vector(dve)
                open_sems(dve, s["xn"], s["norm"])
                if pipe.clip:
                    open_sems(dve, s["logits"])
                if rms:
                    dve.wait_ge(s["weights"], 48)

                def take(t, r, m):
                    return nc.vector.tensor_tensor(at(x, t), at(x, t), pipe.psO[r % 2][:, 0:H], ALU.add)

                def step(st):
                    if st.on(0):
                        t, r, m = st.tile(0)
                        dve.wait_ge(pipe.s["turned"], free(t, 4))
                        if not isinstance(m, int) or m:
                            dve.wait_ge(kept[r], 16 * m)
                        rstd, nmr = (core.rstd2, core.nmr2) if rms else (core.rstd, core.nmr)
                        ins = nc.vector.tensor_scalar(pipe.src[r][:, :], at(x, t), col(rstd, t), col(nmr, t),
                                                      ALU.mult, ALU.add)
                        if rms:
                            ins.then_inc(s["norm"], 1)
                            dve.wait_ge(s["norm"], ready(2 * t))
                            nc.vector.tensor_tensor(pipe.src[r][:, :], pipe.src[r][:, :], nw[:, :],
                                                    ALU.mult).then_inc(s["xn"], 1)
                            nc.vector.tensor_scalar(at(x, t), at(x, t), col(core.rstd1, t), col(core.nmr, t),
                                                    ALU.mult, ALU.add).then_inc(s["norm"], 1)
                        else:
                            ins.then_inc(s["xn"], 1)
                    st = st.behind(AHEAD)
                    if st.on(1) and pipe.clip:
                        t, r, _ = st.tile(1)
                        dve.wait_ge(pipe.s["pg"], ready(t))
                        nc.vector.tensor_copy(at(logits, t), pipe.psG[r % 2][:, 2 * I:2 * I + E]
                                              ).then_inc(s["logits"], 1)
                    if rms and st.on(pipe.down):
                        dve.wait_ge(s["norm"], ready(2 * st.tile(pipe.down)[0] + 1))
                    pipe.vector(dve, st, take)
                pipeline(NT, step, pipe.down + AHEAD)


def moe_route(moe, logits, expert_bias, out):
    core, nc, E, name = moe.core, moe.core.nc, moe.E, moe.name
    NE = moe.tiles
    with ExitStack() as ctx:
        sb, ps = scratch(nc, ctx)
        score = sb(f"{name}_score", [P, NT, E])
        sel = sb(f"{name}_sel", [P, NT, E])
        tmp = sb(f"{name}_tmp", [P, NT, E])
        tmp2 = sb(f"{name}_tmp2", [P, NT, E])
        bias = sb(f"{name}_bias", [P, E])
        top = sb(f"{name}_top", [P, NT, 8])
        idx = sb(f"{name}_idx", [P, NT, 8], U32)
        idxf = sb(f"{name}_idxf", [P, NT, TOPK])
        hot = sb(f"{name}_hot", [P, NT, TOPK, E])
        prod = sb(f"{name}_prod", [P, NT, TOPK, E])
        mask = sb(f"{name}_mask", [P, NT, E], BF16)
        before = sb(f"{name}_before", [P, NT + 1, E], BF16)
        row = sb(f"{name}_row", [P, 8, NT])
        count = sb(f"{name}_count", [P, 4, E])
        counti = sb(f"{name}_counti", [P, E], I32)
        slot = sb(f"{name}_slot", [P, NT, TOPK])
        sloti = sb(f"{name}_sloti", [P, 2, NT, TOPK], I32)
        hi = sb(f"{name}_hi", [P, NT * TOPK])
        lo = sb(f"{name}_lo", [P, NT * TOPK])
        eid = sb(f"{name}_eid", [P, 1])
        ge = sb(f"{name}_ge", [P, E])
        pick = [sb(f"{name}_pick{i}", [P, TOPK, P], FP16) for i in range(2)]
        place = [sb(f"{name}_place{i}", [P, TOPK, NE], FP16) for i in range(2)]
        psR = ps(f"{name}_psR", [P, NT, E])
        psC = ps(f"{name}_psC", [P, E])
        psE = ps(f"{name}_psE", [P, P])
        psI = ps(f"{name}_psI", [P, NE])
        s = core.sems(name + "r", "bias chain act acted mask ranks eid row picks used")

        with nc.Block() as block:
            @block.sync
            def _(sp):
                if expert_bias is not None:
                    sp.dma_start(bias[:, :], expert_bias).then_inc(s["bias"], 16)

            @block.scalar
            def _(act):
                if moe.kind == "sigmoid":
                    nc.scalar.activation(score[:, :, :], logits[:, :, :], ACT.Sigmoid).then_inc(s["acted"], 1)
                elif moe.kind == "softmax":
                    act.wait_ge(s["act"], 1)
                    nc.scalar.activation(tmp[:, :, :], tmp2[:, :, :], ACT.Exp).then_inc(s["acted"], 1)
                else:
                    act.wait_ge(s["act"], 1)
                    nc.scalar.activation(tmp[:, :, :], tmp2[:, :, :], ACT.Exp).then_inc(s["acted"], 1)
                    act.wait_ge(s["act"], 2)
                    nc.scalar.activation(score[:, :, :], tmp2[:, :, :], ACT.Ln).then_inc(s["acted"], 1)
                    act.wait_ge(s["act"], 3)
                    nc.scalar.activation(score[:, :, :], tmp[:, :, :], ACT.Sqrt).then_inc(s["acted"], 1)

            @block.vector
            def _(dve):
                do = Chain(dve, s["chain"])
                V = nc.vector
                dve.wait_ge(s["acted"], 1) if moe.kind == "sigmoid" else None
                if moe.kind == "softmax":
                    rmax, rsum = row[:, 0, :], row[:, 1, :]
                    do(V.tensor_reduce(rmax, logits[:, :, :], AX.X, ALU.max))
                    V.tensor_tensor(tmp2[:, :, :], logits[:, :, :], rmax.unsqueeze(2).broadcast_to([P, NT, E]),
                                    ALU.subtract).then_inc(s["act"], 1)
                    dve.wait_ge(s["acted"], 1)
                    do(V.tensor_reduce(rsum, tmp[:, :, :], AX.X, ALU.add))
                    do(V.reciprocal(rsum, rsum))
                    do(V.tensor_tensor(score[:, :, :], tmp[:, :, :], rsum.unsqueeze(2).broadcast_to([P, NT, E]),
                                       ALU.mult))
                if moe.kind == "softplus":
                    do(V.tensor_scalar(tmp2[:, :, :], logits[:, :, :], -1.0, None, ALU.mult))
                    V.tensor_tensor(tmp2[:, :, :], tmp2[:, :, :], logits[:, :, :], ALU.min).then_inc(s["act"], 1)
                    dve.wait_ge(s["acted"], 1)
                    V.tensor_scalar(tmp2[:, :, :], tmp[:, :, :], 1.0, None, ALU.add).then_inc(s["act"], 1)
                    dve.wait_ge(s["act"], 2)
                    dve.wait_ge(s["acted"], 2)
                    do(V.tensor_scalar(tmp2[:, :, :], tmp2[:, :, :], -1.0, None, ALU.add))
                    do(V.tensor_scalar(sel[:, :, :], tmp2[:, :, :], 0.0, None, ALU.is_equal))
                    do(V.tensor_tensor(tmp2[:, :, :], tmp2[:, :, :], sel[:, :, :], ALU.add))
                    do(V.tensor_tensor(sel[:, :, :], score[:, :, :], sel[:, :, :], ALU.add))
                    do(V.reciprocal(tmp2[:, :, :], tmp2[:, :, :]))
                    do(V.tensor_tensor(sel[:, :, :], sel[:, :, :], tmp2[:, :, :], ALU.mult))
                    do(V.tensor_tensor(tmp[:, :, :], tmp[:, :, :], sel[:, :, :], ALU.mult))
                    V.scalar_tensor_tensor(tmp[:, :, :], logits[:, :, :], 0.0, tmp[:, :, :], ALU.max,
                                           ALU.add).then_inc(s["act"], 1)
                    dve.wait_ge(s["act"], 3)
                    dve.wait_ge(s["acted"], 3)
                choose = score
                if expert_bias is not None:
                    dve.wait_ge(s["bias"], 16)
                    do(V.tensor_tensor(sel[:, :, :], score[:, :, :], bias[:, :].unsqueeze(1).broadcast_to([P, NT, E]),
                                       ALU.add))
                    choose = sel
                for t in range(NT):
                    V.max(top[:, t, :], choose[:, t, :]).then_inc(s["chain"], 1)
                do.n += NT
                dve.wait_ge(s["chain"], do.n)
                for t in range(NT):
                    V.max_index(idx[:, t, :], top[:, t, :], choose[:, t, :]).then_inc(s["chain"], 1)
                do.n += NT
                dve.wait_ge(s["chain"], do.n)
                do(V.tensor_copy(idxf[:, :, :], idx[:, :, 0:TOPK]))
                for k in range(TOPK):
                    V.tensor_tensor(hot[:, :, k, :], core.iota[:, 0:E].unsqueeze(1).broadcast_to([P, NT, E]),
                                    idxf[:, :, k:k + 1].broadcast_to([P, NT, E]), ALU.is_equal).then_inc(s["chain"], 1)
                do.n += TOPK
                dve.wait_ge(s["chain"], do.n)
                V.tensor_tensor(tmp[:, :, :], hot[:, :, 0, :], hot[:, :, 1, :], ALU.add).then_inc(s["chain"], 1)
                V.tensor_tensor(tmp2[:, :, :], hot[:, :, 2, :], hot[:, :, 3, :], ALU.add).then_inc(s["chain"], 1)
                do.n += 2
                dve.wait_ge(s["chain"], do.n)
                do(V.tensor_tensor(mask[:, :, :], tmp[:, :, :], tmp2[:, :, :], ALU.add))
                do(V.memset(before[:, 0, :], 0.0))
                for t in range(NT):
                    ins = V.tensor_tensor(before[:, t + 1, :], before[:, t, :], mask[:, t, :], ALU.add)
                    if t < NT - 1:
                        do(ins)
                    else:
                        ins.then_inc(s["mask"], 1)

                def chosen(dst, values):
                    for k in range(TOPK):
                        V.tensor_tensor(prod[:, :, k, :], hot[:, :, k, :], values, ALU.mult).then_inc(s["chain"], 1)
                    do.n += TOPK
                    dve.wait_ge(s["chain"], do.n)
                    do(V.tensor_reduce(dst, prod[:, :, :, :], AX.X, ALU.add))
                if choose is score:
                    do(V.tensor_copy(out["weight"][:, :, :], top[:, :, 0:TOPK]))
                else:
                    chosen(out["weight"][:, :, :], score[:, :, :])
                total = row[:, 2, :]
                do(V.tensor_reduce(total, out["weight"][:, :, :], AX.X, ALU.add))
                if moe.kind == "softplus":
                    do(V.tensor_scalar(total, total, 1e-20, None, ALU.add))
                do(V.reciprocal(total, total))
                do(V.tensor_tensor(out["weight"][:, :, :], out["weight"][:, :, :],
                                   total.unsqueeze(2).broadcast_to([P, NT, TOPK]), ALU.mult))

                cnt, need, end, start = (count[:, i, :] for i in range(4))
                dve.wait_ge(s["ranks"], 1)
                do(V.tensor_scalar(cnt, psC[:, :], float(P - 1), None, ALU.add))
                do(V.tensor_copy(counti[:, :], cnt))
                do(V.tensor_scalar(counti[:, :], counti[:, :], 7, None, ALU.arith_shift_right))
                do(V.tensor_copy(need, counti[:, :]))
                do(V.tensor_tensor_scan(end, core.onesf[:, 0:E], need, 0.0, ALU.mult, ALU.add))
                do(V.tensor_tensor(start, end, need, ALU.subtract))
                do(V.tensor_scalar(ge[:, :], end, core.part[:, 0:1], None, ALU.is_le))
                do(V.tensor_reduce(eid[:, :], ge[:, :], AX.X, ALU.add))
                V.tensor_scalar(eid[:, :], eid[:, :], float(E - 1), None, ALU.min).then_inc(s["eid"], 1)
                do(V.tensor_scalar(start, start, float(P), None, ALU.mult))
                if moe.kind == "softmax":
                    do(V.tensor_scalar(tmp[:, :, :], psR[:, :, :], float(2 * T * TOPK // E - 1), None, ALU.min))
                    do(V.tensor_tensor(tmp[:, :, :], tmp[:, :, :], start.unsqueeze(1).broadcast_to([P, NT, E]),
                                       ALU.add))
                    chosen(slot[:, :, :], tmp[:, :, :])
                    do(V.tensor_copy(out["read"][:, :, :], slot[:, :, :]))
                do(V.tensor_tensor(tmp[:, :, :], psR[:, :, :], start.unsqueeze(1).broadcast_to([P, NT, E]), ALU.add))
                chosen(slot[:, :, :], tmp[:, :, :])
                if moe.kind != "softmax":
                    do(V.tensor_copy(out["read"][:, :, :], slot[:, :, :]))
                do(V.tensor_copy(sloti[:, 0, :, :], slot[:, :, :]))
                do(V.tensor_scalar(sloti[:, 1, :, :], sloti[:, 0, :, :], 7, None, ALU.arith_shift_right))
                do(V.tensor_copy(hi[:, :], sloti[:, 1, :, :].rearrange("p a b -> p (a b)")))
                do(V.scalar_tensor_tensor(lo[:, :], hi[:, :], -float(P), slot[:, :, :].rearrange("p a b -> p (a b)"),
                                          ALU.mult, ALU.add))
                for t in range(NT):
                    dve.wait_ge(s["used"], free(t, 2))
                    for k in range(TOPK):
                        e = TOPK * t + k
                        V.tensor_scalar(pick[t % 2][:, k, :], core.iotab[:, :], lo[:, e:e + 1], None, ALU.is_equal)
                        ins = V.tensor_scalar(place[t % 2][:, k, :], core.iotab[:, 0:NE], hi[:, e:e + 1],
                                              core.number[:, t:t + 1], ALU.is_equal, ALU.mult)
                    ins.then_inc(s["picks"], 1)
                dve.wait_ge(s["used"], ready(NT - 1))
                do(V.tensor_copy(out["token"][:, 0:NE], psI[:, :]))
                dve.wait_ge(s["row"], 1)
                do(V.tensor_copy(out["expert"][0:1, 0:P], psE[0:1, :]))

            @block.tensor
            def _(pe):
                open_sems(pe, s["used"])
                pe.wait_ge(s["mask"], 1)
                fr = psR[:, :, :].rearrange("p a b -> p (a b)")
                nc.tensor.matmul(fr, core.earlier[:, :], mask[:, :, :].rearrange("p a b -> p (a b)"),
                                 start=True, stop=False)
                nc.tensor.matmul(fr, core.onesb[:, :], before[:, 0:NT, :].rearrange("p a b -> p (a b)"),
                                 start=False, stop=True)
                nc.tensor.matmul(psC[:, :], core.onesb[:, :], before[:, NT, :], start=True,
                                 stop=True).then_inc(s["ranks"], 1)
                pe.wait_ge(s["eid"], 1)
                nc.tensor.matmul(psE[0:1, :], eid[:, 0:1], core.ident[:, :], start=True, stop=True).then_inc(s["row"], 1)
                for t in range(NT):
                    pe.wait_ge(s["picks"], t + 1)
                    for k in range(TOPK):
                        ins = nc.tensor.matmul(psI[:, :], pick[t % 2][:, k, :], place[t % 2][:, k, :],
                                               start=t + k == 0, stop=t * k == (NT - 1) * (TOPK - 1))
                    ins.then_inc(s["used"], 1)


def moe_experts(moe, out):
    core, nc = moe.core, moe.core.nc
    stage, N = moe.name + "e", moe.tiles
    with ExitStack() as ctx:
        sb, ps = scratch(nc, ctx)
        pipe = FfnPipe(core, stage, sb, ps, moe.kind == "softplus")
        y = [sb(f"{stage}_y{i}", [P, H]) for i in range(4)]
        got = [core.sem(f"{stage}_got{i}") for i in range(4)]
        kept = [core.sem(f"{stage}_kept{i}") for i in range(4)]
        w3 = moe.w

        with nc.Block() as block:
            @block.gpsimd
            def _(pool):
                def step(st):
                    if st.on(0):
                        t, r, m = st.tile(0)
                        pool.wait_ge(pipe.s["turned"], free(t, 4))
                        settle(pool)
                        pool.indirect_dma_start(pipe.src[r][:, :], None, core.rows_flat,
                                                bass.IndirectOffsetOnAxis(ap=out["token"][:, t:t + 1].bitcast(U32), axis=0)
                                                ).then_inc(got[r], 16)
                pipeline(N, step, 0)

            @block.sync
            def _(sp):
                def step(st):
                    if st.on(3):
                        t, r, _ = st.tile(3)
                        sp.wait_ge(pipe.s["out"], ready(t))
                        sp.dma_start(at(core.results, t), y[r][:, :]).then_inc(kept[r], 16)
                pipeline(N, step, 3)
                for r in range(4):
                    sp.wait_ge(kept[r], 16 * N // 4)

            @block.tensor
            def _(pe):
                pipe.open_tensor(pe)
                for loaded in moe.loaded:
                    pe.wait_ge(loaded, 16)

                def source(pe, t, r, m):
                    pe.wait_ge(got[r], 16 * (m + 1))

                expert = {}

                def weights(pe, t, part):
                    if t not in expert:
                        expert[t] = pe.value_load(out["expert"][0:1, t:t + 1], min_val=0, max_val=moe.E - 1)
                        e = expert[t]
                    else:
                        e = expert.pop(t)
                    return lambda a, n: w3[:, bass.ds(e, 1), a:a + n].rearrange("p a c -> p (a c)")
                pipeline(N, lambda st: pipe.tensor(pe, st, source, weights), pipe.down)

            @block.scalar
            def _(act):
                pipe.open_scalar(act)
                nc.scalar.preload_act_table(ACT.Silu)
                pipeline(N, lambda st: pipe.scalar(act, st), 1)

            @block.vector
            def _(dve):
                pipe.open_vector(dve)

                def take(t, r, m):
                    if not isinstance(m, int) or m:
                        dve.wait_ge(kept[r], 16 * m)
                    return nc.vector.tensor_copy(y[r][:, :], pipe.psO[r % 2][:, 0:H])
                pipeline(N, lambda st: pipe.vector(dve, st, take), pipe.down)


class Combine:
    RING = 4

    def __init__(self, core, stage, sb, order):
        self.core, self.nc, self.order = core, core.nc, order
        self.rows = [[sb(f"{stage}_row{i}{k}", [P, H]) for k in range(TOPK)] for i in range(self.RING)]
        self.s = core.sems(stage, "summed")
        self.got = [[core.sem(f"{stage}_got{i}{k}") for k in range(TOPK)] for i in range(self.RING)]

    def open_vector(self, dve):
        open_sems(dve, self.s["summed"])

    def added(self, p, k):
        return 2 * TOPK * (p // 2) + 2 * k + p % 2

    def pool(self, pool, p):
        t, slot = self.order[p], p % self.RING
        if p >= self.RING:
            pool.wait_ge(self.s["summed"], ready(self.added(p - self.RING, TOPK - 1)))
            settle(pool)
        for k in range(TOPK):
            e = TOPK * t + k
            pool.indirect_dma_start(self.rows[slot][k][:, :], None, self.core.results_flat[0:self.core.result_rows, :],
                                    bass.IndirectOffsetOnAxis(ap=self.core.read[:, e:e + 1].bitcast(U32), axis=0)
                                    ).then_inc(self.got[slot][k], 16)

    def vector(self, dve, first):
        for k in range(TOPK):
            for p in (first, first + 1):
                t, slot = self.order[p], p % self.RING
                e = TOPK * t + k
                dve.wait_ge(self.got[slot][k], 16 * (p // self.RING + 1))
                if k:
                    dve.wait_ge(self.s["summed"], ready(self.added(p, k - 1)))
                self.nc.vector.scalar_tensor_tensor(at(self.core.x, t), self.rows[slot][k][:, :],
                                                    self.core.weight[:, e:e + 1], at(self.core.x, t),
                                                    ALU.mult, ALU.add).then_inc(self.s["summed"], 1)


def moe_layer(moe, shared, router, expert_bias, norm_w=None):
    core, nc, E, name = moe.core, moe.core.nc, moe.E, moe.name
    with ExitStack() as ctx:
        sb, _ = scratch(nc, ctx)
        out = {"weight": core.weight[:, :].rearrange("p (a b) -> p a b", b=TOPK),
               "read": core.read[:, :].rearrange("p (a b) -> p a b", b=TOPK),
               "token": sb(f"{name}_token", [P, moe.tiles], I32), "expert": sb(f"{name}_expert", [1, P], I32)}
        with ExitStack() as inner:
            logits = inner.enter_context(nc.sbuf_tensor(f"{name}_logits", [P, NT, E], F32))
            moe_dense(moe, shared, router, norm_w, logits)
            moe_route(moe, logits, expert_bias, out)
        core.result_rows = moe.tiles * P
        moe_experts(moe, out)



def layer1_attention(core, shift, gate, gamma, beta, kv, time_decay, time_first, w_out):
    nc, x = core.nc, core.x
    with ExitStack() as ctx:
        sb, _ = scratch(nc, ctx)
        shifted = sb("a1_shifted", [P, NT, H])
        states = sb("a1_states", [P, S])
        layer1_shift(core, shift, gate, shifted)
        layer1_scan(core, gamma, beta, kv, time_decay, time_first, shifted, states)
        layer1_out(core, w_out, states)


def layer1_shift(core, shift, gate, shifted):
    nc, x = core.nc, core.x
    with ExitStack() as ctx:
        sb, ps = scratch(nc, ctx)
        w = sb("a1_w", [P, KH, H])
        g_new, g_old = sb("a1_gnew", [P, H]), sb("a1_gold", [P, H])
        xn = [sb(f"a1_xn{q}", [P, H]) for q in range(4)]
        xt = [sb(f"a1_xt{q}", [P, KH, P]) for q in range(2)]
        new = [sb(f"a1_new{q}", [P, H]) for q in range(2)]
        old = [sb(f"a1_old{q}", [P, H]) for q in range(2)]
        psT = [ps(f"a1_pT{q}", [P, CH]) for q in range(2)]
        psS = [ps(f"a1_pS{q}", [P, CH]) for q in range(2)]
        s = core.sems("a1", "weights gate gates xn turned xt ps new old mixed")

        def fetch(sp):
            sp.dma_start(w[:, :, :], shift).then_inc(s["weights"], 16)
            sp.dma_start(g_new[:, :], gate).then_inc(s["weights"], 16)
        rounds = [slice(n, NT, 4) for n in range(4)]
        combine = Combine(core, "a1c", sb, [4 * q + n for n in range(4) for q in range(4)])
        stats = Stats(core, "n1", sb, x)

        with nc.Block() as block:
            @block.sync
            def _(sp):
                fetch(sp)

            @block.scalar
            def _(act):
                open_sems(act, s["xt"])
                act.wait_ge(s["weights"], 32)
                nc.scalar.activation(g_new[:, :], g_new[:, :], ACT.Sigmoid).then_inc(s["gate"], 1)
                for n in range(4):
                    stats.scalar(act, rounds[n])
                    for q in range(4):
                        e = 4 * n + q
                        act.wait_ge(s["turned"], ready(e))
                        act.wait_ge(s["ps"], free(e, 2))
                        nc.scalar.activation(flat(xt[q % 2][:, :, :]), psT[q % 2][:, 0:H],
                                             ACT.Copy).then_inc(s["xt"], 1)

            @block.tensor
            def _(pe):
                open_sems(pe, s["turned"], s["ps"])
                pe.wait_ge(s["weights"], 32)
                for n in range(4):
                    for q in range(4):
                        e = 4 * n + q
                        pe.wait_ge(s["xn"], ready(e))
                        pe.wait_ge(s["xt"], free(e, 2))
                        for k in range(KH):
                            ins = nc.tensor.transpose(psT[q % 2][:, k * P:(k + 1) * P], xn[q][:, k * P:(k + 1) * P],
                                                      core.ident[:, :])
                        ins.then_inc(s["turned"], 1)
                        pe.wait_ge(s["xt"], ready(e))
                        pe.wait_ge(s["new"], free(e, 2))
                        for k in range(KH):
                            ins = nc.tensor.matmul(psS[q % 2][:, 0:H], xt[q % 2][:, k, :], w[:, k, :],
                                                   start=k == 0, stop=k == KH - 1)
                        ins.then_inc(s["ps"], 1)

            @block.gpsimd
            def _(pool):
                for p in range(NT):
                    combine.pool(pool, p)

            @block.vector
            def _(dve):
                open_sems(dve, s["xn"], s["new"], s["old"], s["mixed"])
                combine.open_vector(dve)
                dve.wait_ge(s["gate"], 1)
                nc.vector.tensor_scalar(g_old[:, :], g_new[:, :], -1.0, 1.0, ALU.mult, ALU.add).then_inc(s["gates"], 1)
                for q in (0, 2):
                    combine.vector(dve, q)
                for n in range(4):
                    dve.wait_ge(combine.s["summed"], ready(TOPK * (4 * n + 3) + TOPK - 1))
                    stats.vector(dve, rounds[n])
                    for q in range(4):
                        e = 4 * n + q
                        t = 4 * q + n
                        dve.wait_ge(s["turned"], free(e, 4))
                        if n:
                            dve.wait_ge(s["old"], ready(4 * n - 4 + (q ^ 1)))
                        nc.vector.tensor_scalar(xn[q][:, :], at(x, t), col(core.rstd, t), col(core.nmr, t),
                                                ALU.mult, ALU.add).then_inc(s["xn"], 1)
                    dve.wait_ge(s["xn"], ready(4 * n + 3))
                    for q in range(4):
                        e = 4 * n + q
                        dve.wait_ge(s["mixed"], free(e, 2))
                        nc.vector.tensor_tensor(old[q % 2][:, :], xn[q ^ 1][:, :], g_old[:, :],
                                                ALU.mult).then_inc(s["old"], 1)
                        dve.wait_ge(s["ps"], ready(e))
                        dve.wait_ge(s["mixed"], free(e, 2))
                        nc.vector.tensor_tensor(new[q % 2][:, :], psS[q % 2][:, 0:H], g_new[:, :],
                                                ALU.mult).then_inc(s["new"], 1)
                        if n < 3 and q % 2:
                            combine.vector(dve, e + 3)
                        dve.wait_ge(s["new"], ready(e))
                        dve.wait_ge(s["old"], ready(e))
                        nc.vector.tensor_tensor(at(shifted, 4 * (q ^ 1) + n), new[q % 2][:, :], old[q % 2][:, :],
                                                ALU.add).then_inc(s["mixed"], 1)


def layer1_scan(core, gamma, beta, kv, time_decay, time_first, shifted, states):
    nc = core.nc
    with ExitStack() as ctx:
        sb, ps = scratch(nc, ctx)
        w = sb("a1_wkv", [P, KH, 2 * NS])
        gam, bet = sb("a1_gamma", [P, H]), sb("a1_beta", [P, H])
        dec, first = sb("a1_dec", [P, 1]), sb("a1_first", [P, 1])
        decays = sb("a1_decays", [P, S])
        sig, gain = sb("a1_sig", [P, CH]), sb("a1_gain", [P, CH])
        wkv = sb("a1_wkvs", [P, S])
        psT = [ps(f"a1_kT{q}", [P, CH]) for q in range(2)]
        psK, psV = ps("a1_pK", [P, CH]), ps("a1_pV", [P, CH])
        s = core.sems("a1k", "weights exps ready scaled gained pk sig gain wkv scan")
        front = Front(core, "a1k", sb, psT, shifted, lambda act, c: act.wait_ge(s["pk"], ready(c - 2)))

        def fetch(sp):
                for dst, src in ((w[:, :, :], kv), (gam[:, :], gamma), (bet[:, :], beta), (dec[:, :], time_decay),
                                 (first[:, :], time_first)):
                    sp.dma_start(dst, src).then_inc(s["weights"], 16)
                core.start_loads(sp)
        norm_stats(core, "n1s", shifted, fetch=fetch)

        with nc.Block() as block:
            @block.scalar
            def _(act):
                front.open(act, "xt")
                open_sems(act, s["sig"], s["gain"])
                act.wait_ge(s["weights"], 80)
                nc.scalar.activation(dec[:, :], dec[:, :], ACT.Exp).then_inc(s["exps"], 1)
                nc.scalar.activation(first[:, :], first[:, :], ACT.Exp).then_inc(s["exps"], 1)
                act.wait_ge(s["ready"], 2)
                with act.Fori(0, 2) as cc:
                    for b in range(B):
                        front.scalar(act, 2 * cc + b, b)
                    act.wait_ge(s["pk"], ready(2 * cc + 1))
                    nc.scalar.activation(sig[:, :], psK[:, :], ACT.Sigmoid).then_inc(s["sig"], 1)
                    act.wait_ge(s["sig"], ready(cc))
                    act.wait_ge(s["wkv"], free(cc, 1))
                    nc.scalar.activation(gain[:, :], sig[:, :], ACT.Exp, scale=first[:, 0:1]).then_inc(s["gain"], 1)

            @block.tensor
            def _(pe):
                front.open(pe, "turned")
                open_sems(pe, s["pk"])
                pe.wait_ge(s["weights"], 80)
                with pe.Fori(0, 2) as cc:
                    for b in range(B):
                        c = 2 * cc + b
                        front.tensor(pe, c)
                        pe.wait_ge(front.s["xt"], ready(SUB * c + SUB - 1))
                        if b == 0:
                            pe.wait_ge(s["wkv"], free(cc, 1))
                        for i, dst in ((0, psK), (1, psV)):
                            for k in range(KH):
                                ins = nc.tensor.matmul(dst[NS * b:NS * (b + 1), :], w[:, k, NS * i:NS * (i + 1)],
                                                       front.xt[b][:, k, :], start=k == 0, stop=k == KH - 1)
                        ins.then_inc(s["pk"], 1)

            @block.gpsimd
            def _(pool):
                front.open(pool, "xn")
                open_sems(pool, s["gained"])
                pool.wait_ge(s["weights"], 80)
                with pool.Fori(0, 2) as cc:
                    for q in range(B * SUB):
                        t = B * SUB * cc + q
                        pool.wait_ge(s["scaled"], ready(t))
                        nc.gpsimd.tensor_tensor(front.xn[q % 4][:, :], front.xn[q % 4][:, :], gam[:, :],
                                                ALU.mult).then_inc(s["gained"], 1)
                        pool.wait_ge(s["gained"], ready(t))
                        nc.gpsimd.tensor_tensor(front.xn[q % 4][:, :], front.xn[q % 4][:, :], bet[:, :],
                                                ALU.add).then_inc(front.s["xn"], 1)

            @block.vector
            def _(dve):
                open_sems(dve, s["scaled"], s["wkv"])
                nc.vector.memset(decays[:, :], 1.0).then_inc(s["scan"], 1)
                dve.wait_ge(s["exps"], 2)
                dve.wait_ge(s["scan"], 1)
                nc.vector.tensor_scalar(decays[:, :], decays[:, :], dec[:, 0:1], None, ALU.mult).then_inc(s["ready"], 1)
                nc.vector.tensor_scalar(first[:, :], first[:, :], -1.0, None, ALU.mult).then_inc(s["ready"], 1)
                with dve.Fori(0, 2) as cc:
                    for b in range(B):
                        front.vector(dve, 2 * cc + b, 2 * b + cc, s["scaled"])
                    dve.wait_ge(s["gain"], ready(cc))
                    nc.vector.tensor_tensor(wkv[:, bass.ds(CH * cc, CH)], psV[:, :], gain[:, :],
                                            ALU.mult).then_inc(s["wkv"], 1)
                dve.wait_ge(s["wkv"], ready(1))
                dve.wait_ge(s["ready"], 2)
                nc.vector.tensor_tensor_scan(states[:, :], decays[:, :], wkv[:, :], 0.0, ALU.mult,
                                             ALU.add).then_inc(s["scan"], 1)


def layer1_out(core, w_out, states):
    nc, x = core.nc, core.x
    with ExitStack() as ctx:
        sb, ps = scratch(nc, ctx)
        w = sb("a1_wo", [P, H])
        psO = [ps(f"a1_pO{q}", [P, CH]) for q in range(4)]
        s = core.sems("a1o", "weights po added")

        with nc.Block() as block:
            @block.sync
            def _(sp):
                sp.dma_start(w[:, :], w_out).then_inc(s["weights"], 16)

            @block.tensor
            def _(pe):
                open_sems(pe, s["po"])
                pe.wait_ge(s["weights"], 16)
                for t in range(NT):
                    b, j = divmod(t, KT)
                    pe.wait_ge(s["added"], free(t, 4))
                    nc.tensor.matmul(psO[t % 4][:, 0:H], states[NS * b:NS * (b + 1), j * P:(j + 1) * P],
                                     w[NS * b:NS * (b + 1), :], start=True, stop=True).then_inc(s["po"], 1)

            @block.vector
            def _(dve):
                open_sems(dve, s["added"])
                with dve.Fori(0, NT // 4) as m:
                    for r in range(4):
                        t = 4 * m + r
                        dve.wait_ge(s["po"], ready(t))
                        nc.vector.tensor_tensor(at(x, t), at(x, t), psO[r][:, 0:H], ALU.add).then_inc(s["added"], 1)



SPLITS = {"q": ((0, 3, 0, False), (3, 2, 0, False), (5, 1, 0, False)),
          "k": ((0, 3, 0, True), (3, 2, 1, True), (5, 1, 2, True))}


def softmax_attention(core, name, w_qkv, w_out, rope):
    with ExitStack() as ctx:
        sb, _ = scratch(core.nc, ctx)
        v = sb(f"{name}_v", [P, BH, KT, VD])
        attention_project(core, name, w_qkv, rope, v)
        mixed = sb(f"{name}_mixed", [P, BH // 4, KT * 4 * D])
        attention_heads(core, name, v, mixed)
        attention_out(core, name, w_out, mixed)


def attention_project(core, name, w_qkv, rope, v):
    nc, x = core.nc, core.x
    stage = name + "p"
    with ExitStack() as ctx:
        sb, ps = scratch(nc, ctx)
        w = sb(f"{stage}_w", [P, KH, 5 if rope else 3, H])
        parts = [sb(f"{stage}_parts{i}", [P, 3, CH], BF16) for i in range(4)]
        rest = [sb(f"{stage}_rest{i}", [P, CH]) for i in range(2)]
        psT = [ps(f"{stage}_pT{i}", [P, CH]) for i in range(2)]
        psV = [ps(f"{stage}_pV{i}", [P, CH]) for i in range(2)]
        psJ = [ps(f"{stage}_pJ{i}", [P, CH]) for i in range(2)]
        if rope:
            psW = [ps(f"{stage}_pW{i}", [P, CH]) for i in range(2)]
            cos, sin = sb(f"{stage}_cos", [P, S]), sb(f"{stage}_sin", [P, S])
            turn_a = [sb(f"{stage}_ta{i}", [P, CH]) for i in range(2)]
            turn_b = [sb(f"{stage}_tb{i}", [P, CH]) for i in range(2)]
        s = core.sems(stage, "weights ones pj turns roped first rest second third pv v")
        written = [core.sem(f"{stage}_written{i}") for i in range(4)]
        front = Front(core, stage, sb, psT, x, lambda act, c: act.wait_ge(s["pv"], ready(SUB * (c - 2) + SUB - 1)))
        n_weights = 48 if rope else 16
        UNITS = (("q", 0), ("q", 1), ("k", 0), ("k", 1))
        U = len(UNITS)
        EARLY = 1

        def fetch(sp):
            sp.dma_start(w[:, :, :, :], w_qkv).then_inc(s["weights"], 16)
            if rope:
                sp.dma_start(cos[:, :], rope[0]).then_inc(s["weights"], 16)
                sp.dma_start(sin[:, :], rope[1]).then_inc(s["weights"], 16)
        combine = Combine(core, name + "c", sb, list(range(NT)))
        stats = Stats(core, name + "n", sb, x)
        chunks = [slice(SUB * c, SUB * (c + 1)) for c in range(NC)]

        with nc.Block() as block:
            @block.sync
            def _(sp):
                fetch(sp)
                for c in range(NC):
                    b, cc = divmod(c, 2)
                    for u, (which, half) in enumerate(UNITS):
                        sp.wait_ge(s["third"], ready(U * c + u))
                        dram = core.stack[which]
                        for seg, count, part, same in SPLITS[which]:
                            src = parts[u][:, part:part + (1 if same else count), :]
                            if same and count > 1:
                                src = src.broadcast_to([P, count, CH])
                            dst = dram[b * H + half * P:b * H + (half + 1) * P, seg:seg + count, cc * CH:(cc + 1) * CH]
                            sp.dma_start(dst, src).then_inc(written[u], 16)
                for u in range(U):
                    sp.wait_ge(written[u], 48 * NC)

            @block.tensor
            def _(pe):
                front.open(pe, "turned")
                open_sems(pe, s["pj"], s["pv"])
                pe.wait_ge(s["weights"], n_weights)

                def value(t):
                    pe.wait_ge(s["v"], free(t, 2))
                    for k in range(KH):
                        ins = nc.tensor.matmul(psV[t % 2][:, 0:H],
                                               front.xt[t // SUB % 2][:, k, t % SUB * P:(t % SUB + 1) * P],
                                               w[:, k, 2, :], start=k == 0, stop=k == KH - 1)
                    ins.then_inc(s["pv"], 1)
                front.tensor(pe, 0)
                for c in range(NC):
                    pe.wait_ge(front.s["xt"], ready(SUB * c + SUB - 1))
                    for u, (which, half) in enumerate(UNITS):
                        e = U * c + u
                        pe.wait_ge(s["turns" if rope else "rest"], free(e, 2))
                        i = "qk".index(which)
                        for dst, j in ((psJ[u % 2], i), (psW[u % 2] if rope else None, 3 + i)):
                            if dst is not None:
                                for k in range(KH):
                                    ins = nc.tensor.matmul(dst[:, :], w[:, k, j, half * P:(half + 1) * P],
                                                           front.xt[c % 2][:, k, :], start=k == 0, stop=k == KH - 1)
                        ins.then_inc(s["pj"], 1)
                        value(SUB * c + u)
                    if c < NC - 1:
                        front.tensor(pe, c + 1)

            @block.scalar
            def _(act):
                front.open(act, "xt")
                open_sems(act, s["first"], s["second"], s["v"])
                act.wait_ge(s["ones"], 1)
                stats.scalar(act, chunks[0])
                front.scalar(act, 0, 0)
                for c in range(NC):
                    for u in range(U):
                        e = U * c + u
                        value = turn_a[u % 2][:, :] if rope else psJ[u % 2][:, :]
                        act.wait_ge(s["roped" if rope else "pj"], ready(e))
                        if c:
                            act.wait_ge(written[u], 48 * c)
                        nc.scalar.activation(parts[u][:, 0, :], value, ACT.Copy).then_inc(s["first"], 1)
                        t = SUB * c + u
                        b, tile = divmod(t, KT)
                        act.wait_ge(s["pv"], ready(t))
                        nc.scalar.activation(v[:, b * HEADS:(b + 1) * HEADS, tile, 0:D],
                                             psV[t % 2][:, 0:H].rearrange("p (h d) -> p h d", d=D),
                                             ACT.Copy).then_inc(s["v"], 1)
                        act.wait_ge(s["rest"], ready(e))
                        nc.scalar.activation(parts[u][:, 1, :], rest[u % 2][:, :],
                                             ACT.Copy).then_inc(s["second"], 1)
                        if u == EARLY and c < NC - 1:
                            stats.scalar(act, chunks[c + 1])
                            front.scalar(act, c + 1, (c + 1) % 2)

            @block.gpsimd
            def _(pool):
                for p in range(NT):
                    combine.pool(pool, p)

            @block.vector
            def _(dve):
                front.open(dve, "xn")
                open_sems(dve, *(s[n] for n in ("rest", "turns", "roped", "third")))
                nc.vector.memset(v[:, :, :, D:VD], 1.0).then_inc(s["ones"], 1)
                dve.wait_ge(s["weights"], n_weights)

                def turn(e):
                    u = e % U
                    dve.wait_ge(s["pj"], ready(e))
                    dve.wait_ge(s["rest"], free(e, 2))
                    pos = slice(e // U % 2 * CH, (e // U % 2 + 1) * CH)
                    nc.vector.tensor_tensor(turn_b[u % 2][:, :], psW[u % 2][:, :], sin[:, pos], ALU.mult)
                    nc.vector.tensor_tensor(turn_a[u % 2][:, :], psJ[u % 2][:, :], cos[:, pos],
                                            ALU.mult).then_inc(s["turns"], 1)
                    dve.wait_ge(s["turns"], ready(e))
                    nc.vector.tensor_tensor(turn_a[u % 2][:, :], turn_a[u % 2][:, :], turn_b[u % 2][:, :],
                                            ALU.add).then_inc(s["roped"], 1)
                combine.open_vector(dve)
                for u in (0, 2):
                    combine.vector(dve, u)

                def prepare(c):
                    dve.wait_ge(combine.s["summed"], ready(TOPK * (U * c + U - 1) + TOPK - 1))
                    stats.vector(dve, chunks[c])
                    front.vector(dve, c)
                prepare(0)
                if rope:
                    turn(0)
                for c in range(NC):
                    for u in range(U):
                        e = U * c + u
                        if rope and u < U - 1:
                            turn(e + 1)
                        dve.wait_ge(s["first"], ready(e))
                        dve.wait_ge(s["third"], free(e, 2))
                        nc.vector.tensor_tensor(rest[u % 2][:, :], turn_a[u % 2][:, :] if rope else psJ[u % 2][:, :],
                                                parts[u][:, 0, :], ALU.subtract).then_inc(s["rest"], 1)
                        if rope and u == U - 1 and c < NC - 1:
                            turn(e + 1)
                        if c < NC - 1 and u <= EARLY:
                            combine.vector(dve, U * (c + 1) + 2 * u)
                        dve.wait_ge(s["second"], ready(e))
                        nc.vector.tensor_tensor(parts[u][:, 2, :], rest[u % 2][:, :], parts[u][:, 1, :],
                                                ALU.subtract).then_inc(s["third"], 1)
                        if u == EARLY and c < NC - 1:
                            prepare(c + 1)


def attention_heads(core, name, v, mixed):
    nc = core.nc
    stage = name + "h"
    GROUPS = BH // 4
    HALF = CH // P
    PIECES = [(0, 0), (1, 0), (0, 1), (1, 1), (0, 2), (1, 5), (0, 3), (1, 2), (1, 6), (1, 4), (1, 7), (1, 3)]
    NP = len(PIECES)
    last_of = [max(i for i, piece in enumerate(PIECES) if piece[0] == c) for c in range(2)]
    TURNS = list(range(8)) + ["maximum 0", "maximum 1"] + list(range(8, NP))
    NU = len(TURNS)
    AHEAD = 2
    PROBS = 6
    MAXIMA = list(range(KT))[::-1]
    MAXIMA_AT = {p + p // 2 + 1: (p,) for p in range(KT)}
    OUTPUTS_AT = 12
    with ExitStack() as ctx:
        sb, ps = scratch(nc, ctx)
        R3 = ROWS + 3
        q_rows = [sb(f"{stage}_q{i}", [R3, S], BF16) for i in range(4)]
        k_rows = [sb(f"{stage}_k{i}", [R3, S], BF16) for i in range(4)]
        neg = sb(f"{stage}_neg", [P, KT])
        left = sb(f"{stage}_left", [P, KT])
        neg3 = [sb(f"{stage}_neg3{i}", [P, KT, 3], BF16) for i in range(2)]
        probs = [sb(f"{stage}_probs{i}", [P, CH]) for i in range(PROBS)]
        values = [sb(f"{stage}_values{i}", [P, KT, VD]) for i in range(4)]
        turned = sb(f"{stage}_turned", [P, S])
        rden = sb(f"{stage}_rden", [P, HALF, 4])
        psM = [ps(f"{stage}_pM{i}", [P, S]) for i in range(2)]
        psX = [ps(f"{stage}_pX{i}", [P, CH]) for i in range(2)]
        psV = [ps(f"{stage}_pV{i}", [P, CH]) for i in range(2)]
        s = core.sems(stage, "ones clear pm max split neg3 px ex values pv copied rden")
        loaded = [core.sem(f"{stage}_loaded{i}") for i in range(4)]

        def groups(eng, body):
            body(0)
            with eng.Fori(1, GROUPS - 1) as g:
                body(g)
            body(GROUPS - 1)

        def final(t):
            return isinstance(t, int) and t == BH - 1

        def ahead(g, r):
            return g + (r + AHEAD) // 4, (r + AHEAD) % 4

        def has_ahead(g, r):
            return not (isinstance(g, int) and 4 * g + r + AHEAD >= BH)

        def turns(t):
            return [j for j in range(NU) if not (final(t) and isinstance(TURNS[j], str))]

        def bank_use(t, j):
            n = 2 + NU * t + j
            return n - 2 if final(t) and j > TURNS.index("maximum 1") else n

        def rows_use(g, r, i):
            if isinstance(g, int) and g == r == 0:
                return i
            return bank_use(4 * g + r - 1, TURNS.index("maximum 0") + i)

        def maximum_use(g, r, p):
            return AHEAD * KT + (34 * g + KT * r + p) - (2 if r == 0 and not (isinstance(g, int) and g == 0) else 0)

        def output_use(g, c):
            if isinstance(g, int) and g == GROUPS - 1:
                return AHEAD * KT + 34 * g + (4 - AHEAD) * KT + c
            return AHEAD * KT + 34 * (g + 1) + KT - 2 + c

        with nc.Block() as block:
            @block.sync
            def _(sp):
                def fetch(t, r):
                    for which, dst in (("q", q_rows[r]), ("k", k_rows[r])):
                        sp.dma_start(dst[0:ROWS, :], core.stack_rows[which][bass.ds(t * ROWS, ROWS), :]
                                     ).then_inc(loaded[r], 16)
                for r in range(4):
                    fetch(r, r)
                core.start_loads(sp)
                with sp.Fori(1, GROUPS) as g:
                    for r in range(4):
                        sp.wait_ge(s["pv"], ready(NP * (4 * g + r - 4) + NP - 1))
                        fetch(4 * g + r, r)

            @block.gpsimd
            def _(pool):
                open_sems(pool, s["values"])

                def take(g):
                    for r in range(4):
                        t = 4 * g + r
                        if not (isinstance(g, int) and g == 0):
                            pool.wait_ge(s["pv"], ready(NP * (t - 4) + NP - 1))
                            settle(pool)
                        nc.gpsimd.tensor_copy(flat(values[r][:, :, :]), v[:, bass.ds(t, 1), :, :].rearrange(
                            "p a k d -> p (a k d)")).then_inc(s["values"], 1)
                groups(pool, take)

            @block.tensor
            def _(pe):
                open_sems(pe, s["pm"], s["px"], s["pv"])
                pe.wait_ge(s["ones"], 4)

                def maximum(g, slot, use, p):
                    u = MAXIMA[p]
                    if p == 0:
                        pe.wait_ge(loaded[slot], 32 * (g + 1))
                    pe.wait_ge(s["max"], free(use, 2))
                    n = (u + 1) * P
                    for a in range(0, n, CH):
                        b = min(a + CH, n)
                        nc.tensor.matmul(psM[p % 2][:, a:b], q_rows[slot][0:ROWS, u * P:(u + 1) * P],
                                         k_rows[slot][0:ROWS, a:b], start=True, stop=b < n)
                    nc.tensor.matmul(psM[p % 2][:, u * P:n], core.identb[:, :], core.mask_q[:, :],
                                     start=False, stop=True).then_inc(s["pm"], 1)

                def maximum_rows(g, r, i):
                    use = rows_use(g, r, i)
                    if i == 0:
                        pe.wait_ge(s["neg3"], ready(4 * g + r))
                    pe.wait_ge(s["ex"], free(use, 2))
                    for j in range(HALF):
                        ins = nc.tensor.matmul(psX[i][ROWS:R3, j * P:(j + 1) * P], neg3[r % 2][:, i * HALF + j, :],
                                               core.identb[:, :], start=True, stop=True)
                    ins.then_inc(s["px"], 1)

                def scores(t, slot, j):
                    c, kt = PIECES[TURNS[j]]
                    off = max(0, kt * P - c * CH)
                    pe.wait_ge(s["ex"], free(bank_use(t, j), 2))
                    diag = kt * P >= c * CH
                    ins = nc.tensor.matmul(psX[j % 2][:, off:CH], k_rows[slot][0:R3, kt * P:(kt + 1) * P],
                                           q_rows[slot][0:R3, c * CH + off:(c + 1) * CH], start=True, stop=not diag)
                    if diag:
                        ins = nc.tensor.matmul(psX[j % 2][:, off:off + P], core.identb[:, :], core.mask_k[:, :],
                                               start=False, stop=True)
                    ins.then_inc(s["px"], 1)

                def weighted(g, r, j):
                    t, i = 4 * g + r, TURNS[j]
                    c, kt = PIECES[i]
                    off = max(0, kt * P - c * CH)
                    if i == 0:
                        pe.wait_ge(s["values"], ready(t))
                    if r == 0 and kt == 0:
                        if isinstance(g, int) and g == 0:
                            pe.wait_ge(s["clear"], 2)
                        else:
                            pe.wait_ge(s["copied"], ready(2 * (g - 1) + c))
                    pe.wait_ge(s["ex"], ready(bank_use(t, j)))
                    nc.tensor.matmul(psV[c][32 * r:32 * r + VD, off:CH], values[r][:, kt, :],
                                     probs[i % PROBS][:, off:CH], start=kt == 0, stop=i == last_of[c]).then_inc(s["pv"], 1)

                def outputs(g):
                    for c in range(2):
                        pe.wait_ge(s["copied"], ready(2 * g + c))
                        pe.wait_ge(s["max"], free(output_use(g, c), 2))
                        for j in range(HALF):
                            ins = nc.tensor.transpose(psM[c][:, j * P:(j + 1) * P],
                                                      turned[:, (c * HALF + j) * P:(c * HALF + j + 1) * P], core.ident[:, :])
                        ins.then_inc(s["pm"], 1)

                def head(g, r):
                    t = 4 * g + r
                    order = turns(t)
                    for n, j in enumerate(order):
                        if n + 2 < len(order):
                            turn = order[n + 2]
                            if isinstance(TURNS[turn], int):
                                scores(t, r, turn)
                            else:
                                maximum_rows(g if r < 3 else g + 1, (r + 1) % 4, turn - TURNS.index("maximum 0"))
                        elif not final(t):
                            scores(t + 1, (r + 1) % 4, n + 2 - NU)
                        if has_ahead(g, r):
                            for p in MAXIMA_AT.get(n, ()):
                                maximum(*ahead(g, r), maximum_use(g, r, p), p)
                        if isinstance(TURNS[j], int):
                            weighted(g, r, j)
                        if n == OUTPUTS_AT and r == 0 and not (isinstance(g, int) and g == 0):
                            outputs(g - 1)

                for t in range(AHEAD):
                    for p in range(KT):
                        maximum(0, t, KT * t + p, p)
                for i in range(2):
                    maximum_rows(0, 0, i)
                pe.wait_ge(s["ex"], ready(1))
                scores(0, 0, 0)
                scores(0, 0, 1)

                def body(g):
                    for r in range(4):
                        head(g, r)
                groups(pe, body)
                outputs(GROUPS - 1)

            @block.scalar
            def _(act):
                open_sems(act, s["ex"], s["copied"])
                nc.scalar.preload_act_table(ACT.Exp)

                def rows(g, r, i):
                    act.wait_ge(s["px"], ready(rows_use(g, r, i)))
                    nc.scalar.activation(q_rows[r][ROWS:R3, i * CH:(i + 1) * CH], psX[i % 2][ROWS:R3, :],
                                         ACT.Copy).then_inc(s["ex"], 1)

                def copy(g, c):
                    act.wait_ge(s["pv"], ready(NP * (4 * g + 3) + last_of[c]))
                    if not (isinstance(g, int) and g == 0):
                        act.wait_ge(s["max"], ready(output_use(g - 1, c)))
                    nc.scalar.activation(turned[:, c * CH:(c + 1) * CH], psV[c][:, :], ACT.Copy).then_inc(s["copied"], 1)

                def body(g):
                    for r in range(4):
                        t = 4 * g + r
                        for j in turns(t):
                            if isinstance(TURNS[j], str):
                                rows(g if r < 3 else g + 1, (r + 1) % 4, j - TURNS.index("maximum 0"))
                                continue
                            i = TURNS[j]
                            c, kt = PIECES[i]
                            off = max(0, kt * P - c * CH)
                            act.wait_ge(s["px"], ready(bank_use(t, j)))
                            act.wait_ge(s["pv"], free(NP * t + i, PROBS))
                            nc.scalar.activation(probs[i % PROBS][:, off:CH], psX[j % 2][:, off:CH], ACT.Exp,
                                                 scale=float(D) ** -0.5).then_inc(s["ex"], 1)
                            if r == 3 and i == last_of[0] + 3:
                                copy(g, 0)
                            if r == 0 and i == 1 and not (isinstance(g, int) and g == 0):
                                copy(g - 1, 1)
                for i in range(2):
                    rows(0, 0, i)
                groups(act, body)
                copy(GROUPS - 1, 1)

            @block.vector
            def _(dve):
                open_sems(dve, *(s[n] for n in ("max", "split", "neg3", "rden")))
                for i in range(4):
                    nc.vector.memset(k_rows[i][ROWS:R3, :], 1.0).then_inc(s["ones"], 1)
                for c in range(2):
                    nc.vector.memset(psV[c][:, :], 0.0).then_inc(s["clear"], 1)

                def maxima(t, use, slot):
                    for p, u in enumerate(MAXIMA):
                        dve.wait_ge(s["pm"], ready(use(p)))
                        nc.vector.tensor_reduce(neg[:, u:u + 1], psM[p % 2][:, 0:(u + 1) * P], AX.X, ALU.max,
                                                negate=True).then_inc(s["max"], 1)
                    dve.wait_ge(s["max"], ready(use(KT - 1)))
                    parts = neg3[slot]
                    nc.vector.tensor_copy(parts[:, :, 0], neg[:, :]).then_inc(s["split"], 1)
                    dve.wait_ge(s["split"], ready(3 * t))
                    nc.vector.tensor_tensor(left[:, :], neg[:, :], parts[:, :, 0], ALU.subtract).then_inc(s["split"], 1)
                    dve.wait_ge(s["split"], ready(3 * t + 1))
                    nc.vector.tensor_copy(parts[:, :, 1], left[:, :]).then_inc(s["split"], 1)
                    dve.wait_ge(s["split"], ready(3 * t + 2))
                    nc.vector.tensor_tensor(parts[:, :, 2], left[:, :], parts[:, :, 1],
                                            ALU.subtract).then_inc(s["neg3"], 1)
                    dve.wait_ge(s["neg3"], ready(t))

                def divide(g):
                    for c in range(2):
                        dve.wait_ge(s["pm"], ready(output_use(g, c)))
                        if c:
                            dve.wait_ge(s["max"], ready(output_use(g, 0)))
                        elif not (isinstance(g, int) and g == 0):
                            dve.wait_ge(s["max"], ready(output_use(g - 1, 1)))
                        out = psM[c][:, 0:CH].rearrange("p (q r w) -> p q r w", q=HALF, r=4)
                        nc.vector.reciprocal(rden[:, :, :], out[:, :, :, D]).then_inc(s["rden"], 1)
                        dve.wait_ge(s["rden"], ready(2 * g + c))
                        dst = at(mixed, g)[:, c * HALF * 4 * D:(c + 1) * HALF * 4 * D].rearrange(
                            "p (q r d) -> p q r d", q=HALF, r=4)
                        nc.vector.tensor_tensor(dst, out[:, :, :, 0:D],
                                                rden[:, :, :].unsqueeze(3).broadcast_to([P, HALF, 4, D]),
                                                ALU.mult).then_inc(s["max"], 1)

                def body(g):
                    for r in range(4):
                        if has_ahead(g, r):
                            maxima(4 * g + r + AHEAD, lambda p: maximum_use(g, r, p), r % 2)
                        if r == 0 and not (isinstance(g, int) and g == 0):
                            divide(g - 1)
                for t in range(AHEAD):
                    maxima(t, lambda p: KT * t + p, t)
                groups(dve, body)
                divide(GROUPS - 1)


def attention_out(core, name, w_out, mixed):
    nc, x = core.nc, core.x
    stage = name + "o"
    with ExitStack() as ctx:
        sb, ps = scratch(nc, ctx)
        w = sb(f"{stage}_w", [P, KH, H])
        row = [sb(f"{stage}_row{i}", [P, H]) for i in range(4)]
        xt = [sb(f"{stage}_xt{i}", [P, KH, P]) for i in range(2)]
        psT = [ps(f"{stage}_pT{i}", [P, CH]) for i in range(2)]
        psO = [ps(f"{stage}_pO{i}", [P, CH]) for i in range(2)]
        s = core.sems(stage, "weights row turned xt po added")
        groups = HEADS // 4

        with nc.Block() as block:
            @block.sync
            def _(sp):
                sp.dma_start(w[:, :, :], w_out).then_inc(s["weights"], 16)

            @block.gpsimd
            def _(pool):
                open_sems(pool, s["row"])
                with pool.Fori(0, B) as b:
                    for q in range(KT):
                        pool.wait_ge(s["turned"], free(KT * b + q, 4))
                        settle(pool)
                        src = mixed[:, bass.ds(b * groups, groups), q * 4 * D:(q + 1) * 4 * D]
                        nc.gpsimd.tensor_copy(row[q % 4][:, :].rearrange("p (g c) -> p g c", g=groups),
                                              src).then_inc(s["row"], 1)

            @block.tensor
            def _(pe):
                open_sems(pe, s["turned"], s["po"])
                pe.wait_ge(s["weights"], 16)

                def product(t, q):
                    pe.wait_ge(s["xt"], ready(t))
                    pe.wait_ge(s["added"], free(t, 2))
                    for k in range(KH):
                        ins = nc.tensor.matmul(psO[q % 2][:, 0:H], xt[q % 2][:, k, :], w[:, k, :],
                                               start=k == 0, stop=k == KH - 1)
                    ins.then_inc(s["po"], 1)
                with pe.Fori(0, B) as b:
                    for q in range(KT):
                        t = KT * b + q
                        pe.wait_ge(s["row"], ready(t))
                        pe.wait_ge(s["xt"], free(t, 2))
                        for k in range(KH):
                            ins = nc.tensor.transpose(psT[q % 2][:, k * P:(k + 1) * P], row[q % 4][:, k * P:(k + 1) * P],
                                                      core.ident[:, :])
                        ins.then_inc(s["turned"], 1)
                        if q:
                            product(t - 1, q - 1)
                    product(KT * b + KT - 1, KT - 1)

            @block.scalar
            def _(act):
                open_sems(act, s["xt"])
                with act.Fori(0, B) as b:
                    for q in range(KT):
                        t = KT * b + q
                        act.wait_ge(s["turned"], ready(t))
                        act.wait_ge(s["po"], free(t, 2))
                        nc.scalar.activation(flat(xt[q % 2][:, :, :]), psT[q % 2][:, 0:H], ACT.Copy).then_inc(s["xt"], 1)

            @block.vector
            def _(dve):
                open_sems(dve, s["added"])
                with dve.Fori(0, B) as b:
                    for q in range(KT):
                        t = KT * b + q
                        dve.wait_ge(s["po"], ready(t))
                        nc.vector.tensor_tensor(at(x, t), at(x, t), psO[q % 2][:, 0:H], ALU.add).then_inc(s["added"], 1)



def last_ffn(core, w_gu, w_down, w_down_last, scales, down_scale, x_out):
    nc, x = core.nc, core.x
    with ExitStack() as ctx:
        sb, ps = scratch(nc, ctx)
        NI = -(-FI // P)
        width = [min(P, FI - i * P) for i in range(NI)]
        w = sb("f_wgu", [P, KH, 2 * FI])
        wd = sb("f_wd", [P, NI, H])
        sc = {n: sb(f"f_{n}", [P, NI]) for n in ("gs", "us")}
        ds = sb("f_ds", [P, H])
        act_g = [sb(f"f_act{i}", [P, CH]) for i in range(2)]
        hid = [sb(f"f_hid{i}", [P, NI, CH]) for i in range(2)]
        res = [sb(f"f_res{i}", [P, H]) for i in range(2)]
        psT = [ps(f"f_pT{i}", [P, CH]) for i in range(2)]
        psG = [ps(f"f_pG{i}", [P, CH]) for i in range(2)]
        psU = [ps(f"f_pU{i}", [P, CH]) for i in range(2)]
        psO = [ps(f"f_pO{i}", [P, CH]) for i in range(2)]
        s = core.sems("f", "weights pu act hid po res added stored")
        front = Front(core, "f", sb, psT, x, lambda act, c: act.wait_ge(s["pu"], ready(NI * (c - 1) - 1)))

        def fetch(sp):
            last = width[-1]
            loads = [(w[:, :, :], w_gu), (wd[:, 0:NI - 1, :], w_down), (wd[0:last, NI - 1, :], w_down_last),
                     (ds[:, :], down_scale)]
            for n in ("gs", "us"):
                loads += [(sc[n][:, 0:NI - 1], scales[n][0]), (sc[n][0:last, NI - 1:NI], scales[n][1])]
            for dst, src in loads:
                sp.dma_start(dst, src).then_inc(s["weights"], 16)
        norm_stats(core, "fn", x, fetch=fetch)

        with nc.Block() as block:
            @block.sync
            def _(sp):
                for c in range(NC):
                    tiles = slice(SUB * c, SUB * (c + 1))
                    sp.wait_ge(s["added"], ready(SUB * c + SUB - 1))
                    sp.dma_start(x_out[:, tiles, :], x[:, tiles, :]).then_inc(s["stored"], 16)
                sp.wait_ge(s["stored"], 16 * NC)

            @block.tensor
            def _(pe):
                front.open(pe, "turned")
                open_sems(pe, s["pu"], s["po"])
                pe.wait_ge(s["weights"], 8 * 16)

                def products(c):
                    pe.wait_ge(front.s["xt"], ready(SUB * c + SUB - 1))
                    for i in range(NI):
                        pe.wait_ge(s["hid"], free(NI * c + i, 2))
                        for dst, base in ((psG[i % 2], 0), (psU[i % 2], FI)):
                            for k in range(KH):
                                ins = nc.tensor.matmul(dst[0:width[i], :],
                                                       w[:, k, base + i * P:base + i * P + width[i]],
                                                       front.xt[c % 2][:, k, :], start=k == 0, stop=k == KH - 1)
                        ins.then_inc(s["pu"], 1)

                def outputs(c):
                    pe.wait_ge(s["hid"], ready(NI * c + NI - 1))
                    for sub in range(SUB):
                        pe.wait_ge(s["res"], free(SUB * c + sub, 2))
                        for i in range(NI):
                            ins = nc.tensor.matmul(psO[sub % 2][:, 0:H],
                                                   hid[c % 2][0:width[i], i, sub * P:(sub + 1) * P],
                                                   wd[0:width[i], i, :], start=i == 0, stop=i == NI - 1)
                        ins.then_inc(s["po"], 1)
                front.tensor(pe, 0)
                for c in range(NC):
                    products(c)
                    if c < NC - 1:
                        front.tensor(pe, c + 1)
                    if c:
                        outputs(c - 1)
                outputs(NC - 1)

            @block.scalar
            def _(act):
                front.open(act, "xt")
                open_sems(act, s["act"])
                nc.scalar.preload_act_table(ACT.Silu)
                act.wait_ge(s["weights"], 8 * 16)
                front.scalar(act, 0, 0)
                for c in range(NC):
                    for i in range(NI):
                        act.wait_ge(s["pu"], ready(NI * c + i))
                        act.wait_ge(s["hid"], free(NI * c + i, 2))
                        nc.scalar.activation(act_g[i % 2][0:width[i], :], psG[i % 2][0:width[i], :], ACT.Silu,
                                             scale=sc["gs"][0:width[i], i:i + 1]).then_inc(s["act"], 1)
                    if c < NC - 1:
                        front.scalar(act, c + 1, (c + 1) % 2)

            @block.vector
            def _(dve):
                front.open(dve, "xn")
                open_sems(dve, s["hid"], s["res"], s["added"])
                dve.wait_ge(s["weights"], 8 * 16)

                def add(c):
                    for sub in range(SUB):
                        t = SUB * c + sub
                        dve.wait_ge(s["po"], ready(t))
                        dve.wait_ge(s["added"], free(t, 2))
                        nc.vector.tensor_tensor(res[sub % 2][:, :], psO[sub % 2][:, 0:H], ds[:, :],
                                                ALU.mult).then_inc(s["res"], 1)
                        dve.wait_ge(s["res"], ready(t))
                        nc.vector.tensor_tensor(at(x, t), at(x, t), res[sub % 2][:, :],
                                                ALU.add).then_inc(s["added"], 1)
                front.vector(dve, 0)
                for c in range(NC):
                    if c < NC - 1:
                        front.vector(dve, c + 1)
                    if c > 1:
                        dve.wait_ge(s["po"], ready(SUB * (c - 2) + SUB - 1))
                    for i in range(NI):
                        dve.wait_ge(s["act"], ready(NI * c + i))
                        nc.vector.scalar_tensor_tensor(hid[c % 2][0:width[i], i, :], psU[i % 2][0:width[i], :],
                                                       sc["us"][0:width[i], i:i + 1], act_g[i % 2][0:width[i], :],
                                                       ALU.mult, ALU.mult).then_inc(s["hid"], 1)
                    if c:
                        add(c - 1)
                add(NC - 1)



def constants(core, x_in, x_loaded):
    nc = core.nc
    s = core.sems("const", "iota chain")
    with nc.Block() as block:
        @block.sync
        def _(sp):
            sp.dma_start(core.x[:, :, :], x_in).then_inc(x_loaded, 16)
            sp.wait_ge(x_loaded, 16)

        @block.gpsimd
        def _(pool):
            nc.gpsimd.iota(core.number[:, :], [[P, NT]], base=0, channel_multiplier=1,
                           allow_small_or_imprecise_dtypes=True).then_inc(s["iota"], 1)
            nc.gpsimd.iota(core.iota[:, :], [[1, P]], base=0, channel_multiplier=0,
                           allow_small_or_imprecise_dtypes=True).then_inc(s["iota"], 1)
            nc.gpsimd.iota(core.part[:, :], [[0, 1]], base=0, channel_multiplier=1,
                           allow_small_or_imprecise_dtypes=True).then_inc(s["iota"], 1)

        @block.vector
        def _(dve):
            dve.wait_ge(s["iota"], 3)
            do = Chain(dve, s["chain"])
            V, part = nc.vector, core.part[:, 0:1]
            do(V.tensor_scalar(core.ident[:, :], core.iota[:, :], part, None, ALU.is_equal))
            do(V.tensor_scalar(core.identb[:, :], core.iota[:, :], part, None, ALU.is_equal))
            do(V.tensor_copy(core.iotab[:, :], core.iota[:, :]))
            do(V.tensor_scalar(core.earlier[:, :], core.iota[:, :], part, None, ALU.is_gt))
            do(V.tensor_scalar(core.mask_q[:, :], core.iota[:, :], part, NEG, ALU.is_gt, ALU.mult))
            do(V.tensor_scalar(core.mask_k[:, :], core.iota[:, :], part, NEG, ALU.is_lt, ALU.mult))
            do(V.memset(core.onesb[:, :], 1.0))
            do(V.memset(core.onesf[:, :], 1.0))


def load(core, sem, dst, src):
    core.behind.append((dst, src, sem))


def program(nc, a, out):
    x_in = a["x"].rearrange("(t p) h -> p t h", p=P)
    x_out = out.rearrange("(t p) h -> p t h", p=P)
    with ExitStack() as ctx:
        core = Core(nc)
        sb, _ = scratch(nc, ctx)
        core.x = sb("x", [P, NT, H])
        core.rstd, core.nmr = sb("rstd", [P, NT]), sb("nmr", [P, NT])
        core.rstd1, core.rstd2, core.nmr2 = (sb(n, [P, NT]) for n in ("rstd1", "rstd2", "nmr2"))
        core.iota, core.part = sb("iota", [P, P]), sb("part", [P, 1])
        core.number = sb("number", [P, NT])
        core.ident, core.identb = sb("ident", [P, P]), sb("identb", [P, P], BF16)
        core.iotab, core.earlier = sb("iotab", [P, P], BF16), sb("earlier", [P, P], BF16)
        core.mask_q, core.mask_k = sb("mask_q", [P, P], BF16), sb("mask_k", [P, P], BF16)
        core.onesb, core.onesf = sb("onesb", [P, P], BF16), sb("onesf", [P, 32])
        big = sb("experts", [P, 32, WE])
        rows = nc.dram_tensor("rows", (T, H), F32, kind="Internal").ap()
        results = nc.dram_tensor("results", (96 * P, H), F32, kind="Internal").ap()
        core.rows_flat, core.results_flat = rows, results
        core.rows = rows.rearrange("(t p) h -> p t h", p=P)
        core.results = results.rearrange("(t p) h -> p t h", p=P)
        core.stack = {w: nc.dram_tensor(f"stack_{w}", (B * H, SEGS, S), BF16, kind="Internal").ap() for w in "qk"}
        core.stack_rows = {w: ap.rearrange("c g s -> (c g) s") for w, ap in core.stack.items()}
        core.weight, core.read = sb("weight", [P, NT * TOPK]), sb("read", [P, NT * TOPK], I32)
        x_loaded, load0, load1a, load1b, load2 = (core.sem(n) for n in (
            "x_loaded", "load0", "load1a", "load1b", "load2"))

        constants(core, x_in, x_loaded)

        def experts(name, E, kind, *loaded):
            m = Moe(core, name, E, kind, big)
            m.loaded = loaded
            return m

        half = 16
        load(core, load0, big[:, 0:half, :], a["m0_w"])
        load(core, load1b, big[:, half:, :], a["m1_w"][:, half:, :])
        with core.layer():
            layer0_attention(core, a["a0_wv"], a["a0_wg"], a["a0_bg"], a["a0_wq"], a["a0_bq"], a["a0_wo"])
        with core.layer():
            moe_layer(experts("m0", 16, "sigmoid", load0), a["m0_ws"], a["m0_wr"], a["m0_bias"])
        load(core, load1a, big[:, 0:half, :], a["m1_w"][:, 0:half, :])
        with core.layer():
            layer1_attention(core, a["a1_shift"], a["a1_gate"], a["a1_gamma"], a["a1_beta"], a["a1_kv"],
                         a["a1_decay"], a["a1_first"], a["a1_out"])
        with core.layer():
            moe_layer(experts("m1", 32, "softplus", load1a, load1b), a["m1_ws"], a["m1_wr"], a["m1_bias"])
        load(core, load2, big[:, :, :], a["m2_w"])
        with core.layer():
            softmax_attention(core, "a2", a["a2_w"], a["a2_out"], None)
        with core.layer():
            moe_layer(experts("m2", 32, "softmax", load2), a["m2_ws"], a["m2_wr"], None, a["m2_norm"])
        with core.layer():
            softmax_attention(core, "a3", a["a3_w"], a["a3_out"], (a["rope_cos"], a["rope_sin"]))
        with core.layer():
            last_ffn(core, a["f_gu"], a["f_down"], a["f_down_last"],
                 {n: (a[f"f_{n}"], a[f"f_{n}_last"]) for n in ("gs", "us")}, a["f_ds"], x_out)



def by_half(w):
    return w.reshape(KH, P, -1).transpose(1, 0, 2)


def wide(v):
    return np.broadcast_to(v.reshape(1, -1), (P, v.size))


def expert_rows(gate_up, down):
    e = gate_up.shape[0]
    gu = gate_up.reshape(e, KH, P, 2 * I).transpose(2, 0, 1, 3).reshape(P, e, KH * 2 * I)
    return np.concatenate([gu, down.transpose(1, 0, 2)], axis=2)


def swiglu(gate, up, down):
    return expert_rows(np.concatenate([gate, up], axis=1).transpose(0, 2, 1), down.transpose(0, 2, 1))


def heads_columns(w):
    return w.reshape(KH, P, 3, H).transpose(1, 0, 2, 3)


def rope_tables():
    inv = (1.0 / np.float32(10000.0) ** (np.arange(0, D, 2, dtype=np.float32) / np.float32(D))).astype(np.float32)
    ang = np.outer(np.arange(S, dtype=np.float32), inv).astype(np.float32)
    ang = np.concatenate([ang, ang], axis=1)
    sign = np.where(np.arange(D) % 2 == 0, -1.0, 1.0)
    return (np.tile(np.cos(ang.astype(np.float64)).T, (P // D, 1)).astype(np.float32),
            np.tile((np.sin(ang.astype(np.float64)) * sign).T, (P // D, 1)).astype(np.float32))


def layouts(i):
    a = {"x": i["L0_attn_x"].reshape(T, H)}
    for n in "vgqo":
        a[f"a0_w{n}"] = by_half(i[f"L0_attn_W{n}"])
    for n in "gq":
        a[f"a0_b{n}"] = i[f"L0_attn_b{n}"].reshape(KH, P).T
    a["m0_w"] = swiglu(i["L0_ffn_w_gate"], i["L0_ffn_w_up"], i["L0_ffn_w_down"])
    a["m0_ws"] = swiglu(i["L0_ffn_sw_gate"][None], i["L0_ffn_sw_up"][None], i["L0_ffn_sw_down"][None])[:, 0]
    a["m0_wr"] = by_half(i["L0_ffn_gate_w"].T)
    a["m0_bias"] = wide(i["L0_ffn_expert_bias"])
    a["a1_shift"] = by_half(i["L1_attn_W_shift"].T)
    a["a1_gate"] = wide(i["L1_attn_gate"])
    a["a1_gamma"] = wide(i["L1_attn_ln_gamma"])
    a["a1_beta"] = wide(i["L1_attn_ln_beta"])
    a["a1_kv"] = np.concatenate([by_half(i["L1_attn_W_key"].T), by_half(i["L1_attn_W_value"].T)], axis=2)
    a["a1_decay"] = np.tile(i["L1_attn_time_decay"].reshape(NS, 1), (B, 1))
    a["a1_first"] = np.tile(i["L1_attn_time_first"].reshape(NS, 1), (B, 1))
    a["a1_out"] = np.tile(i["L1_attn_W_output"].T, (B, 1))
    a["m1_w"] = swiglu(i["L1_ffn_gate_w"], i["L1_ffn_up_w"], i["L1_ffn_down_w"])
    a["m1_ws"] = swiglu(i["L1_ffn_shared_gate_w"][None], i["L1_ffn_shared_up_w"][None],
                        i["L1_ffn_shared_down_w"][None])[:, 0]
    a["m1_wr"] = by_half(i["L1_ffn_router_w"].T)
    a["m1_bias"] = wide(i["L1_ffn_expert_bias"])
    a["a2_w"] = heads_columns(i["L2_attn_w_qkv"])
    a["a2_out"] = by_half(i["L2_attn_w_out"])
    a["m2_w"] = expert_rows(i["L2_ffn_w13"], i["L2_ffn_w2"])
    a["m2_ws"] = expert_rows(np.concatenate([i["L2_ffn_shared_gate_w"], i["L2_ffn_shared_up_w"]], axis=1)[None],
                             i["L2_ffn_shared_down_w"][None])[:, 0]
    a["m2_wr"] = by_half(i["L2_ffn_gate_w"].T)
    a["m2_norm"] = wide(i["L2_ffn_norm_w"])
    w = heads_columns(i["L3_attn_Wqkv"].T)
    swap = np.arange(H) ^ 1
    a["a3_w"] = np.concatenate([w, w[:, :, 0:2][:, :, :, swap]], axis=2)
    a["a3_out"] = by_half(i["L3_attn_Wout"].T)
    a["rope_cos"], a["rope_sin"] = rope_tables()
    a["f_gu"] = np.concatenate([by_half(i["L3_ffn_gate_w"].T), by_half(i["L3_ffn_up_w"].T)], axis=2)
    down = i["L3_ffn_down_w"].T
    full = FI // P
    a["f_down"] = down[:full * P].reshape(full, P, H).transpose(1, 0, 2)
    a["f_down_last"] = down[full * P:]
    for n, key in (("gs", "gate_s"), ("us", "up_s")):
        v = i[f"L3_ffn_{key}"]
        a[f"f_{n}"] = v[:full * P].reshape(full, P).T
        a[f"f_{n}_last"] = v[full * P:].reshape(-1, 1)
    a["f_ds"] = wide(i["L3_ffn_down_s"])
    return a


def kernel(**inputs):
    import concourse.bacc as bacc
    from concourse.bass_utils import run_bass_kernel_spmd as run

    nc = bacc.Bacc("TRN2", target_bir_lowering=False, num_devices=1)
    arrays, args = {}, {}
    for name, value in layouts({k: np.asarray(v) for k, v in inputs.items()}).items():
        value = np.ascontiguousarray(value)
        arrays["in_" + name] = value
        args[name] = nc.dram_tensor("in_" + name, value.shape, mybir.dt.from_np(value.dtype), kind="ExternalInput").ap()
    out = nc.dram_tensor("out_0", (T, H), F32, kind="ExternalOutput").ap()
    program(nc, args, out)
    result = run(nc, [arrays], core_ids=[0])
    return result.results[0]["out_0"].reshape(B, S, H)
```
